# Optimizing a Trainium2 kernel written in Bass

```python
import numpy as np
import jax
import jax.numpy as jnp

def _softmax(x, axis=-1):
    return jax.nn.softmax(x, axis=axis)
def _gelu(x):
    return jax.nn.gelu(x, approximate=True)
def _silu(x):
    return jax.nn.silu(x)
def _sigmoid(x):
    return jax.nn.sigmoid(x)
def _layernorm(x, axis=-1, eps=1e-5):
    m = jnp.mean(x, axis=axis, keepdims=True)
    v = jnp.var(x, axis=axis, keepdims=True)
    return (x - m) / jnp.sqrt(v + eps)
def _scatter_add(tgt, idx, src, axis=0):
    return tgt.at[idx].add(src)
def _segment_sum(src, seg, n):
    return jax.ops.segment_sum(src, seg, n)

kernel_name = 'mk_conv_preact_d2_conv_nchw768_657c54'

def setup_inputs(seed: int = 0):
    np.random.seed(seed)
    _w = jnp.asarray
    def _rec_inputs():
        import jax
        import jax.numpy as jnp
        _gk = jax.random.key(seed)
        x = -0.0001538 + 1 * jax.random.normal(jax.random.fold_in(_gk, 1), (8, 768, 32, 32), jnp.float32)
        return x
    x = _rec_inputs()
    def _L0_conv_setup():
        import jax, jax.numpy as jnp
        import numpy as np
        DIM = 768
        HEADS = 12
        HEAD_DIM = DIM // HEADS
        SCALE = HEAD_DIM ** (-0.5)
        key = jax.random.key(seed)
        ks = jax.random.split(key, 5)
        x = jax.random.normal(ks[0], (8, DIM, 32, 32), dtype=jnp.float32)
        w_qkv = jax.random.normal(ks[1], (DIM, 3 * DIM), dtype=jnp.float32) * DIM ** (-0.5)
        b_qkv = jax.random.normal(ks[2], (3 * DIM,), dtype=jnp.float32) * 0.02
        w_proj = jax.random.normal(ks[3], (DIM, DIM), dtype=jnp.float32) * DIM ** (-0.5)
        b_proj = jax.random.normal(ks[4], (DIM,), dtype=jnp.float32) * 0.02
        return {'x': x, 'w_qkv': w_qkv, 'b_qkv': b_qkv, 'w_proj': w_proj, 'b_proj': b_proj}
    _L0_conv_all = _L0_conv_setup()
    _L0_conv_in = {k: v for k, v in _L0_conv_all.items() if k in ('w_qkv', 'b_qkv', 'w_proj', 'b_proj', )}
    del _L0_conv_all

    def _L1_conv_setup():
        import jax, jax.numpy as jnp
        import numpy as np
        NUM_BLOCKS = 8
        SPARSITY_THRESHOLD = 0.01
        SCALE = 0.02

        def _complex_mul(xr, xi, w):
            wr, wi = (w[..., 0], w[..., 1])
            out_r = jnp.einsum('bnhwi,nio->bnhwo', xr, wr) - jnp.einsum('bnhwi,nio->bnhwo', xi, wi)
            out_i = jnp.einsum('bnhwi,nio->bnhwo', xr, wi) + jnp.einsum('bnhwi,nio->bnhwo', xi, wr)
            return (out_r, out_i)

        def _complex_add(xr, xi, b):
            return (xr + b[None, :, None, None, :, 0], xi + b[None, :, None, None, :, 1])
        key = jax.random.key(seed)
        k_x, k_w1, k_b1, k_w2, k_b2 = jax.random.split(key, 5)
        B, C, H, W = (2, 768, 240, 240)
        bs = C // NUM_BLOCKS
        return {'x': jax.random.normal(k_x, (B, C, H, W), dtype=jnp.float32), 'w1': SCALE * jax.random.normal(k_w1, (NUM_BLOCKS, bs, bs, 2), dtype=jnp.float32), 'b1': SCALE * jax.random.normal(k_b1, (NUM_BLOCKS, bs, 2), dtype=jnp.float32), 'w2': SCALE * jax.random.normal(k_w2, (NUM_BLOCKS, bs, bs, 2), dtype=jnp.float32), 'b2': SCALE * jax.random.normal(k_b2, (NUM_BLOCKS, bs, 2), dtype=jnp.float32)}
    _L1_conv_all = _L1_conv_setup()
    _L1_conv_in = {k: v for k, v in _L1_conv_all.items() if k in ('w1', 'b1', 'w2', 'b2', )}
    del _L1_conv_all

    return {
        "x": x,
        "L0_conv_w_qkv": _L0_conv_in["w_qkv"],
        "L0_conv_b_qkv": _L0_conv_in["b_qkv"],
        "L0_conv_w_proj": _L0_conv_in["w_proj"],
        "L0_conv_b_proj": _L0_conv_in["b_proj"],
        "L1_conv_w1": _L1_conv_in["w1"],
        "L1_conv_b1": _L1_conv_in["b1"],
        "L1_conv_w2": _L1_conv_in["w2"],
        "L1_conv_b2": _L1_conv_in["b2"],
    }

def reference(x, L0_conv_w_qkv, L0_conv_b_qkv, L0_conv_w_proj, L0_conv_b_proj, L1_conv_w1, L1_conv_b1, L1_conv_w2, L1_conv_b2):
    import jax
    import jax.numpy as jnp
    def _L0_conv_ref(x, w_qkv, b_qkv, w_proj, b_proj):
        import jax, jax.numpy as jnp
        import numpy as np
        DIM = 768
        HEADS = 12
        HEAD_DIM = DIM // HEADS
        SCALE = HEAD_DIM ** (-0.5)
        B, C, H, W = x.shape
        N = H * W
        t = x.reshape(B, C, N).transpose(0, 2, 1)
        qkv = t @ w_qkv + b_qkv
        qkv = qkv.reshape(B, N, 3, HEADS, HEAD_DIM).transpose(2, 0, 3, 1, 4)
        q, k, v = (qkv[0], qkv[1], qkv[2])
        attn = jnp.einsum('bhnd,bhmd->bhnm', q, k) * SCALE
        attn = jax.nn.softmax(attn, axis=-1)
        o = jnp.einsum('bhnm,bhmd->bhnd', attn, v)
        o = o.transpose(0, 2, 1, 3).reshape(B, N, C)
        o = o @ w_proj + b_proj
        return o.reshape(B, H, W, C).transpose(0, 3, 1, 2)

    def _L1_conv_ref(x, w1, b1, w2, b2):
        import jax, jax.numpy as jnp
        import numpy as np
        NUM_BLOCKS = 8
        SPARSITY_THRESHOLD = 0.01
        SCALE = 0.02

        def _complex_mul(xr, xi, w):
            wr, wi = (w[..., 0], w[..., 1])
            out_r = jnp.einsum('bnhwi,nio->bnhwo', xr, wr) - jnp.einsum('bnhwi,nio->bnhwo', xi, wi)
            out_i = jnp.einsum('bnhwi,nio->bnhwo', xr, wi) + jnp.einsum('bnhwi,nio->bnhwo', xi, wr)
            return (out_r, out_i)

        def _complex_add(xr, xi, b):
            return (xr + b[None, :, None, None, :, 0], xi + b[None, :, None, None, :, 1])
        B, C, H, W = x.shape
        nb = NUM_BLOCKS
        bs = C // nb
        xv = x.reshape(B, nb, bs, H, W)
        xf = jnp.fft.rfft2(xv, axes=(-2, -1), norm='ortho')
        xf = jnp.transpose(xf, (0, 1, 3, 4, 2))
        xr, xi = (jnp.real(xf), jnp.imag(xf))
        xr, xi = _complex_mul(xr, xi, w1)
        xr, xi = _complex_add(xr, xi, b1)
        magnitude = jnp.sqrt(xr * xr + xi * xi + 1e-08)
        mask = (magnitude > SPARSITY_THRESHOLD).astype(xr.dtype)
        xr = xr * mask
        xi = xi * mask
        xr, xi = _complex_mul(xr, xi, w2)
        xr, xi = _complex_add(xr, xi, b2)
        xf = jax.lax.complex(xr, xi)
        xf = jnp.transpose(xf, (0, 1, 4, 2, 3))
        out = jnp.fft.irfft2(xf, s=(H, W), axes=(-2, -1), norm='ortho')
        return out.reshape(B, C, H, W)

    def _gn(v, G=32, eps=1e-5):
        B_, C_, H_, W_ = v.shape
        g = v.reshape(B_, G, C_ // G, H_, W_)
        m = jnp.mean(g, axis=(2, 3, 4), keepdims=True)
        s = jnp.var(g, axis=(2, 3, 4), keepdims=True)
        return ((g - m) / jnp.sqrt(s + eps)).reshape(v.shape)

    def _ln_c(v, eps=1e-6):
        m = jnp.mean(v, axis=1, keepdims=True)
        s = jnp.var(v, axis=1, keepdims=True)
        return (v - m) / jnp.sqrt(s + eps)

    def _ln_t(v, eps=1e-5):
        m = jnp.mean(v, axis=-1, keepdims=True)
        s = jnp.var(v, axis=-1, keepdims=True)
        return (v - m) / jnp.sqrt(s + eps)

    def _to_tokens(v):
        B_, C_, H_, W_ = v.shape
        return v.reshape(B_, C_, H_ * W_).transpose(0, 2, 1)
    def _from_tokens(t, like):
        B_, C_, H_, W_ = like.shape
        return t.transpose(0, 2, 1).reshape(B_, C_, H_, W_)

    x = x + _L0_conv_ref(_gn(x), L0_conv_w_qkv, L0_conv_b_qkv, L0_conv_w_proj, L0_conv_b_proj)
    x = x + _L1_conv_ref(_gn(x), L1_conv_w1, L1_conv_b1, L1_conv_w2, L1_conv_b2)
    return x


_drawn_inputs = setup_inputs


def setup_inputs(seed=0):
    import zlib

    import numpy as np

    out = dict(_drawn_inputs(seed))
    spreads = {}
    factors = {'L0_conv_b_qkv': 2.96, 'L0_conv_b_proj': 2.786, 'L1_conv_b1': 7.1}
    for name, (base, spread) in spreads.items():
        noise = np.random.default_rng([zlib.crc32(name.encode()), seed]).standard_normal(out[name].shape)
        drawn = base * np.exp(spread * noise) if base else spread * noise
        out[name] = jnp.asarray(drawn.astype(out[name].dtype))
    for name, factor in factors.items():
        out[name] = (out[name] * factor).astype(out[name].dtype)
    return out
```

```python
import math
from contextlib import ExitStack

import numpy as np
import concourse.bass as bass
from concourse import mybir

F32 = mybir.dt.float32
F32R = mybir.dt.float32r
ACT = mybir.ActivationFunctionType
ALU = mybir.AluOpType
AX = mybir.AxisListType

P = 128
C = 768
CT = C // P
H = W = 32
N = H * W
NT = N // P
HALF = N // 2
HEADS = 12
D = C // HEADS
GROUP = C // 32
NBLK = 8
BS = C // NBLK
KW = W // 2 + 1
FQ = (H // 2) * KW
FEPS = 1e-8
THRESH = np.float32(0.01)


def largest_square():
    t = np.float32(THRESH * THRESH)
    while np.sqrt(np.nextafter(t, np.float32(1))) <= THRESH:
        t = np.nextafter(t, np.float32(1))
    while np.sqrt(t) > THRESH:
        t = np.nextafter(t, np.float32(0))
    return float(t)


def after(turn, per_turn, k):
    return turn * per_turn + (per_turn + k + 1)


def f(ap):
    return ap.bitcast(F32)


AVG_PAIRS = [(a, b) for b in range(3) for a in range(3)
             if (a * P) // GROUP <= ((b + 1) * P - 1) // GROUP and (b * P) // GROUP <= ((a + 1) * P - 1) // GROUP]


def group_average(pe, out, avg, col):
    last = None
    for b in range(3):
        ins = [i for i, p in enumerate(AVG_PAIRS) if p[1] == b]
        for n, i in enumerate(ins):
            last = pe.matmul(out(b), avg[:, i, :], col(AVG_PAIRS[i][0]), start=(n == 0), stop=(n == len(ins) - 1))
    return last


def finish_stats(nc, block_args, mv, cols, avg, mean, rstd, small, ps, sems, eps=1e-5):
    (dve_ready, pe_done, act_done) = sems
    dve, pe, act = block_args
    NCOL = cols
    v3 = lambda ap: ap.rearrange("p (n t) -> p t n", t=3)
    cm = small[:, 0, 0:NCOL]
    e = small[:, 1, 0:NCOL]

    def on_vector():
        dve.tensor_copy(cm, mv[:, :, 0]).then_inc(dve_ready, 1)
        dve.wait_ge(pe_done, 1)
        dve.tensor_copy(mean, ps[:, 0:NCOL]).then_inc(dve_ready, 1)
        dve.wait_ge(dve_ready, 2)
        dve.tensor_tensor(e, cm, mean, ALU.subtract).then_inc(dve_ready, 1)
        dve.wait_ge(dve_ready, 3)
        dve.tensor_tensor(e, e, e, ALU.mult).then_inc(dve_ready, 1)
        dve.wait_ge(dve_ready, 4)
        dve.tensor_tensor(e, e, mv[:, :, 1], ALU.add).then_inc(dve_ready, 1)
        dve.wait_ge(pe_done, 2)
        dve.tensor_scalar(e, ps[:, 64:64 + NCOL], eps, None, ALU.add).then_inc(dve_ready, 1)
        dve.wait_ge(act_done, 1)
        dve.reciprocal(rstd, cm).then_inc(dve_ready, 1)

    def on_tensor():
        for r, (src, o) in enumerate(((cm, 0), (e, 64))):
            pe.wait_ge(dve_ready, 1 if r == 0 else 5)
            dst = ps[:, o:o + NCOL]
            group_average(pe, lambda b: v3(dst)[:, b, :], avg, lambda a: v3(src)[:, a, :]).then_inc(pe_done, 1)

    def on_scalar():
        act.wait_ge(dve_ready, 6)
        act.activation(cm, e, ACT.Sqrt).then_inc(act_done, 1)

    return on_vector, on_tensor, on_scalar


def stats_stage(nc, B, x, avg_in, ident_in, avg, ident, mean, rstd):
    RING = 3
    with ExitStack() as ctx:
        sb = lambda n, s, d=F32: ctx.enter_context(nc.sbuf_tensor(n, s, d))
        sem = lambda n: ctx.enter_context(nc.semaphore(n))
        xt = sb("st_x", [P, RING, CT, N])
        bn = sb("st_bn", [P, 2, 6 * CT * 2])
        mv = sb("st_mv", [P, B * CT, 2])
        small = sb("st_small", [P, 2, B * CT])
        ps = ctx.enter_context(nc.psum_tensor("st_ps", [P, 512], F32))
        loaded = [sem(f"st_loaded{r}") for r in range(RING)]
        avg_loaded, read, bn_done, agg_done = sem("st_avg"), sem("st_read"), sem("st_bn_done"), sem("st_agg_done")
        sems = (sem("st_dve_ready"), sem("st_pe_done"), sem("st_act_done"))
        block = ctx.enter_context(nc.Block())

        @block.sync
        def _(sp):
            sp.dma_start(avg[:, :, :], avg_in).then_inc(avg_loaded, 16)
            sp.dma_start(ident[:, :], ident_in).then_inc(avg_loaded, 16)
            for b in range(B):
                if b >= RING:
                    sp.wait_ge(bn_done, 2 * CT * (b - RING + 1))
                sp.dma_start(xt[:, b % RING, :, :], x[b].rearrange("(t p) n -> p t n", p=P)).then_inc(loaded[b % RING], 16)

        @block.vector
        def _(dve):
            bnv = bn[:, :, :].rearrange("p r (t h s) -> p r t h s", t=CT, h=2)
            for b in range(B):
                dve.wait_ge(loaded[b % RING], 16 * (b // RING + 1))
                if b >= 2:
                    dve.wait_ge(agg_done, CT * (b - 1))
                for t in range(CT):
                    for h in range(2):
                        dve.bn_stats(bnv[:, b % 2, t, h, :], xt[:, b % RING, t, h * HALF:(h + 1) * HALF]).then_inc(bn_done, 1)
                dve.wait_ge(bn_done, 2 * CT * (b + 1))
                for t in range(CT):
                    dve.bn_aggr(mv[:, b * CT + t, :], bnv[:, b % 2, t, :, :].rearrange("p h s -> p (h s)")).then_inc(agg_done, 1)
            dve.wait_ge(agg_done, B * CT)
            finish_stats(nc, (dve, None, None), mv, B * CT, avg, mean[:, :], rstd[:, :], small, ps, sems)[0]()

        @block.tensor
        def _(pe):
            pe.wait_ge(avg_loaded, 32)
            finish_stats(nc, (None, pe, None), mv, B * CT, avg, mean[:, :], rstd[:, :], small, ps, sems)[1]()

        @block.scalar
        def _(act):
            finish_stats(nc, (None, None, act), mv, B * CT, avg, mean[:, :], rstd[:, :], small, ps, sems)[2]()


def qkv_stage(nc, B, x, w_qkv, b_qkv, mean, rstd, qk_scr, v_scr):
    RING = 4
    QK_TILES = 2 * CT
    VW = 384
    VH = VW // D
    PER_HALF = QK_TILES + (NT // 2) * (C // VW)
    ITEMS = 2 * PER_HALF
    PIECES = 2 * CT
    with ExitStack() as ctx:
        sb = lambda n, s, d=F32: ctx.enter_context(nc.sbuf_tensor(n, s, d))
        sem = lambda n: ctx.enter_context(nc.semaphore(n))
        wh = sb("q_wh", [P, CT, 3 * C], F32R)
        wl = sb("q_wl", [P, CT, 3 * C], F32R)
        xs = sb("q_x", [P, CT, N])
        xh = sb("q_xh", [P, 2, CT, HALF], F32R)
        xl = sb("q_xl", [P, 2, CT, HALF], F32R)
        ob = sb("q_out", [P, RING, 2 * HALF], F32R)
        bias = sb("q_bias", [P, QK_TILES])
        ps = ctx.enter_context(nc.psum_tensor("q_ps", [P, RING, 512], F32))
        wst = xs[:, :, :].rearrange("p t n -> p (t n)")[:, 0:2 * 3 * C].rearrange("p (s n) -> p s n", s=2)
        w_loaded = [sem("q_w_loaded0"), sem("q_w_loaded1")]
        bias_loaded, x_loaded = sem("q_bias_loaded"), sem("q_x_loaded")
        wh_done, wl_done = sem("q_wh_done"), sem("q_wl_done")
        norm_done, xh_done, xl_done = sem("q_norm_done"), sem("q_xh_done"), sem("q_xl_done")
        mm_done, hi_done, lo_done = sem("q_mm_done"), sem("q_hi_done"), sem("q_lo_done")
        stored = [sem(f"q_stored{r}") for r in range(RING)]
        block = ctx.enter_context(nc.Block())

        def item(s):
            h, r = divmod(s, PER_HALF)
            return (h, r, None) if r < QK_TILES else (h, (r - QK_TILES) // 2, (r - QK_TILES) % 2)

        PIECE_AT = {1 + k: (1, k) for k in range(CT)}
        NEXT_AT = {PER_HALF + 2 + k: (0, k) for k in range(CT)}

        @block.sync
        def _(sp):
            sp.dma_start(bias[:, :], b_qkv[0:2 * C].rearrange("(m p) -> p m", p=P), allow_slow_non_contiguous=True).then_inc(bias_loaded, 16)
            for t in range(CT):
                if t >= 2:
                    sp.wait_ge(wl_done, t - 1)
                sp.dma_start(wst[:, t % 2, :], w_qkv[t * P:(t + 1) * P, :]).then_inc(w_loaded[t % 2], 16)
            for r in range(RING):
                sp.sem_inc(stored[r], 16 * ITEMS // RING)

            def batch(b):
                for s in range(ITEMS):
                    h, m, vc = item(s)
                    r = s % RING
                    sp.wait_ge(lo_done, after(b, ITEMS, s))
                    if vc is None:
                        kind = 0 if m < CT else 2
                        row = b * C + (m % CT) * P
                        sp.dma_start(qk_scr[kind:kind + 2, bass.ds(row, P), h * HALF:(h + 1) * HALF].rearrange("k p n -> p k n"),
                                     f(ob[:, r, :]).rearrange("p (k n) -> p k n", k=2)).then_inc(stored[r], 16)
                    else:
                        sp.dma_start(v_scr[bass.ds(b * HEADS + vc * VH, VH), :, h * (NT // 2) + m, :].rearrange("g p e -> p g e"),
                                     f(ob[:, r, 0:2 * VW]).rearrange("p (g e) -> p g e", g=VH)).then_inc(stored[r], 16)
            with sp.Fori(0, B) as b:
                batch(b)
            for r in range(RING):
                sp.wait_ge(stored[r], 16 * ITEMS // RING * (B + 1))

        @block.gpsimd
        def _(pool):
            pool.wait_ge(wl_done, CT)
            with pool.Fori(0, B) as b:
                pool.wait_ge(xl_done, after(b, PIECES, -1))
                pool.dma_start(xs[:, :, :], x[b].rearrange("(t p) n -> p t n", p=P)).then_inc(x_loaded, 16)

        @block.scalar
        def _(act):
            act.sem_inc(hi_done, ITEMS)
            act.sem_inc(xh_done, PIECES)
            for t in range(CT):
                act.wait_ge(w_loaded[t % 2], 16 * (t // 2 + 1))
                act.activation(wh[:, t, :], wst[:, t % 2, :], ACT.Copy).then_inc(wh_done, 1)
            act.wait_ge(bias_loaded, 16)

            def piece(b, h, t):
                act.wait_ge(norm_done, after(b, PIECES, h * CT + t))
                if t == 0:
                    act.wait_ge(mm_done, after(b, ITEMS, h * PER_HALF + PER_HALF - 1 - ITEMS))
                act.activation(xh[:, h, t, :], xs[:, t, h * HALF:(h + 1) * HALF], ACT.Copy).then_inc(xh_done, 1)

            for t in range(CT):
                piece(0, 0, t)

            def batch(b, last):
                for s in range(ITEMS):
                    if s in PIECE_AT:
                        piece(b, *PIECE_AT[s])
                    if s in NEXT_AT and not last:
                        piece(b + 1, *NEXT_AT[s])
                    h, m, vc = item(s)
                    r = s % RING
                    act.wait_ge(mm_done, after(b, ITEMS, s))
                    act.wait_ge(stored[r], 16 * after(b, ITEMS // RING, s // RING - 1))
                    if vc is None:
                        act.activation(ob[:, r, 0:HALF], ps[:, r, :], ACT.Identity, bias=bias[:, m:m + 1]).then_inc(hi_done, 1)
                    else:
                        dst = ob[:, r, 0:2 * VW].rearrange("p (g k e) -> p g k e", g=VH, k=2)[:, :, 0, :]
                        act.activation(dst, ps[:, r, 0:VW].rearrange("p (g e) -> p g e", g=VH), ACT.Copy).then_inc(hi_done, 1)
            if B > 1:
                with act.Fori(0, B - 1) as b:
                    batch(b, False)
            batch(B - 1, True)

        @block.vector
        def _(dve):
            for q, n in ((lo_done, ITEMS), (xl_done, PIECES), (norm_done, PIECES)):
                dve.sem_inc(q, n)
            for t in range(CT):
                dve.wait_ge(wh_done, t + 1)
                dve.tensor_tensor(wl[:, t, :], wst[:, t % 2, :], f(wh[:, t, :]), ALU.subtract).then_inc(wl_done, 1)
            dve.wait_ge(bias_loaded, 16)

            def norm(b, h, t):
                if h == 0 and t == 0:
                    dve.wait_ge(x_loaded, 16 * (b + 1))
                sl = xs[:, t, h * HALF:(h + 1) * HALF]
                col = b * CT + t
                dve.tensor_scalar(sl, sl, mean[:, bass.ds(col, 1)], rstd[:, bass.ds(col, 1)], ALU.subtract, ALU.mult).then_inc(norm_done, 1)

            def rest(b, h, t):
                dve.wait_ge(xh_done, after(b, PIECES, h * CT + t))
                dve.tensor_tensor(xl[:, h, t, :], xs[:, t, h * HALF:(h + 1) * HALF], f(xh[:, h, t, :]), ALU.subtract).then_inc(xl_done, 1)

            for t in range(CT):
                norm(0, 0, t)
            for t in range(CT):
                rest(0, 0, t)

            def batch(b, last):
                for s in range(ITEMS):
                    for table, bb in ((PIECE_AT, b), (NEXT_AT, b + 1)):
                        if table is NEXT_AT and last:
                            continue
                        if s + 1 in table:
                            norm(bb, *table[s + 1])
                        if s in table:
                            rest(bb, *table[s])
                    h, m, vc = item(s)
                    r = s % RING
                    dve.wait_ge(hi_done, after(b, ITEMS, s))
                    if vc is None:
                        dve.scalar_tensor_tensor(ob[:, r, HALF:2 * HALF], ps[:, r, :], bias[:, m:m + 1], f(ob[:, r, 0:HALF]),
                                                 ALU.add, ALU.subtract).then_inc(lo_done, 1)
                    else:
                        o4 = ob[:, r, 0:2 * VW].rearrange("p (g k e) -> p g k e", g=VH, k=2)
                        dve.tensor_tensor(o4[:, :, 1, :], ps[:, r, 0:VW].rearrange("p (g e) -> p g e", g=VH), f(o4[:, :, 0, :]),
                                          ALU.subtract).then_inc(lo_done, 1)
            if B > 1:
                with dve.Fori(0, B - 1) as b:
                    batch(b, False)
            batch(B - 1, True)

        @block.tensor
        def _(pe):
            pe.sem_inc(mm_done, ITEMS)
            pe.wait_ge(wl_done, CT)
            with pe.Fori(0, B) as b:
                for s in range(ITEMS):
                    h, m, vc = item(s)
                    r = s % RING
                    if s % PER_HALF == 0:
                        pe.wait_ge(xl_done, after(b, PIECES, h * CT + CT - 1))
                    pe.wait_ge(lo_done, after(b, ITEMS, s - RING))
                    k = 0
                    for t in range(CT):
                        for a, o in ((xh, wh), (xh, wl), (xl, wh)):
                            if vc is None:
                                mm = pe.matmul(ps[:, r, :], o[:, t, m * P:(m + 1) * P], a[:, h, t, :],
                                               start=(k == 0), stop=(k == 3 * CT - 1))
                            else:
                                mm = pe.matmul(ps[:, r, 0:VW], a[:, h, t, m * P:(m + 1) * P],
                                               o[:, t, 2 * C + vc * VW:2 * C + (vc + 1) * VW], start=(k == 0), stop=(k == 3 * CT - 1))
                            k += 1
                    mm.then_inc(mm_done, 1)


def attend_stage(nc, B, ident, qk_scr, v_scr, o_scr):
    HB = 3
    ST = HB * NT
    TURNS = B * HEADS // HB
    RS, RP = 2, 4
    LEAD_S, LEAD_M = 3, NT + 4
    POOL_KEYS = (2, 5)
    DVE_KEYS = [c for c in range(NT) if c not in POOL_KEYS]
    with ExitStack() as ctx:
        sb = lambda n, s, d=F32: ctx.enter_context(nc.sbuf_tensor(n, s, d))
        sem = lambda n: ctx.enter_context(nc.semaphore(n))
        k1 = sb("a_k1", [P, HB, N], F32R)
        k2 = sb("a_k2", [D + 1, HB, N], F32R)
        q1 = sb("a_q1", [P, HB, N], F32R)
        q2 = sb("a_q2", [D + 1, HB, N], F32R)
        v = sb("a_v", [P, HB, NT, 4, D], F32R)
        prob = sb("a_prob", [P, RP, N])
        ph = sb("a_ph", [P, RP, N], F32R)
        pl = sb("a_pl", [P, RP, N], F32R)
        mx = sb("a_mx", [P, HB, NT])
        rec = sb("a_rec", [D, 2, HALF])
        ob = sb("a_o", [D, HB, N])
        ps_s = ctx.enter_context(nc.psum_tensor("a_ps_s", [P, RS, N], F32))
        ps_m = ctx.enter_context(nc.psum_tensor("a_ps_m", [P, N], F32))
        ps_o = ctx.enter_context(nc.psum_tensor("a_ps_o", [P, N], F32))
        qk_loaded = [sem(f"a_qk_loaded{r}") for r in range(HB)]
        v_loaded = [sem(f"a_v_loaded{r}") for r in range(HB)]
        o_stored = [sem(f"a_o_stored{r}") for r in range(HB)]
        consts_set = sem("a_consts_set")
        max_mm, max_read, turned, shift_set = sem("a_max_mm"), sem("a_max_read"), sem("a_turned"), sem("a_shift_set")
        scores_done, exp_done, hi_done, dve_lo, pool_lo = (sem("a_scores_done"), sem("a_exp_done"), sem("a_hi_done"),
                                                           sem("a_dve_lo"), sem("a_pool_lo"))
        pv_done, rec_done, norm_done = sem("a_pv_done"), sem("a_rec_done"), sem("a_norm_done")
        block = ctx.enter_context(nc.Block())
        halves = [slice(h * HALF, (h + 1) * HALF) for h in range(2)]

        def wait_lo(eng, turn, s):
            h, c = s // NT, s % NT
            if c in POOL_KEYS:
                eng.wait_ge(pool_lo, after(turn, HB * len(POOL_KEYS), h * len(POOL_KEYS) + POOL_KEYS.index(c)))
            else:
                eng.wait_ge(dve_lo, after(turn, HB * len(DVE_KEYS), h * len(DVE_KEYS) + DVE_KEYS.index(c)))

        @block.sync
        def _(sp):
            for r in range(HB):
                sp.sem_inc(o_stored[r], 16)
            sp.wait_ge(consts_set, 3)

            def load_qk(g, r):
                rows = bass.ds(g * D, D)
                for dst, kind in ((q1[0:D, r, :], 0), (k2[0:D, r, :], 2), (k1[0:D, r, :], 2), (k1[D:P, r, :], 3),
                                  (q1[D:P, r, :], 0), (q2[0:D, r, :], 1)):
                    sp.dma_start(f(dst), qk_scr[kind, rows, :]).then_inc(qk_loaded[r], 16)

            def load_v(g, r):
                sp.dma_start(f(v[:, r, :, 0::2, :]).rearrange("p c k e -> p (c k) e"), v_scr[g].rearrange("p c (k e) -> p (c k) e", k=2)).then_inc(v_loaded[r], 16)

            for r in range(HB):
                load_qk(r, r)
                load_v(r, r)

            def turn(i, last):
                for r in range(HB):
                    if not last:
                        sp.wait_ge(scores_done, after(i, ST, r * NT + NT - 1))
                        load_qk(i * HB + (HB + r), r)
                        sp.wait_ge(pv_done, after(i, 2 * ST, 2 * (r * NT + NT) - 1))
                        load_v(i * HB + (HB + r), r)
                    sp.wait_ge(norm_done, after(i, 2 * HB, 2 * r + 1))
                    sp.dma_start(o_scr[bass.ds((i * HB + r) * D, D), :], ob[:, r, :]).then_inc(o_stored[r], 16)
            with sp.Fori(0, TURNS - 1) as i:
                turn(i, False)
            turn(TURNS - 1, True)
            for r in range(HB):
                sp.wait_ge(o_stored[r], 16 * (TURNS + 1))

        @block.tensor
        def _(pe):
            for q, n in ((max_mm, ST), (turned, HB), (scores_done, ST), (pv_done, 2 * ST)):
                pe.sem_inc(q, n)

            def row_max(i, s):
                j, s = divmod(s, ST)
                i, r, c = i + j, s // NT, s % NT
                if c == 0:
                    pe.wait_ge(qk_loaded[r], 96 * (i + 1))
                    pe.wait_ge(shift_set, after(i, HB, r - 1))
                pe.wait_ge(max_read, after(i, ST, s - 1))
                for h in halves:
                    mm = pe.matmul(ps_m[:, h], q1[0:D, r, c * P:(c + 1) * P], k2[0:D, r, h], start=True, stop=True)
                mm.then_inc(max_mm, 1)

            def turn_max(i, r):
                j, r = divmod(r, HB)
                i = i + j
                pe.wait_ge(max_read, after(i, ST, r * NT + NT - 1))
                for c in range(NT):
                    mm = pe.transpose(ps_m[0:1, c * P:(c + 1) * P], mx[:, r, c:c + 1], ident[:, :])
                mm.then_inc(turned, 1)

            def scores(i, s):
                j, s = divmod(s, ST)
                i, r, c = i + j, s // NT, s % NT
                if c == 0:
                    pe.wait_ge(shift_set, after(i, HB, r))
                pe.wait_ge(exp_done, after(i, ST, s - RS))
                for h in halves:
                    pe.matmul(ps_s[:, s % RS, h], k1[:, r, c * P:(c + 1) * P], q1[:, r, h], start=True, stop=False)
                    mm = pe.matmul(ps_s[:, s % RS, h], k2[:, r, c * P:(c + 1) * P], q2[:, r, h], start=False, stop=True)
                mm.then_inc(scores_done, 1)

            def weighted(i, s):
                r, c, w = s // NT, s % NT, s % RP
                pe.wait_ge(hi_done, after(i, ST, s))
                wait_lo(pe, i, s)
                if c == 0:
                    pe.wait_ge(v_loaded[r], 16 * (i + 1))
                vo = v[:, r, c, 0:2, :].rearrange("p k e -> p (k e)")
                vz = v[:, r, c, 2:4, :].rearrange("p k e -> p (k e)")
                for n, h in enumerate(halves):
                    if c == 0:
                        pe.wait_ge(norm_done, after(i, 2 * HB, 2 * (r - 1) + n))
                    pe.matmul(ps_o[:, h], vo, ph[:, w, h], start=(c == 0), stop=False)
                    pe.matmul(ps_o[:, h], vo, pl[:, w, h], start=False, stop=False)
                    pe.matmul(ps_o[:, h], vz, ph[:, w, h], start=False, stop=(c == NT - 1)).then_inc(pv_done, 1)

            for s in range(NT):
                row_max(0, s)
            turn_max(0, 0)
            for s in range(LEAD_S):
                scores(0, s)
                row_max(0, NT + s)
            row_max(0, NT + LEAD_S)

            def turn(i, last):
                for s in range(ST):
                    weighted(i, s)
                    if s % NT == LEAD_M - NT and not (last and s // NT == HB - 1):
                        turn_max(i, s // NT + 1)
                    if not (last and s + LEAD_S >= ST):
                        scores(i, s + LEAD_S)
                    if not (last and s + LEAD_M >= ST):
                        row_max(i, s + LEAD_M)
            with pe.Fori(0, TURNS - 1) as i:
                turn(i, False)
            turn(TURNS - 1, True)

        @block.scalar
        def _(act):
            for q, n in ((exp_done, ST), (hi_done, ST), (shift_set, HB)):
                act.sem_inc(q, n)

            def shift(i, r):
                j, r = divmod(r, HB)
                i = i + j
                act.wait_ge(turned, after(i, HB, r))
                act.wait_ge(qk_loaded[r], 96 * (i + 1))
                act.activation(q2[D:D + 1, r, :], ps_m[0:1, :], ACT.Copy, scale=-1.0).then_inc(shift_set, 1)

            def exps(i, s):
                j, s = divmod(s, ST)
                i = i + j
                act.wait_ge(scores_done, after(i, ST, s))
                wait_lo(act, *((i, s - RP) if s >= RP else (i - 1, s - RP + ST)))
                act.activation(prob[:, s % RP, :], ps_s[:, s % RS, :], ACT.Exp, scale=1 / math.sqrt(D)).then_inc(exp_done, 1)

            def high(i, s):
                j, s = divmod(s, ST)
                i = i + j
                act.wait_ge(exp_done, after(i, ST, s))
                act.wait_ge(pv_done, after(i, 2 * ST, 2 * (s - RP) + 1))
                act.activation(ph[:, s % RP, :], prob[:, s % RP, :], ACT.Copy).then_inc(hi_done, 1)

            shift(0, 0)
            exps(0, 0)
            exps(0, 1)
            high(0, 0)

            def turn(i, last):
                for s in range(ST):
                    if not (last and s + 2 >= ST):
                        exps(i, s + 2)
                    if s % NT == LEAD_M - NT and not (last and s // NT == HB - 1):
                        shift(i, s // NT + 1)
                    if not (last and s + 1 >= ST):
                        high(i, s + 1)
            with act.Fori(0, TURNS - 1) as i:
                turn(i, False)
            turn(TURNS - 1, True)

        @block.vector
        def _(dve):
            for q, n in ((max_read, ST), (dve_lo, HB * len(DVE_KEYS)), (rec_done, 2 * HB), (norm_done, 2 * HB)):
                dve.sem_inc(q, n)
            dve.memset(f(k2[D:D + 1, :, :]), 1.0).then_inc(consts_set, 1)
            dve.memset(f(v[:, :, :, 1, :]), 1.0).then_inc(consts_set, 1)
            dve.memset(f(v[:, :, :, 3, :]), 0.0).then_inc(consts_set, 1)

            def take_max(i, s):
                j, s = divmod(s, ST)
                i, r, c = i + j, s // NT, s % NT
                dve.wait_ge(max_mm, after(i, ST, s))
                if c == 0:
                    dve.wait_ge(turned, after(i, HB, r - HB))
                dve.reduce_max(mx[:, r, c:c + 1], ps_m[:, :], axis=AX.X).then_inc(max_read, 1)

            def low(i, s):
                j, s = divmod(s, ST)
                i, w = i + j, s % RP
                if s % NT in POOL_KEYS:
                    return
                dve.wait_ge(hi_done, after(i, ST, s))
                dve.wait_ge(pv_done, after(i, 2 * ST, 2 * (s - RP) + 1))
                dve.tensor_tensor(pl[:, w, :], prob[:, w, :], f(ph[:, w, :]), ALU.subtract).then_inc(dve_lo, 1)

            def normalise(i, r):
                for n, h in enumerate(halves):
                    dve.wait_ge(pv_done, after(i, 2 * ST, 2 * (r * NT + NT - 1) + n))
                    dve.reciprocal(rec[:, n, :], ps_o[D:P, h]).then_inc(rec_done, 1)
                    if n == 0:
                        dve.wait_ge(o_stored[r], 16 * (i + 1))
                    dve.wait_ge(rec_done, after(i, 2 * HB, 2 * r + n))
                    dve.tensor_tensor(ob[:, r, h], ps_o[0:D, h], rec[:, n, :], ALU.mult).then_inc(norm_done, 1)

            for s in range(LEAD_M - 1):
                take_max(0, s)
            low(0, 0)

            def turn(i, last):
                for s in range(ST):
                    if not (last and s + LEAD_M - 1 >= ST):
                        take_max(i, s + LEAD_M - 1)
                    if not (last and s + 1 >= ST):
                        low(i, s + 1)
                    if s % NT == NT - 1:
                        normalise(i, s // NT)
            with dve.Fori(0, TURNS - 1) as i:
                turn(i, False)
            turn(TURNS - 1, True)

        @block.gpsimd
        def _(pool):
            pool.sem_inc(pool_lo, HB * len(POOL_KEYS))
            with pool.Fori(0, TURNS) as i:
                for s in range(ST):
                    if s % NT in POOL_KEYS:
                        w = s % RP
                        pool.wait_ge(hi_done, after(i, ST, s))
                        pool.wait_ge(pv_done, after(i, 2 * ST, 2 * (s - RP) + 1))
                        pool.tensor_tensor(pl[:, w, :], prob[:, w, :], f(ph[:, w, :]), ALU.subtract).then_inc(pool_lo, 1)


W1C, W2C = 3 * BS, 2 * 2 * BS
WCOLS = 2 * (W1C + W2C)


def project_stage(nc, B, x, w_proj, b_proj, b_v, w1, w2, b2, o_scr, x1_scr, w_scr, avg, mean, rstd):
    RING = 4
    ITEMS = 2 * CT
    PIECES = 2 * CT
    with ExitStack() as ctx:
        sb = lambda n, s, d=F32: ctx.enter_context(nc.sbuf_tensor(n, s, d))
        sem = lambda n: ctx.enter_context(nc.semaphore(n))
        wh, wl = sb("p_wh", [P, CT, C], F32R), sb("p_wl", [P, CT, C], F32R)
        ws = sb("p_ws", [P, CT, C])
        bp, bv = sb("p_bp", [P, CT]), sb("p_bv", [P, CT])
        of = sb("p_o", [P, 2, CT, HALF])
        oh, ol = sb("p_oh", [P, 2, CT, HALF], F32R), sb("p_ol", [P, 2, CT, HALF], F32R)
        xt = sb("p_x", [P, RING, HALF])
        fw = sb("p_fw", [BS + 1, WCOLS], F32R)
        fs = sb("p_fs", [BS + 1, 2, BS, 2])
        fa = sb("p_fa", [BS + 1, W1C + W2C])
        bn = sb("p_bn", [P, 12 * CT])
        bn_all = sb("p_bn_all", [P, B * 12 * CT])
        mv = sb("p_mv", [P, B * CT, 2])
        small = sb("p_small", [P, 2, B * CT])
        ps = ctx.enter_context(nc.psum_tensor("p_ps", [P, RING, 512], F32))
        ps_g = ctx.enter_context(nc.psum_tensor("p_ps_g", [P, 512], F32))
        w_loaded, wh_done, wl_done = sem("p_w_loaded"), sem("p_wh_done"), sem("p_wl_done")
        fs_loaded, fa_done, fh_done, fl_done, fw_stored = sem("p_fs_loaded"), sem("p_fa_done"), sem("p_fh_done"), sem("p_fl_done"), sem("p_fw_stored")
        o_loaded = [sem("p_o_loaded0"), sem("p_o_loaded1")]
        x_loaded = [sem(f"p_x_loaded{r}") for r in range(RING)]
        stored = [sem(f"p_stored{r}") for r in range(RING)]
        oh_done, ol_done, mm_done, add_done = sem("p_oh_done"), sem("p_ol_done"), sem("p_mm_done"), sem("p_add_done")
        bn_done, kept, agg_done = sem("p_bn_done"), sem("p_kept"), sem("p_agg_done")
        sems = (sem("p_dve_ready"), sem("p_pe_done"), sem("p_act_done"))
        block = ctx.enter_context(nc.Block())
        half = lambda h: slice(h * HALF, (h + 1) * HALF)

        @block.sync
        def _(sp):
            sp.dma_start(ws[:, :, :], w_proj.rearrange("(t p) n -> p t n", p=P)).then_inc(w_loaded, 16)
            sp.dma_start(bp[:, :], b_proj.rearrange("(m p) -> p m", p=P), allow_slow_non_contiguous=True).then_inc(w_loaded, 16)
            sp.dma_start(bv[:, :], b_v.rearrange("(m p) -> p m", p=P), allow_slow_non_contiguous=True).then_inc(w_loaded, 16)
            for r in range(RING):
                sp.sem_inc(stored[r], 16 * ITEMS // RING)

            def load_o(b, h):
                sp.wait_ge(ol_done, after(b, PIECES, h * CT + CT - 1 - PIECES))
                sp.dma_start(of[:, h, :, :], o_scr[bass.ds(b * C, C), half(h)].rearrange("(t p) n -> p t n", p=P)).then_inc(o_loaded[h], 16)

            def batch(b, last):
                for s in range(ITEMS):
                    h, m, r = s // CT, s % CT, s % RING
                    if s in (0, 3) and not last:
                        load_o(b + 1, s // 3)
                    sp.wait_ge(add_done, after(b, ITEMS, s))
                    sp.dma_start(x1_scr[bass.ds(b * C + m * P, P), half(h)], xt[:, r, :]).then_inc(stored[r], 16)

            load_o(0, 0)
            load_o(0, 1)
            if B > 1:
                with sp.Fori(0, B - 1) as b:
                    batch(b, False)
            batch(B - 1, True)
            for r in range(RING):
                sp.wait_ge(stored[r], 16 * ITEMS // RING * (B + 1))

        @block.gpsimd
        def _(pool):
            for blk in range(NBLK):
                if blk:
                    pool.wait_ge(fa_done, 5 * blk)
                pool.dma_start(fs[0:BS, 0, :, :], w1[blk]).then_inc(fs_loaded, 16)
                pool.dma_start(fs[0:BS, 1, :, :], w2[blk]).then_inc(fs_loaded, 16)
                pool.dma_start(fs[BS:BS + 1, 1, :, :], b2[blk:blk + 1]).then_inc(fs_loaded, 16)
                pool.wait_ge(fl_done, blk + 1)
                pool.dma_start(w_scr[blk], f(fw[:, :])).then_inc(fw_stored, 16)
            with pool.Fori(0, B) as b:
                for s in range(ITEMS):
                    h, m, r = s // CT, s % CT, s % RING
                    pool.wait_ge(stored[r], 16 * after(b, ITEMS // RING, s // RING - 1))
                    pool.wait_ge(bn_done, after(b, ITEMS, s - RING))
                    pool.dma_start(xt[:, r, :], x[b, m * P:(m + 1) * P, half(h)]).then_inc(x_loaded[r], 16)
            pool.wait_ge(fw_stored, 16 * NBLK)

        @block.scalar
        def _(act):
            act.sem_inc(oh_done, PIECES)
            act.wait_ge(w_loaded, 48)
            act.activation(wh[:, :, :], ws[:, :, :], ACT.Copy).then_inc(wh_done, 1)
            for blk in range(NBLK):
                act.wait_ge(fa_done, 5 * (blk + 1))
                if blk:
                    act.wait_ge(fw_stored, 16 * blk)
                act.activation(fw[:, 0:WCOLS // 2], fa[:, :], ACT.Copy).then_inc(fh_done, 1)
            with act.Fori(0, B) as b:
                for h in range(2):
                    act.wait_ge(o_loaded[h], 16 * (b + 1))
                    act.wait_ge(mm_done, after(b, ITEMS, h * CT + CT - 1 - ITEMS))
                    for t in range(CT):
                        act.activation(oh[:, h, t, :], of[:, h, t, :], ACT.Identity, bias=bv[:, t:t + 1]).then_inc(oh_done, 1)
            finish_stats(nc, (None, None, act), mv, B * CT, avg, mean[:, :], rstd[:, :], small, ps_g, sems)[2]()

        @block.vector
        def _(dve):
            for q, n in ((ol_done, PIECES), (add_done, ITEMS), (bn_done, ITEMS)):
                dve.sem_inc(q, n)
            dve.wait_ge(wh_done, 1)
            dve.tensor_tensor(wl[:, :, :], ws[:, :, :], f(wh[:, :, :]), ALU.subtract).then_inc(wl_done, 1)
            dve.memset(fa[BS:BS + 1, :], 0.0).then_inc(wl_done, 1)
            dve.wait_ge(wl_done, 2)
            for blk in range(NBLK):
                dve.wait_ge(fs_loaded, 48 * (blk + 1))
                if blk:
                    dve.wait_ge(fl_done, blk)
                a1 = fa[0:BS, 0:W1C].rearrange("p (k n) -> p k n", k=3)
                a2 = fa[0:BS, W1C:].rearrange("p (k n) -> p k n", k=4)
                s1, s2 = fs[0:BS, 0, :, :].rearrange("p n k -> p k n"), fs[0:BS, 1, :, :].rearrange("p n k -> p k n")
                dve.tensor_copy(a1[:, 0:2, :], s1).then_inc(fa_done, 1)
                dve.tensor_scalar(a1[:, 2, :], s1[:, 1, :], -1.0, None, ALU.mult).then_inc(fa_done, 1)
                dve.tensor_copy(a2[:, 0:2, :], s2).then_inc(fa_done, 1)
                dve.tensor_scalar(a2[:, 2, :], s2[:, 1, :], -1.0, None, ALU.mult)
                dve.tensor_copy(a2[:, 3, :], s2[:, 0, :]).then_inc(fa_done, 1)
                dve.tensor_copy(fa[BS:BS + 1, W1C:W1C + 2 * BS].rearrange("p (k n) -> p k n", k=2),
                                fs[BS:BS + 1, 1, :, :].rearrange("p n k -> p k n")).then_inc(fa_done, 1)
                dve.wait_ge(fh_done, blk + 1)
                dve.tensor_tensor(fw[:, WCOLS // 2:], fa[:, :], f(fw[:, 0:WCOLS // 2]), ALU.subtract).then_inc(fl_done, 1)
            bnv = bn[:, :].rearrange("p (t h s) -> p t h s", t=CT, h=2)

            def split(b, h):
                for t in range(CT):
                    dve.wait_ge(oh_done, after(b, PIECES, h * CT + t))
                    dve.scalar_tensor_tensor(ol[:, h, t, :], of[:, h, t, :], bv[:, t:t + 1], f(oh[:, h, t, :]),
                                             ALU.add, ALU.subtract).then_inc(ol_done, 1)
            split(0, 0)

            def batch(b, last):
                for s in range(ITEMS):
                    h, m, r = s // CT, s % CT, s % RING
                    if s == 1:
                        split(b, 1)
                    if s == CT + 1 and not last:
                        split(b + 1, 0)
                    dve.wait_ge(mm_done, after(b, ITEMS, s))
                    dve.wait_ge(x_loaded[r], 16 * (b * (ITEMS // RING) + s // RING + 1))
                    dve.scalar_tensor_tensor(xt[:, r, :], ps[:, r, :], bp[:, m:m + 1], xt[:, r, :], ALU.add, ALU.add).then_inc(add_done, 1)
                    dve.wait_ge(add_done, after(b, ITEMS, s))
                    dve.bn_stats(bnv[:, m, h, :], xt[:, r, :]).then_inc(bn_done, 1)
                dve.wait_ge(bn_done, after(b, ITEMS, ITEMS - 1))
                dve.tensor_scalar(bn_all[:, bass.ds(b * 12 * CT, 12 * CT)], bn[:, :], 1.0, None, ALU.mult).then_inc(kept, 1)
            if B > 1:
                with dve.Fori(0, B - 1) as b:
                    batch(b, False)
            batch(B - 1, True)
            dve.wait_ge(kept, B)
            for t in range(B * CT):
                dve.bn_aggr(mv[:, t, :], bn_all[:, 12 * t:12 * t + 12]).then_inc(agg_done, 1)
            dve.wait_ge(agg_done, B * CT)
            finish_stats(nc, (dve, None, None), mv, B * CT, avg, mean[:, :], rstd[:, :], small, ps_g, sems)[0]()

        @block.tensor
        def _(pe):
            pe.sem_inc(mm_done, ITEMS)
            pe.wait_ge(wl_done, 1)
            with pe.Fori(0, B) as b:
                for s in range(ITEMS):
                    h, m, r = s // CT, s % CT, s % RING
                    if m == 0:
                        pe.wait_ge(ol_done, after(b, PIECES, h * CT + CT - 1))
                    pe.wait_ge(add_done, after(b, ITEMS, s - RING))
                    k = 0
                    for t in range(CT):
                        for a, o in ((oh, wh), (oh, wl), (ol, wh)):
                            mm = pe.matmul(ps[:, r, :], o[:, t, m * P:(m + 1) * P], a[:, h, t, :], start=(k == 0), stop=(k == 3 * CT - 1))
                            k += 1
                    mm.then_inc(mm_done, 1)
            finish_stats(nc, (None, pe, None), mv, B * CT, avg, mean[:, :], rstd[:, :], small, ps_g, sems)[1]()


HN = HALF // P
KCH = 5
REST = FQ - 2 * P


def filter_stage(nc, B, ident, df_in, di_in, b1, x1_scr, w_scr, mean, rstd, out):
    QT = 3
    QB = NBLK // 2
    QC = QT * P
    TURNS = 2 * B
    T2 = largest_square()
    HP = 4 * FQ + P - REST
    with ExitStack() as ctx:
        sb = lambda n, s, d=F32: ctx.enter_context(nc.sbuf_tensor(n, s, d))
        sem = lambda n: ctx.enter_context(nc.semaphore(n))
        df = sb("f_df", [P, 2, 2, HN, 2 * FQ], F32R)
        di = sb("f_di", [P, 2, 2, KCH, HALF], F32R)
        wt = sb("f_w", [BS + 1, 2, WCOLS], F32R)
        bt = sb("f_b1", [BS, 2, 2])
        xs = sb("f_x", [P, QT, N])
        ev = sb("f_ev", [P, QT, HALF])
        xt = sb("f_xt", [P, 2, NT, QC], F32R)
        xf = sb("f_xf", [BS, 2, 2, 4, FQ], F32R)
        hf = sb("f_hf", [BS, 2, FQ])
        sq = sb("f_sq", [BS, 2, FQ])
        hh = sb("f_hh", [BS + 1, 2, HP], F32R)
        y = sb("f_y", [P, 2, 2, KCH, QC], F32R)
        xr = sb("f_xr", [P, QT, N])
        ps_f = ctx.enter_context(nc.psum_tensor("f_ps_f", [P, 2, 512], F32))
        ps_a = ctx.enter_context(nc.psum_tensor("f_ps_a", [P, 2, 512], F32))
        ps_b = ctx.enter_context(nc.psum_tensor("f_ps_b", [P, 2, 512], F32))
        ps_i = ctx.enter_context(nc.psum_tensor("f_ps_i", [P, 2, 512], F32))
        c_loaded = [sem("f_c_loaded0"), sem("f_c_loaded1")]
        c_hi, c_lo, pad_set = sem("f_c_hi"), sem("f_c_lo"), sem("f_pad_set")
        w_loaded = [sem("f_w_loaded0"), sem("f_w_loaded1")]
        x_loaded = sem("f_x_loaded")
        r_loaded = [sem(f"f_r_loaded{t}") for t in range(QT)]
        stored = [sem(f"f_stored{t}") for t in range(QT)]
        norm_done, fold_done = sem("f_norm_done"), sem("f_fold_done")
        t_mm, t_hi, t_lo = sem("f_t_mm"), sem("f_t_hi"), sem("f_t_lo")
        f_mm, f_hi, f_lo = sem("f_f_mm"), sem("f_f_hi"), sem("f_f_lo")
        a_mm, a_out, sq_done, mag_done, mask_done, h_hi, h_lo = (sem("f_a_mm"), sem("f_a_out"), sem("f_sq_done"), sem("f_mag_done"), sem("f_mask_done"),
                                                                 sem("f_h_hi"), sem("f_h_lo"))
        b_mm, y_hi, y_lo = sem("f_b_mm"), sem("f_y_hi"), sem("f_y_lo")
        i_mm, add1, add2 = sem("f_i_mm"), sem("f_add1"), sem("f_add2")
        block = ctx.enter_context(nc.Block())
        FI = 4 * QB
        TI = NT
        BI = 2 * 3 * QB
        RI = FI + TI
        CONST = ([("d", p, t) for p in range(2) for t in range(HN)] + [("i", p, c) for p in range(2) for c in range(KCH)])

        def cslot(n):
            kind, p, t = CONST[n]
            width = 2 * FQ if kind == "d" else HALF
            src = (df_in if kind == "d" else di_in)[:, p, t, :]
            dst = (df if kind == "d" else di)
            return xs[:, n % 2, 0:width], src, dst[:, 0, p, t, :], dst[:, 1, p, t, :]

        @block.sync
        def _(sp):
            for n in range(len(CONST)):
                if n >= 2:
                    sp.wait_ge(c_lo, n - 1)
                st, src, _, _ = cslot(n)
                sp.dma_start(st, src).then_inc(c_loaded[n % 2], 16)
            for t in range(QT):
                sp.sem_inc(stored[t], 16)
            sp.wait_ge(c_lo, len(CONST))

            def load_x(k):
                sp.dma_start(xs[:, :, :], x1_scr[bass.ds(k * QC, QC), :].rearrange("(t p) n -> p t n", p=P)).then_inc(x_loaded, 16)

            load_x(0)

            def turn(k, par, last):
                for j in range(QB):
                    sp.wait_ge(b_mm, after(k, BI, (j - 2) * 6 + 5))
                    blk = par * QB + j
                    sp.dma_start(f(wt[:, j % 2, :]), w_scr[bass.ds(blk, 1), :, :].rearrange("a p n -> p (a n)")).then_inc(w_loaded[j % 2], 16)
                    sp.dma_start(bt[:, j % 2, :], b1[bass.ds(blk, 1), :, :].rearrange("a p n -> p (a n)")).then_inc(w_loaded[j % 2], 16)
                    if j == 1 and not last:
                        sp.wait_ge(fold_done, after(k, 2 * QT, 2 * QT - 1))
                        sp.wait_ge(t_mm, after(k, TI, TI - 1))
                        load_x(k + 1)
                    if j == 1:
                        for t in range(QT):
                            sp.wait_ge(stored[t], 16 * (k + 1))
                            sp.dma_start(xr[:, t, :], x1_scr[bass.ds(k * QC + t * P, P), :]).then_inc(r_loaded[t], 16)
                for t in range(QT):
                    sp.wait_ge(add2, after(k, 2 * QT, 2 * t + 1))
                    sp.dma_start(out[bass.ds(k * QC + t * P, P), :], xr[:, t, :]).then_inc(stored[t], 16)
            with sp.Fori(0, TURNS - 1) as k:
                turn(k, k % 2, False)
            turn(TURNS - 1, 1, True)
            for t in range(QT):
                sp.wait_ge(stored[t], 16 * (TURNS + 1))

        @block.tensor
        def _(pe):
            for q, n in ((t_mm, TI), (f_mm, FI), (a_mm, 4 * QB), (b_mm, BI), (i_mm, 2 * QT)):
                pe.sem_inc(q, n)
            pe.wait_ge(c_lo, len(CONST))
            pe.wait_ge(pad_set, 4)

            def turned(k, ts):
                for n in ts:
                    par, t = divmod(n, HN)
                    src = ev if par == 0 else xs
                    if n == 0:
                        pe.wait_ge(fold_done, after(k, 2 * QT, 2 * QT - 1))
                    if n >= 2:
                        pe.wait_ge(t_lo, after(k, TI, n - 2))
                    else:
                        pe.wait_ge(f_lo, after(k, FI, n - 2))
                    for q in range(QT):
                        lo = (0 if par == 0 else HALF) + t * P
                        mm = pe.transpose(ps_f[:, n % 2, q * P:(q + 1) * P], src[:, q, lo:lo + P], ident[:, :])
                    mm.then_inc(t_mm, 1)

            def forward(k, j):
                for n in range(4):
                    par, ri = divmod(n, 2)
                    i = 4 * j + n
                    if i == 0:
                        pe.wait_ge(t_lo, after(k, TI, TI - 1))
                    if i >= 2:
                        pe.wait_ge(f_lo, after(k, FI, i - 2))
                    q = 0
                    for t in range(HN):
                        for a, c in ((0, 0), (0, 1), (1, 0)):
                            mm = pe.matmul(ps_f[0:BS, i % 2, 0:FQ], xt[:, a, par * HN + t, j * BS:(j + 1) * BS],
                                           df[:, c, par, t, ri * FQ:(ri + 1) * FQ], start=(q == 0), stop=(q == 3 * HN - 1))
                            q += 1
                    mm.then_inc(f_mm, 1)

            def first(k, j):
                w = wt[0:BS, j % 2, :].rearrange("p (a n) -> p a n", a=2)
                pe.wait_ge(w_loaded[j % 2], 64 * k + 32 * (j // 2 + 1))
                for n in range(4):
                    par, ri = divmod(n, 2)
                    i = 4 * j + n
                    pe.wait_ge(f_lo, after(k, FI, 4 * j + 2 * par + 1))
                    pe.wait_ge(a_out, after(k, FI, i - 2))
                    q = 0
                    for s, col in ((0, 0 if ri == 0 else 1), (1, 2 if ri == 0 else 0)):
                        for a, c in ((0, 0), (0, 1), (1, 0)):
                            mm = pe.matmul(ps_a[0:BS, i % 2, 0:FQ], w[:, c, col * BS:(col + 1) * BS],
                                           xf[:, j % 2, a, 2 * par + s, :], start=(q == 0), stop=(q == 5))
                            q += 1
                    mm.then_inc(a_mm, 1)

            def second(k, j):
                w = wt[:, j % 2, :].rearrange("p (a n) -> p a n", a=2)
                pe.wait_ge(h_lo, after(k, 2 * QB, 2 * j + 1))
                for n in range(6):
                    par, ch = divmod(n, 3)
                    i = 6 * j + n
                    pe.wait_ge(y_lo, after(k, BI, i - 2))
                    q = 0
                    for s in range(2):
                        rows = BS + 1 if s == 0 else BS
                        col = (2 * par + s) * FQ + ch * P
                        for a, c in ((0, 0), (0, 1), (1, 0)):
                            mm = pe.matmul(ps_b[:, i % 2, 0:2 * BS], hh[0:rows, a, col:col + P],
                                           w[0:rows, c, W1C + s * 2 * BS:W1C + (s + 1) * 2 * BS], start=(q == 0), stop=(q == 5))
                            q += 1
                    mm.then_inc(b_mm, 1)

            def inverse(k, t):
                pe.wait_ge(y_lo, after(k, BI, 6 * min(QB - 1, ((t + 1) * P - 1) // BS) + 5))
                for par in range(2):
                    pe.wait_ge(add2, after(k, 2 * QT, 2 * t - 1))
                    q = 0
                    for c in range(KCH):
                        rows = P if c < KCH - 1 else 64
                        for a, e in ((0, 0), (0, 1), (1, 0)):
                            mm = pe.matmul(ps_i[:, par, :], y[0:rows, a, par, c, t * P:(t + 1) * P], di[0:rows, e, par, c, :],
                                           start=(q == 0), stop=(q == 3 * KCH - 1))
                            q += 1
                    mm.then_inc(i_mm, 1)

            turned(0, range(TI))

            def turn(k, last):
                forward(k, 0)
                forward(k, 1)
                first(k, 0)
                forward(k, 2)
                second(k, 0)
                first(k, 1)
                forward(k, 3)
                second(k, 1)
                first(k, 2)
                inverse(k, 0)
                second(k, 2)
                first(k, 3)
                inverse(k, 1)
                second(k, 3)
                if not last:
                    turned(k + 1, range(TI))
                inverse(k, 2)
            with pe.Fori(0, TURNS - 1) as k:
                turn(k, False)
            turn(TURNS - 1, True)

        @block.scalar
        def _(act):
            for q, n in ((t_hi, TI), (f_hi, FI), (a_out, FI), (sq_done, 2 * QB), (h_hi, 2 * QB), (y_hi, BI)):
                act.sem_inc(q, n)
            for n in range(len(CONST)):
                st, _, hi, _ = cslot(n)
                act.wait_ge(c_loaded[n % 2], 16 * (n // 2 + 1))
                act.activation(hi, st, ACT.Copy).then_inc(c_hi, 1)
            act.wait_ge(pad_set, 4)

            def turned(k):
                for n in range(TI):
                    act.wait_ge(t_mm, after(k, TI, n))
                    if n == 0:
                        act.wait_ge(f_mm, after(k, FI, -1))
                    act.activation(xt[:, 0, n, :], ps_f[:, n % 2, 0:QC], ACT.Copy).then_inc(t_hi, 1)

            def forward(k, j):
                for n in range(4):
                    i = 4 * j + n
                    act.wait_ge(f_mm, after(k, FI, i))
                    if n == 0:
                        act.wait_ge(a_mm, after(k, FI, 4 * (j - 2) + 3))
                    act.activation(xf[:, j % 2, 0, n, :], ps_f[0:BS, i % 2, 0:FQ], ACT.Copy).then_inc(f_hi, 1)

            def first(k, j):
                for par in range(2):
                    u = 2 * j + par
                    if par == 0:
                        act.wait_ge(w_loaded[j % 2], 64 * k + 32 * (j // 2 + 1))
                    act.wait_ge(h_lo, after(k, 2 * QB, u - 1))
                    for ri in range(2):
                        i = 2 * u + ri
                        act.wait_ge(a_mm, after(k, FI, i))
                        act.activation(hf[:, ri, :], ps_a[0:BS, i % 2, 0:FQ], ACT.Identity, bias=bt[:, j % 2, ri:ri + 1]).then_inc(a_out, 1)
                    act.wait_ge(a_out, after(k, FI, 2 * u + 1))
                    act.wait_ge(mag_done, after(k, 2 * QB, u - 1))
                    act.activation(sq[:, :, :], hf[:, :, :], ACT.Square).then_inc(sq_done, 1)
                    act.wait_ge(mag_done, after(k, 2 * QB, u))
                    if par == 0:
                        act.wait_ge(b_mm, after(k, BI, 6 * (j - 1) + 5))
                    act.activation(hh[0:BS, 0, 2 * par * FQ:2 * (par + 1) * FQ], hf[:, :, :].rearrange("p r n -> p (r n)"), ACT.Copy).then_inc(h_hi, 1)

            def second(k, j):
                for n in range(6):
                    par, ch = divmod(n, 3)
                    i = 6 * j + n
                    act.wait_ge(b_mm, after(k, BI, i))
                    if j == 0 and n == 0:
                        act.wait_ge(i_mm, after(k, 2 * QT, -1))
                    src = ps_b[:, i % 2, 0:2 * BS].rearrange("p (r n) -> p r n", r=2)
                    cs = slice(j * BS, (j + 1) * BS)
                    if ch < 2:
                        act.activation(y[:, 0, par, ch:ch + 3:2, cs], src, ACT.Copy).then_inc(y_hi, 1)
                    else:
                        act.activation(y[0:REST, 0, par, KCH - 1, cs], src[0:REST, 0, :], ACT.Copy)
                        act.activation(y[32:32 + REST, 0, par, KCH - 1, cs], src[0:REST, 1, :], ACT.Copy).then_inc(y_hi, 1)

            turned(0)

            def turn(k, last):
                forward(k, 0)
                forward(k, 1)
                first(k, 0)
                forward(k, 2)
                second(k, 0)
                first(k, 1)
                forward(k, 3)
                second(k, 1)
                first(k, 2)
                second(k, 2)
                first(k, 3)
                second(k, 3)
                if not last:
                    turned(k + 1)
            with act.Fori(0, TURNS - 1) as k:
                turn(k, False)
            turn(TURNS - 1, True)

        @block.vector
        def _(dve):
            for q, n in ((norm_done, QT), (fold_done, 2 * QT), (t_lo, TI), (f_lo, FI), (mag_done, 2 * QB), (mask_done, 4 * QB),
                         (h_lo, 2 * QB), (y_lo, BI), (add1, 2 * QT), (add2, 2 * QT)):
                dve.sem_inc(q, n)
            for n in range(len(CONST)):
                st, _, hi, lo = cslot(n)
                dve.wait_ge(c_hi, n + 1)
                dve.tensor_tensor(lo, st, f(hi), ALU.subtract).then_inc(c_lo, 1)
            dve.memset(f(hh[:, :, 4 * FQ:HP]), 0.0).then_inc(pad_set, 1)
            dve.wait_ge(pad_set, 1)
            dve.memset(f(hh[BS:BS + 1, 0, :]), 1.0).then_inc(pad_set, 1)
            dve.memset(f(hh[BS:BS + 1, 1, :]), 0.0).then_inc(pad_set, 1)
            dve.memset(f(y[0:64, :, :, KCH - 1, :]), 0.0).then_inc(pad_set, 1)

            def fold(k):
                dve.wait_ge(x_loaded, 16 * (k + 1))
                for t in range(QT):
                    col = k * QT + t
                    dve.tensor_scalar(xs[:, t, :], xs[:, t, :], mean[:, bass.ds(col, 1)], rstd[:, bass.ds(col, 1)],
                                      ALU.subtract, ALU.mult).then_inc(norm_done, 1)
                dve.wait_ge(t_mm, after(k, TI, -1))
                for t in range(QT):
                    dve.wait_ge(norm_done, after(k, QT, t))
                    dve.tensor_tensor(ev[:, t, :], xs[:, t, 0:HALF], xs[:, t, HALF:N], ALU.add).then_inc(fold_done, 1)
                    dve.tensor_tensor(xs[:, t, HALF:N], xs[:, t, 0:HALF], xs[:, t, HALF:N], ALU.subtract).then_inc(fold_done, 1)

            def turned(k):
                for n in range(TI):
                    dve.wait_ge(t_hi, after(k, TI, n))
                    dve.tensor_tensor(xt[:, 1, n, :], ps_f[:, n % 2, 0:QC], f(xt[:, 0, n, :]), ALU.subtract).then_inc(t_lo, 1)

            def forward(k, j):
                for n in range(4):
                    i = 4 * j + n
                    dve.wait_ge(f_hi, after(k, FI, i))
                    dve.tensor_tensor(xf[:, j % 2, 1, n, :], ps_f[0:BS, i % 2, 0:FQ], f(xf[:, j % 2, 0, n, :]), ALU.subtract).then_inc(f_lo, 1)

            def first(k, j):
                for par in range(2):
                    u = 2 * j + par
                    cols = slice(2 * par * FQ, 2 * (par + 1) * FQ)
                    dve.wait_ge(sq_done, after(k, 2 * QB, u))
                    dve.tensor_tensor(sq[:, 0, :], sq[:, 0, :], sq[:, 1, :], ALU.add).then_inc(mask_done, 1)
                    dve.wait_ge(mask_done, after(k, 4 * QB, 2 * u))
                    dve.tensor_scalar(sq[:, 0, :], sq[:, 0, :], FEPS, T2, ALU.add, ALU.is_gt).then_inc(mask_done, 1)
                    dve.wait_ge(mask_done, after(k, 4 * QB, 2 * u + 1))
                    dve.tensor_tensor(hf[:, :, :], hf[:, :, :], sq[:, 0:1, :].broadcast_to([BS, 2, FQ]), ALU.mult).then_inc(mag_done, 1)
                    dve.wait_ge(h_hi, after(k, 2 * QB, u))
                    dve.tensor_tensor(hh[0:BS, 1, cols], hf[:, :, :].rearrange("p r n -> p (r n)"), f(hh[0:BS, 0, cols]), ALU.subtract).then_inc(h_lo, 1)

            def second(k, j):
                for n in range(6):
                    par, ch = divmod(n, 3)
                    i = 6 * j + n
                    src = ps_b[:, i % 2, 0:2 * BS].rearrange("p (r n) -> p r n", r=2)
                    cs = slice(j * BS, (j + 1) * BS)
                    dve.wait_ge(y_hi, after(k, BI, i))
                    if ch < 2:
                        dve.tensor_tensor(y[:, 1, par, ch:ch + 3:2, cs], src, f(y[:, 0, par, ch:ch + 3:2, cs]), ALU.subtract).then_inc(y_lo, 1)
                    else:
                        for r in range(2):
                            rows = slice(32 * r, 32 * r + REST)
                            op = dve.tensor_tensor(y[rows, 1, par, KCH - 1, cs], src[0:REST, r, :], f(y[rows, 0, par, KCH - 1, cs]), ALU.subtract)
                        op.then_inc(y_lo, 1)

            def inverse(k, t):
                dve.wait_ge(r_loaded[t], 16 * (k + 1))
                for q, h in enumerate((slice(0, HALF), slice(HALF, N))):
                    dve.wait_ge(i_mm, after(k, 2 * QT, 2 * t))
                    dve.tensor_tensor(xr[:, t, h], ps_i[:, 0, :], xr[:, t, h], ALU.add).then_inc(add1, 1)
                for q, h in enumerate((slice(0, HALF), slice(HALF, N))):
                    dve.wait_ge(i_mm, after(k, 2 * QT, 2 * t + 1))
                    dve.wait_ge(add1, after(k, 2 * QT, 2 * t + q))
                    dve.tensor_tensor(xr[:, t, h], xr[:, t, h], ps_i[:, 1, :], ALU.add if q == 0 else ALU.subtract).then_inc(add2, 1)

            fold(0)
            turned(0)

            def turn(k, last):
                forward(k, 0)
                forward(k, 1)
                first(k, 0)
                forward(k, 2)
                second(k, 0)
                first(k, 1)
                forward(k, 3)
                second(k, 1)
                first(k, 2)
                inverse(k, 0)
                second(k, 2)
                first(k, 3)
                if not last:
                    fold(k + 1)
                inverse(k, 1)
                second(k, 3)
                if not last:
                    turned(k + 1)
                inverse(k, 2)
            with dve.Fori(0, TURNS - 1) as k:
                turn(k, False)
            turn(TURNS - 1, True)


def build(nc, B, x, w_qkv, b_qkv, w_proj, b_proj, w1, b1, w2, b2, avg_in, ident_in, df_in, di_in, out):
    xv = x.rearrange("b c h w -> b c (h w)")
    qk_scr = nc.dram_tensor("qk_scr", [4, B * C, N], F32, kind="Internal").ap()
    v_scr = nc.dram_tensor("v_scr", [B * HEADS, P, NT, 2 * D], F32, kind="Internal").ap()
    o_scr = nc.dram_tensor("o_scr", [B * C, N], F32, kind="Internal").ap()
    x1_scr = nc.dram_tensor("x1_scr", [B * C, N], F32, kind="Internal").ap()
    w_scr = nc.dram_tensor("w_scr", [NBLK, BS + 1, WCOLS], F32, kind="Internal").ap()
    with ExitStack() as ctx:
        sb = lambda n, s, d=F32: ctx.enter_context(nc.sbuf_tensor(n, s, d))
        mean, rstd, ident = sb("mean", [P, B * CT]), sb("rstd", [P, B * CT]), sb("ident", [P, P])
        with nc.sbuf_tensor("avg", [P, len(AVG_PAIRS), P], F32) as avg:
            stats_stage(nc, B, xv, avg_in, ident_in, avg, ident, mean, rstd)
            qkv_stage(nc, B, xv, w_qkv, b_qkv, mean, rstd, qk_scr, v_scr)
            attend_stage(nc, B, ident, qk_scr, v_scr, o_scr)
            project_stage(nc, B, xv, w_proj, b_proj, b_qkv[2 * C:3 * C], w1, w2, b2, o_scr, x1_scr, w_scr, avg, mean, rstd)
        filter_stage(nc, B, ident, df_in, di_in, b1, x1_scr, w_scr, mean, rstd, out.rearrange("b c h w -> (b c) (h w)"))


def constants():
    avg = np.zeros([P, len(AVG_PAIRS), P], np.float32)
    for i, (a, b) in enumerate(AVG_PAIRS):
        ga, gb = (a * P + np.arange(P)) // GROUP, (b * P + np.arange(P)) // GROUP
        avg[:, i, :] = (ga[:, None] == gb[None, :]) / GROUP
    h, w = np.divmod(np.arange(HALF), W)
    df = np.zeros([P, 2, HN, 2 * FQ], np.float32)
    di = np.zeros([P, 2, KCH, HALF], np.float32)
    for par in range(2):
        kh, kw = np.divmod(np.arange(FQ), KW)
        kh = 2 * kh + par
        turn = (kh[:, None] * h[None, :] * (W // 1) + kw[:, None] * w[None, :] * H) % (H * W)
        ang = 2 * np.pi * turn / (H * W)
        s = 1 / math.sqrt(H * W)
        re, im = np.cos(ang) * s, -np.sin(ang) * s
        full = np.concatenate([re, im], 0).T
        df[:, par] = full.reshape(HN, P, 2 * FQ).transpose(1, 0, 2)
        c = np.where((kw == 0) | (kw == W // 2), 1.0, 2.0)[:, None]
        ire, iim = c * re, c * im
        for ch in range(2):
            di[:, par, ch] = ire[ch * P:(ch + 1) * P]
            di[:, par, 2 + ch] = iim[ch * P:(ch + 1) * P]
        di[0:REST, par, 4] = ire[2 * P:]
        di[32:32 + REST, par, 4] = iim[2 * P:]
    return {"avg": avg, "ident": np.eye(P, dtype=np.float32), "df": df, "di": di}


_INS = ["x", "L0_conv_w_qkv", "L0_conv_b_qkv", "L0_conv_w_proj", "L0_conv_b_proj", "L1_conv_w1", "L1_conv_b1", "L1_conv_w2", "L1_conv_b2"]


def kernel(**inputs):
    import concourse.bacc as bacc
    from concourse.bass_utils import run_bass_kernel_spmd

    nc = bacc.Bacc("TRN2", target_bir_lowering=False, num_devices=1)
    arrays, args = {}, []
    for name, a in [(n, np.ascontiguousarray(inputs[n])) for n in _INS] + list(constants().items()):
        arrays[f"in_{name}"] = a
        args.append(nc.dram_tensor(f"in_{name}", a.shape, mybir.dt.from_np(a.dtype), kind="ExternalInput").ap())
    x = arrays["in_x"]
    out = nc.dram_tensor("out_0", x.shape, F32, kind="ExternalOutput").ap()
    build(nc, x.shape[0], *args, out)
    r = run_bass_kernel_spmd(nc, [arrays], core_ids=[0])
    return r.results[0]["out_0"]
```

```python
import math
from contextlib import ExitStack

import numpy as np
import concourse.bass as bass
from concourse import mybir

F32 = mybir.dt.float32
F32R = mybir.dt.float32r
ACT = mybir.ActivationFunctionType
ALU = mybir.AluOpType
AX = mybir.AxisListType

P = 128
C = 768
CT = C // P
H = W = 32
N = H * W
NT = N // P
HALF = N // 2
HEADS = 12
D = C // HEADS
GROUP = C // 32
NBLK = 8
BS = C // NBLK
KW = W // 2 + 1
FQ = (H // 2) * KW
FEPS = 1e-8
THRESH = np.float32(0.01)


def largest_square():
    t = np.float32(THRESH * THRESH)
    while np.sqrt(np.nextafter(t, np.float32(1))) <= THRESH:
        t = np.nextafter(t, np.float32(1))
    while np.sqrt(t) > THRESH:
        t = np.nextafter(t, np.float32(0))
    return float(t)


def after(turn, per_turn, k):
    return turn * per_turn + (per_turn + k + 1)


def f(ap):
    return ap.bitcast(F32)


AVG_PAIRS = [(a, b) for b in range(3) for a in range(3)
             if (a * P) // GROUP <= ((b + 1) * P - 1) // GROUP and (b * P) // GROUP <= ((a + 1) * P - 1) // GROUP]


def group_average(pe, out, avg, col):
    last = None
    for b in range(3):
        ins = [i for i, p in enumerate(AVG_PAIRS) if p[1] == b]
        for n, i in enumerate(ins):
            last = pe.matmul(out(b), avg[:, i, :], col(AVG_PAIRS[i][0]), start=(n == 0), stop=(n == len(ins) - 1))
    return last


def finish_stats(nc, block_args, mv, cols, avg, mean, rstd, small, ps, sems, eps=1e-5):
    (dve_ready, pe_done, act_done) = sems
    dve, pe, act = block_args
    NCOL = cols
    v3 = lambda ap: ap.rearrange("p (n t) -> p t n", t=3)
    cm = small[:, 0, 0:NCOL]
    e = small[:, 1, 0:NCOL]

    def on_vector():
        dve.tensor_copy(cm, mv[:, :, 0]).then_inc(dve_ready, 1)
        dve.wait_ge(pe_done, 1)
        dve.tensor_copy(mean, ps[:, 0:NCOL]).then_inc(dve_ready, 1)
        dve.wait_ge(dve_ready, 2)
        dve.tensor_tensor(e, cm, mean, ALU.subtract).then_inc(dve_ready, 1)
        dve.wait_ge(dve_ready, 3)
        dve.tensor_tensor(e, e, e, ALU.mult).then_inc(dve_ready, 1)
        dve.wait_ge(dve_ready, 4)
        dve.tensor_tensor(e, e, mv[:, :, 1], ALU.add).then_inc(dve_ready, 1)
        dve.wait_ge(pe_done, 2)
        dve.tensor_scalar(e, ps[:, 64:64 + NCOL], eps, None, ALU.add).then_inc(dve_ready, 1)
        dve.wait_ge(act_done, 1)
        dve.reciprocal(rstd, cm).then_inc(dve_ready, 1)

    def on_tensor():
        for r, (src, o) in enumerate(((cm, 0), (e, 64))):
            pe.wait_ge(dve_ready, 1 if r == 0 else 5)
            dst = ps[:, o:o + NCOL]
            group_average(pe, lambda b: v3(dst)[:, b, :], avg, lambda a: v3(src)[:, a, :]).then_inc(pe_done, 1)

    def on_scalar():
        act.wait_ge(dve_ready, 6)
        act.activation(cm, e, ACT.Sqrt).then_inc(act_done, 1)

    return on_vector, on_tensor, on_scalar


def stats_stage(nc, B, x, avg_in, ident_in, avg, ident, mean, rstd):
    RING = 3
    with ExitStack() as ctx:
        sb = lambda n, s, d=F32: ctx.enter_context(nc.sbuf_tensor(n, s, d))
        sem = lambda n: ctx.enter_context(nc.semaphore(n))
        xt = sb("st_x", [P, RING, CT, N])
        bn = sb("st_bn", [P, 2, 6 * CT * 2])
        mv = sb("st_mv", [P, B * CT, 2])
        small = sb("st_small", [P, 2, B * CT])
        ps = ctx.enter_context(nc.psum_tensor("st_ps", [P, 512], F32))
        loaded = [sem(f"st_loaded{r}") for r in range(RING)]
        avg_loaded, read, bn_done, agg_done = sem("st_avg"), sem("st_read"), sem("st_bn_done"), sem("st_agg_done")
        sems = (sem("st_dve_ready"), sem("st_pe_done"), sem("st_act_done"))
        block = ctx.enter_context(nc.Block())

        @block.sync
        def _(sp):
            sp.dma_start(avg[:, :, :], avg_in).then_inc(avg_loaded, 16)
            sp.dma_start(ident[:, :], ident_in).then_inc(avg_loaded, 16)
            for b in range(B):
                if b >= RING:
                    sp.wait_ge(bn_done, 2 * CT * (b - RING + 1))
                sp.dma_start(xt[:, b % RING, :, :], x[b].rearrange("(t p) n -> p t n", p=P)).then_inc(loaded[b % RING], 16)

        @block.vector
        def _(dve):
            bnv = bn[:, :, :].rearrange("p r (t h s) -> p r t h s", t=CT, h=2)
            for b in range(B):
                dve.wait_ge(loaded[b % RING], 16 * (b // RING + 1))
                if b >= 2:
                    dve.wait_ge(agg_done, CT * (b - 1))
                for t in range(CT):
                    for h in range(2):
                        dve.bn_stats(bnv[:, b % 2, t, h, :], xt[:, b % RING, t, h * HALF:(h + 1) * HALF]).then_inc(bn_done, 1)
                dve.wait_ge(bn_done, 2 * CT * (b + 1))
                for t in range(CT):
                    dve.bn_aggr(mv[:, b * CT + t, :], bnv[:, b % 2, t, :, :].rearrange("p h s -> p (h s)")).then_inc(agg_done, 1)
            dve.wait_ge(agg_done, B * CT)
            finish_stats(nc, (dve, None, None), mv, B * CT, avg, mean[:, :], rstd[:, :], small, ps, sems)[0]()

        @block.tensor
        def _(pe):
            pe.wait_ge(avg_loaded, 32)
            finish_stats(nc, (None, pe, None), mv, B * CT, avg, mean[:, :], rstd[:, :], small, ps, sems)[1]()

        @block.scalar
        def _(act):
            finish_stats(nc, (None, None, act), mv, B * CT, avg, mean[:, :], rstd[:, :], small, ps, sems)[2]()


def qkv_stage(nc, B, x, w_qkv, b_qkv, mean, rstd, qk_scr, v_scr):
    RING = 4
    QK_TILES = 2 * CT
    VW = 384
    VH = VW // D
    PER_HALF = QK_TILES + (NT // 2) * (C // VW)
    ITEMS = 2 * PER_HALF
    PIECES = 2 * CT
    with ExitStack() as ctx:
        sb = lambda n, s, d=F32: ctx.enter_context(nc.sbuf_tensor(n, s, d))
        sem = lambda n: ctx.enter_context(nc.semaphore(n))
        wh = sb("q_wh", [P, CT, 3 * C], F32R)
        wl = sb("q_wl", [P, CT, 3 * C], F32R)
        xs = sb("q_x", [P, CT, N])
        xh = sb("q_xh", [P, 2, CT, HALF], F32R)
        xl = sb("q_xl", [P, 2, CT, HALF], F32R)
        ob = sb("q_out", [P, RING, 2 * HALF], F32R)
        bias = sb("q_bias", [P, QK_TILES])
        ps = ctx.enter_context(nc.psum_tensor("q_ps", [P, RING, 512], F32))
        wst = xs[:, :, :].rearrange("p t n -> p (t n)")[:, 0:2 * 3 * C].rearrange("p (s n) -> p s n", s=2)
        w_loaded = [sem("q_w_loaded0"), sem("q_w_loaded1")]
        bias_loaded, x_loaded = sem("q_bias_loaded"), sem("q_x_loaded")
        wh_done, wl_done = sem("q_wh_done"), sem("q_wl_done")
        norm_done, xh_done, xl_done = sem("q_norm_done"), sem("q_xh_done"), sem("q_xl_done")
        mm_done, hi_done, lo_done = sem("q_mm_done"), sem("q_hi_done"), sem("q_lo_done")
        stored = [sem(f"q_stored{r}") for r in range(RING)]
        block = ctx.enter_context(nc.Block())

        def item(s):
            h, r = divmod(s, PER_HALF)
            return (h, r, None) if r < QK_TILES else (h, (r - QK_TILES) // 2, (r - QK_TILES) % 2)

        PIECE_AT = {1 + k: (1, k) for k in range(CT)}
        NEXT_AT = {PER_HALF + 2 + k: (0, k) for k in range(CT)}

        @block.sync
        def _(sp):
            sp.dma_start(bias[:, :], b_qkv[0:2 * C].rearrange("(m p) -> p m", p=P), allow_slow_non_contiguous=True).then_inc(bias_loaded, 16)
            for t in range(CT):
                if t >= 2:
                    sp.wait_ge(wl_done, t - 1)
                sp.dma_start(wst[:, t % 2, :], w_qkv[t * P:(t + 1) * P, :]).then_inc(w_loaded[t % 2], 16)
            for r in range(RING):
                sp.sem_inc(stored[r], 16 * ITEMS // RING)

            def batch(b):
                for s in range(ITEMS):
                    h, m, vc = item(s)
                    r = s % RING
                    sp.wait_ge(lo_done, after(b, ITEMS, s))
                    if vc is None:
                        kind = 0 if m < CT else 2
                        row = b * C + (m % CT) * P
                        sp.dma_start(qk_scr[kind:kind + 2, bass.ds(row, P), h * HALF:(h + 1) * HALF].rearrange("k p n -> p k n"),
                                     f(ob[:, r, :]).rearrange("p (k n) -> p k n", k=2)).then_inc(stored[r], 16)
                    else:
                        sp.dma_start(v_scr[bass.ds(b * HEADS + vc * VH, VH), :, h * (NT // 2) + m, :].rearrange("g p e -> p g e"),
                                     f(ob[:, r, 0:2 * VW]).rearrange("p (g e) -> p g e", g=VH)).then_inc(stored[r], 16)
            with sp.Fori(0, B) as b:
                batch(b)
            for r in range(RING):
                sp.wait_ge(stored[r], 16 * ITEMS // RING * (B + 1))

        @block.gpsimd
        def _(pool):
            pool.wait_ge(wl_done, CT)
            with pool.Fori(0, B) as b:
                pool.wait_ge(xl_done, after(b, PIECES, -1))
                pool.dma_start(xs[:, :, :], x[b].rearrange("(t p) n -> p t n", p=P)).then_inc(x_loaded, 16)

        @block.scalar
        def _(act):
            act.sem_inc(hi_done, ITEMS)
            act.sem_inc(xh_done, PIECES)
            for t in range(CT):
                act.wait_ge(w_loaded[t % 2], 16 * (t // 2 + 1))
                act.activation(wh[:, t, :], wst[:, t % 2, :], ACT.Copy).then_inc(wh_done, 1)
            act.wait_ge(bias_loaded, 16)

            def piece(b, h, t):
                act.wait_ge(norm_done, after(b, PIECES, h * CT + t))
                if t == 0:
                    act.wait_ge(mm_done, after(b, ITEMS, h * PER_HALF + PER_HALF - 1 - ITEMS))
                act.activation(xh[:, h, t, :], xs[:, t, h * HALF:(h + 1) * HALF], ACT.Copy).then_inc(xh_done, 1)

            for t in range(CT):
                piece(0, 0, t)

            def batch(b, last):
                for s in range(ITEMS):
                    if s in PIECE_AT:
                        piece(b, *PIECE_AT[s])
                    if s in NEXT_AT and not last:
                        piece(b + 1, *NEXT_AT[s])
                    h, m, vc = item(s)
                    r = s % RING
                    act.wait_ge(mm_done, after(b, ITEMS, s))
                    act.wait_ge(stored[r], 16 * after(b, ITEMS // RING, s // RING - 1))
                    if vc is None:
                        act.activation(ob[:, r, 0:HALF], ps[:, r, :], ACT.Identity, bias=bias[:, m:m + 1]).then_inc(hi_done, 1)
                    else:
                        dst = ob[:, r, 0:2 * VW].rearrange("p (g k e) -> p g k e", g=VH, k=2)[:, :, 0, :]
                        act.activation(dst, ps[:, r, 0:VW].rearrange("p (g e) -> p g e", g=VH), ACT.Copy).then_inc(hi_done, 1)
            if B > 1:
                with act.Fori(0, B - 1) as b:
                    batch(b, False)
            batch(B - 1, True)

        @block.vector
        def _(dve):
            for q, n in ((lo_done, ITEMS), (xl_done, PIECES), (norm_done, PIECES)):
                dve.sem_inc(q, n)
            for t in range(CT):
                dve.wait_ge(wh_done, t + 1)
                dve.tensor_tensor(wl[:, t, :], wst[:, t % 2, :], f(wh[:, t, :]), ALU.subtract).then_inc(wl_done, 1)
            dve.wait_ge(bias_loaded, 16)

            def norm(b, h, t):
                if h == 0 and t == 0:
                    dve.wait_ge(x_loaded, 16 * (b + 1))
                sl = xs[:, t, h * HALF:(h + 1) * HALF]
                col = b * CT + t
                dve.tensor_scalar(sl, sl, mean[:, bass.ds(col, 1)], rstd[:, bass.ds(col, 1)], ALU.subtract, ALU.mult).then_inc(norm_done, 1)

            def rest(b, h, t):
                dve.wait_ge(xh_done, after(b, PIECES, h * CT + t))
                dve.tensor_tensor(xl[:, h, t, :], xs[:, t, h * HALF:(h + 1) * HALF], f(xh[:, h, t, :]), ALU.subtract).then_inc(xl_done, 1)

            for t in range(CT):
                norm(0, 0, t)
            for t in range(CT):
                rest(0, 0, t)

            def batch(b, last):
                for s in range(ITEMS):
                    for table, bb in ((PIECE_AT, b), (NEXT_AT, b + 1)):
                        if table is NEXT_AT and last:
                            continue
                        if s + 1 in table:
                            norm(bb, *table[s + 1])
                        if s in table:
                            rest(bb, *table[s])
                    h, m, vc = item(s)
                    r = s % RING
                    dve.wait_ge(hi_done, after(b, ITEMS, s))
                    if vc is None:
                        dve.scalar_tensor_tensor(ob[:, r, HALF:2 * HALF], ps[:, r, :], bias[:, m:m + 1], f(ob[:, r, 0:HALF]),
                                                 ALU.add, ALU.subtract).then_inc(lo_done, 1)
                    else:
                        o4 = ob[:, r, 0:2 * VW].rearrange("p (g k e) -> p g k e", g=VH, k=2)
                        dve.tensor_tensor(o4[:, :, 1, :], ps[:, r, 0:VW].rearrange("p (g e) -> p g e", g=VH), f(o4[:, :, 0, :]),
                                          ALU.subtract).then_inc(lo_done, 1)
            if B > 1:
                with dve.Fori(0, B - 1) as b:
                    batch(b, False)
            batch(B - 1, True)

        @block.tensor
        def _(pe):
            pe.sem_inc(mm_done, ITEMS)
            pe.wait_ge(wl_done, CT)
            with pe.Fori(0, B) as b:
                for s in range(ITEMS):
                    h, m, vc = item(s)
                    r = s % RING
                    if s % PER_HALF == 0:
                        pe.wait_ge(xl_done, after(b, PIECES, h * CT + CT - 1))
                    pe.wait_ge(lo_done, after(b, ITEMS, s - RING))
                    k = 0
                    for t in range(CT):
                        for a, o in ((xh, wh), (xh, wl), (xl, wh)):
                            if vc is None:
                                mm = pe.matmul(ps[:, r, :], o[:, t, m * P:(m + 1) * P], a[:, h, t, :],
                                               start=(k == 0), stop=(k == 3 * CT - 1))
                            else:
                                mm = pe.matmul(ps[:, r, 0:VW], a[:, h, t, m * P:(m + 1) * P],
                                               o[:, t, 2 * C + vc * VW:2 * C + (vc + 1) * VW], start=(k == 0), stop=(k == 3 * CT - 1))
                            k += 1
                    mm.then_inc(mm_done, 1)


def attend_stage(nc, B, ident, qk_scr, v_scr, o_scr, den_scr):
    HB = 3
    ST = HB * NT
    TURNS = B * HEADS // HB
    RS, RP = 2, 4
    TURN = 3
    LEAD_S, LEAD_M = 3, NT + 5
    with ExitStack() as ctx:
        sb = lambda n, s, d=F32: ctx.enter_context(nc.sbuf_tensor(n, s, d))
        sem = lambda n: ctx.enter_context(nc.semaphore(n))
        k1 = sb("a_k1", [P, HB, N], F32R)
        k2 = sb("a_k2", [D + 1, HB, N], F32R)
        q1 = sb("a_q1", [P, HB, N], F32R)
        q2 = sb("a_q2", [D + 1, HB, N], F32R)
        v = sb("a_v", [P, HB, NT, 4, D], F32R)
        prob = sb("a_prob", [P, RP, N])
        ph = sb("a_ph", [P, RP, N], F32R)
        pl = sb("a_pl", [P, RP, N], F32R)
        mx = sb("a_mx", [P, HB, NT])
        ob = sb("a_o", [P, HB, N])
        ps_s = ctx.enter_context(nc.psum_tensor("a_ps_s", [P, RS, N], F32))
        ps_m = ctx.enter_context(nc.psum_tensor("a_ps_m", [P, N], F32))
        ps_o = ctx.enter_context(nc.psum_tensor("a_ps_o", [P, N], F32))
        qk_loaded = [sem(f"a_qk_loaded{r}") for r in range(HB)]
        v_loaded = [sem(f"a_v_loaded{r}") for r in range(HB)]
        o_stored = [sem(f"a_o_stored{r}") for r in range(HB)]
        consts_set = sem("a_consts_set")
        max_mm, max_read, turned, shift_set = sem("a_max_mm"), sem("a_max_read"), sem("a_turned"), sem("a_shift_set")
        scores_done, exp_done, hi_done, lo_done = sem("a_scores_done"), sem("a_exp_done"), sem("a_hi_done"), sem("a_lo_done")
        pv_done, sums_out = sem("a_pv_done"), sem("a_sums_out")
        block = ctx.enter_context(nc.Block())
        halves = [slice(h * HALF, (h + 1) * HALF) for h in range(2)]

        @block.sync
        def _(sp):
            for r in range(HB):
                sp.sem_inc(o_stored[r], 32)
            sp.wait_ge(consts_set, 3)

            def load_qk(g, r):
                rows = bass.ds(g * D, D)
                for dst, kind in ((q1[0:D, r, :], 0), (k2[0:D, r, :], 2), (k1[0:D, r, :], 2), (k1[D:P, r, :], 3),
                                  (q1[D:P, r, :], 0), (q2[0:D, r, :], 1)):
                    sp.dma_start(f(dst), qk_scr[kind, rows, :]).then_inc(qk_loaded[r], 16)

            def load_v(g, r):
                sp.dma_start(f(v[:, r, :, 0::2, :]).rearrange("p c k e -> p (c k) e"), v_scr[g].rearrange("p c (k e) -> p (c k) e", k=2)).then_inc(v_loaded[r], 16)

            for r in range(HB):
                load_qk(r, r)
                load_v(r, r)

            def turn(i, last):
                for r in range(HB):
                    if not last:
                        sp.wait_ge(scores_done, after(i, ST, r * NT + NT - 1))
                        load_qk(i * HB + (HB + r), r)
                        sp.wait_ge(pv_done, after(i, 2 * ST, 2 * (r * NT + NT) - 1))
                        load_v(i * HB + (HB + r), r)
                    sp.wait_ge(sums_out, after(i, 2 * HB, 2 * r + 1))
                    sp.dma_start(o_scr[bass.ds((i * HB + r) * D, D), :], ob[0:D, r, :]).then_inc(o_stored[r], 16)
                    sp.dma_start(den_scr[bass.ds(i * HB + r, 1), :], ob[D:D + 1, r, :]).then_inc(o_stored[r], 16)
            with sp.Fori(0, TURNS - 1) as i:
                turn(i, False)
            turn(TURNS - 1, True)
            for r in range(HB):
                sp.wait_ge(o_stored[r], 32 * (TURNS + 1))

        @block.tensor
        def _(pe):
            for q, n in ((max_mm, ST), (turned, HB), (scores_done, ST), (pv_done, 2 * ST)):
                pe.sem_inc(q, n)

            def row_max(i, s):
                j, s = divmod(s, ST)
                i, r, c = i + j, s // NT, s % NT
                if c == 0:
                    pe.wait_ge(qk_loaded[r], 96 * (i + 1))
                    pe.wait_ge(shift_set, after(i, HB, r - 1))
                pe.wait_ge(max_read, after(i, ST, s - 1))
                for h in halves:
                    mm = pe.matmul(ps_m[:, h], q1[0:D, r, c * P:(c + 1) * P], k2[0:D, r, h], start=True, stop=True)
                mm.then_inc(max_mm, 1)

            def turn_max(i, r):
                j, r = divmod(r, HB)
                i = i + j
                pe.wait_ge(max_read, after(i, ST, r * NT + NT - 1))
                for c in range(NT):
                    mm = pe.transpose(ps_m[0:1, c * P:(c + 1) * P], mx[:, r, c:c + 1], ident[:, :])
                mm.then_inc(turned, 1)

            def scores(i, s):
                j, s = divmod(s, ST)
                i, r, c = i + j, s // NT, s % NT
                if c == 0:
                    pe.wait_ge(shift_set, after(i, HB, r))
                pe.wait_ge(exp_done, after(i, ST, s - RS))
                for h in halves:
                    pe.matmul(ps_s[:, s % RS, h], k1[:, r, c * P:(c + 1) * P], q1[:, r, h], start=True, stop=False)
                    mm = pe.matmul(ps_s[:, s % RS, h], k2[:, r, c * P:(c + 1) * P], q2[:, r, h], start=False, stop=True)
                mm.then_inc(scores_done, 1)

            def weighted(i, s):
                r, c, w = s // NT, s % NT, s % RP
                pe.wait_ge(hi_done, after(i, ST, s))
                pe.wait_ge(lo_done, after(i, ST, s))
                if c == 0:
                    pe.wait_ge(v_loaded[r], 16 * (i + 1))
                vo = v[:, r, c, 0:2, :].rearrange("p k e -> p (k e)")
                vz = v[:, r, c, 2:4, :].rearrange("p k e -> p (k e)")
                for n, h in enumerate(halves):
                    if c == 0:
                        pe.wait_ge(sums_out, after(i, 2 * HB, 2 * (r - 1) + n))
                    pe.matmul(ps_o[:, h], vo, ph[:, w, h], start=(c == 0), stop=False)
                    pe.matmul(ps_o[:, h], vo, pl[:, w, h], start=False, stop=False)
                    pe.matmul(ps_o[:, h], vz, ph[:, w, h], start=False, stop=(c == NT - 1)).then_inc(pv_done, 1)

            for s in range(NT):
                row_max(0, s)
            turn_max(0, 0)
            for s in range(TURN + 2):
                if s < LEAD_S:
                    scores(0, s)
                row_max(0, NT + s)

            def turn(i, last):
                for s in range(ST):
                    if not (last and s + LEAD_S >= ST):
                        scores(i, s + LEAD_S)
                    if s % NT == TURN + 1 and not (last and s + LEAD_M - 1 >= ST):
                        row_max(i, s + LEAD_M - 1)
                    weighted(i, s)
                    if s % NT == TURN:
                        if not (last and s // NT == HB - 1):
                            turn_max(i, s // NT + 1)
                    elif not (last and s + LEAD_M >= ST):
                        row_max(i, s + LEAD_M)
            with pe.Fori(0, TURNS - 1) as i:
                turn(i, False)
            turn(TURNS - 1, True)

        @block.scalar
        def _(act):
            for q, n in ((exp_done, ST), (hi_done, ST), (shift_set, HB)):
                act.sem_inc(q, n)

            def shift(i, r):
                j, r = divmod(r, HB)
                i = i + j
                act.wait_ge(turned, after(i, HB, r))
                act.wait_ge(qk_loaded[r], 96 * (i + 1))
                act.activation(q2[D:D + 1, r, :], ps_m[0:1, :], ACT.Copy, scale=-1.0).then_inc(shift_set, 1)

            def exps(i, s):
                j, s = divmod(s, ST)
                i = i + j
                act.wait_ge(scores_done, after(i, ST, s))
                act.wait_ge(lo_done, after(i, ST, s - RP))
                act.activation(prob[:, s % RP, :], ps_s[:, s % RS, :], ACT.Exp, scale=1 / math.sqrt(D)).then_inc(exp_done, 1)

            def high(i, s):
                j, s = divmod(s, ST)
                i = i + j
                act.wait_ge(exp_done, after(i, ST, s))
                act.wait_ge(pv_done, after(i, 2 * ST, 2 * (s - RP) + 1))
                act.activation(ph[:, s % RP, :], prob[:, s % RP, :], ACT.Copy).then_inc(hi_done, 1)

            shift(0, 0)
            for s in range(2):
                exps(0, s)
                high(0, s)

            def turn(i, last):
                for s in range(ST):
                    if not (last and s + 2 >= ST):
                        exps(i, s + 2)
                    if s % NT == TURN + 1 and not (last and s // NT == HB - 1):
                        shift(i, s // NT + 1)
                    if not (last and s + 2 >= ST):
                        high(i, s + 2)
            with act.Fori(0, TURNS - 1) as i:
                turn(i, False)
            turn(TURNS - 1, True)

        @block.vector
        def _(dve):
            for q, n in ((max_read, ST), (lo_done, ST), (sums_out, 2 * HB)):
                dve.sem_inc(q, n)
            dve.memset(f(k2[D:D + 1, :, :]), 1.0).then_inc(consts_set, 1)
            dve.memset(f(v[:, :, :, 1, :]), 1.0).then_inc(consts_set, 1)
            dve.memset(f(v[:, :, :, 3, :]), 0.0).then_inc(consts_set, 1)

            def take_max(i, s):
                j, s = divmod(s, ST)
                i, r, c = i + j, s // NT, s % NT
                dve.wait_ge(max_mm, after(i, ST, s))
                if c == 0:
                    dve.wait_ge(turned, after(i, HB, r - HB))
                dve.reduce_max(mx[:, r, c:c + 1], ps_m[:, :], axis=AX.X).then_inc(max_read, 1)

            def low(i, s):
                j, s = divmod(s, ST)
                i, w = i + j, s % RP
                dve.wait_ge(hi_done, after(i, ST, s))
                dve.wait_ge(pv_done, after(i, 2 * ST, 2 * (s - RP) + 1))
                dve.tensor_tensor(pl[:, w, :], prob[:, w, :], f(ph[:, w, :]), ALU.subtract).then_inc(lo_done, 1)

            def take_sums(i, r):
                for n, h in enumerate(halves):
                    dve.wait_ge(pv_done, after(i, 2 * ST, 2 * (r * NT + NT - 1) + n))
                    if n == 0:
                        dve.wait_ge(o_stored[r], 32 * (i + 1))
                    dve.tensor_copy(ob[:, r, h], ps_o[:, h]).then_inc(sums_out, 1)

            for s in range(LEAD_M - 1):
                take_max(0, s)
            low(0, 0)
            low(0, 1)

            def turn(i, last):
                for s in range(ST):
                    if not (last and s + LEAD_M - 1 >= ST):
                        take_max(i, s + LEAD_M - 1)
                    if s % NT == NT - 1:
                        take_sums(i, s // NT)
                    if not (last and s + 2 >= ST):
                        low(i, s + 2)
            with dve.Fori(0, TURNS - 1) as i:
                turn(i, False)
            turn(TURNS - 1, True)


W1C, W2C = 3 * BS, 2 * 2 * BS
WCOLS = 2 * (W1C + W2C)


def project_stage(nc, B, x, w_proj, b_proj, b_v, w1, w2, b2, o_scr, den_scr, rec_scr, x1_scr, w_scr, avg, mean, rstd):
    RING = 4
    ITEMS = 2 * CT
    PIECES = 2 * CT
    with ExitStack() as ctx:
        sb = lambda n, s, d=F32: ctx.enter_context(nc.sbuf_tensor(n, s, d))
        sem = lambda n: ctx.enter_context(nc.semaphore(n))
        wh, wl = sb("p_wh", [P, CT, C], F32R), sb("p_wl", [P, CT, C], F32R)
        ws = sb("p_ws", [P, CT, C])
        bp, bv = sb("p_bp", [P, CT]), sb("p_bv", [P, CT])
        of = sb("p_o", [P, 2, CT, HALF])
        rb = sb("p_rb", [P, 2, CT, HALF])
        rec = sb("p_rec", [P, B * HEADS * NT])
        oh, ol = sb("p_oh", [P, 2, CT, HALF], F32R), sb("p_ol", [P, 2, CT, HALF], F32R)
        xt = sb("p_x", [P, RING, HALF])
        fw = sb("p_fw", [BS + 1, WCOLS], F32R)
        fs = sb("p_fs", [BS + 1, 2, BS, 2])
        fa = sb("p_fa", [BS + 1, W1C + W2C])
        bn = sb("p_bn", [P, 12 * CT])
        bn_all = sb("p_bn_all", [P, B * 12 * CT])
        mv = sb("p_mv", [P, B * CT, 2])
        small = sb("p_small", [P, 2, B * CT])
        ps = ctx.enter_context(nc.psum_tensor("p_ps", [P, RING, 512], F32))
        ps_g = ctx.enter_context(nc.psum_tensor("p_ps_g", [P, 512], F32))
        w_loaded, wh_done, wl_done = sem("p_w_loaded"), sem("p_wh_done"), sem("p_wl_done")
        fs_loaded, fa_done, fh_done, fl_done, fw_stored = sem("p_fs_loaded"), sem("p_fa_done"), sem("p_fh_done"), sem("p_fl_done"), sem("p_fw_stored")
        o_loaded = [sem("p_o_loaded0"), sem("p_o_loaded1")]
        x_loaded = [sem(f"p_x_loaded{r}") for r in range(RING)]
        stored = [sem(f"p_stored{r}") for r in range(RING)]
        oh_done, ol_done, mm_done, add_done = sem("p_oh_done"), sem("p_ol_done"), sem("p_mm_done"), sem("p_add_done")
        den_loaded, rec_done, rec_stored, on_done = sem("p_den_loaded"), sem("p_rec_done"), sem("p_rec_stored"), sem("p_on_done")
        bn_done, kept, agg_done = sem("p_bn_done"), sem("p_kept"), sem("p_agg_done")
        sems = (sem("p_dve_ready"), sem("p_pe_done"), sem("p_act_done"))
        block = ctx.enter_context(nc.Block())
        half = lambda h: slice(h * HALF, (h + 1) * HALF)

        @block.sync
        def _(sp):
            sp.dma_start(rec[:, :], den_scr.rearrange("g n -> (g n)").rearrange("(p c) -> p c", p=P)).then_inc(den_loaded, 16)
            sp.dma_start(ws[:, :, :], w_proj.rearrange("(t p) n -> p t n", p=P)).then_inc(w_loaded, 16)
            sp.dma_start(bp[:, :], b_proj.rearrange("(m p) -> p m", p=P), allow_slow_non_contiguous=True).then_inc(w_loaded, 16)
            sp.dma_start(bv[:, :], b_v.rearrange("(m p) -> p m", p=P), allow_slow_non_contiguous=True).then_inc(w_loaded, 16)
            for r in range(RING):
                sp.sem_inc(stored[r], 16 * ITEMS // RING)

            def load_o(b, h):
                sp.wait_ge(ol_done, after(b, PIECES, h * CT + CT - 1 - PIECES))
                sp.dma_start(of[:, h, :, :], o_scr[bass.ds(b * C, C), half(h)].rearrange("(t p) n -> p t n", p=P)).then_inc(o_loaded[h], 16)
                for j in range(2):
                    src = rec_scr.rearrange("(g j) n -> j g n", j=2)[j:j + 1, bass.ds(b * CT, CT), half(h)]
                    sp.dma_start(rb[j * D:(j + 1) * D, h, :, :], src.broadcast_to([D, CT, HALF])).then_inc(o_loaded[h], 16)

            def batch(b, last):
                for s in range(ITEMS):
                    h, m, r = s // CT, s % CT, s % RING
                    if s in (0, 3) and not last:
                        load_o(b + 1, s // 3)
                    sp.wait_ge(add_done, after(b, ITEMS, s))
                    sp.dma_start(x1_scr[bass.ds(b * C + m * P, P), half(h)], xt[:, r, :]).then_inc(stored[r], 16)

            sp.wait_ge(rec_done, 1)
            sp.dma_start(rec_scr.rearrange("g n -> (g n)").rearrange("(p c) -> p c", p=P), rec[:, :]).then_inc(rec_stored, 16)
            sp.wait_ge(rec_stored, 16)
            load_o(0, 0)
            load_o(0, 1)
            if B > 1:
                with sp.Fori(0, B - 1) as b:
                    batch(b, False)
            batch(B - 1, True)
            for r in range(RING):
                sp.wait_ge(stored[r], 16 * ITEMS // RING * (B + 1))

        @block.gpsimd
        def _(pool):
            def weights(blk):
                pool.wait_ge(fl_done, blk + 1)
                pool.dma_start(w_scr[blk], f(fw[:, :])).then_inc(fw_stored, 16)
                if blk + 1 < NBLK:
                    load_weights(blk + 1)

            def load_weights(blk):
                if blk:
                    pool.wait_ge(fa_done, 5 * blk)
                pool.dma_start(fs[0:BS, 0, :, :], w1[blk]).then_inc(fs_loaded, 16)
                pool.dma_start(fs[0:BS, 1, :, :], w2[blk]).then_inc(fs_loaded, 16)
                pool.dma_start(fs[BS:BS + 1, 1, :, :], b2[blk:blk + 1]).then_inc(fs_loaded, 16)

            def batch(b, last):
                for s in range(ITEMS):
                    h, m, r = s // CT, s % CT, s % RING
                    pool.wait_ge(stored[r], 16 * after(b, ITEMS // RING, s // RING - 1))
                    pool.wait_ge(bn_done, after(b, ITEMS, s - RING))
                    pool.dma_start(xt[:, r, :], x[b, m * P:(m + 1) * P, half(h)]).then_inc(x_loaded[r], 16)
                    if last and s >= RING:
                        weights(s - RING)
            load_weights(0)
            if B > 1:
                with pool.Fori(0, B - 1) as b:
                    batch(b, False)
            batch(B - 1, True)
            pool.wait_ge(fw_stored, 16 * NBLK)

        @block.scalar
        def _(act):
            act.sem_inc(oh_done, PIECES)
            act.wait_ge(w_loaded, 48)
            act.activation(wh[:, :, :], ws[:, :, :], ACT.Copy).then_inc(wh_done, 1)
            with act.Fori(0, B) as b:
                for h in range(2):
                    act.wait_ge(mm_done, after(b, ITEMS, h * CT + CT - 1 - ITEMS))
                    for t in range(CT):
                        act.wait_ge(on_done, after(b, PIECES, h * CT + t))
                        act.activation(oh[:, h, t, :], of[:, h, t, :], ACT.Identity, bias=bv[:, t:t + 1]).then_inc(oh_done, 1)
            for blk in range(NBLK):
                act.wait_ge(fa_done, 5 * (blk + 1))
                if blk:
                    act.wait_ge(fw_stored, 16 * blk)
                act.activation(fw[:, 0:WCOLS // 2], fa[:, :], ACT.Copy).then_inc(fh_done, 1)
            finish_stats(nc, (None, None, act), mv, B * CT, avg, mean[:, :], rstd[:, :], small, ps_g, sems)[2]()

        @block.vector
        def _(dve):
            for q, n in ((ol_done, PIECES), (on_done, PIECES), (add_done, ITEMS), (bn_done, ITEMS)):
                dve.sem_inc(q, n)
            dve.wait_ge(den_loaded, 16)
            dve.reciprocal(rec[:, :], rec[:, :]).then_inc(rec_done, 1)
            dve.wait_ge(wh_done, 1)
            dve.tensor_tensor(wl[:, :, :], ws[:, :, :], f(wh[:, :, :]), ALU.subtract).then_inc(wl_done, 1)
            dve.memset(fa[BS:BS + 1, :], 0.0).then_inc(wl_done, 1)
            dve.wait_ge(wl_done, 2)

            def arrange(blk):
                dve.wait_ge(fs_loaded, 48 * (blk + 1))
                if blk:
                    dve.wait_ge(fl_done, blk)
                a1 = fa[0:BS, 0:W1C].rearrange("p (k n) -> p k n", k=3)
                a2 = fa[0:BS, W1C:].rearrange("p (k n) -> p k n", k=4)
                s1, s2 = fs[0:BS, 0, :, :].rearrange("p n k -> p k n"), fs[0:BS, 1, :, :].rearrange("p n k -> p k n")
                dve.tensor_copy(a1[:, 0:2, :], s1).then_inc(fa_done, 1)
                dve.tensor_scalar(a1[:, 2, :], s1[:, 1, :], -1.0, None, ALU.mult).then_inc(fa_done, 1)
                dve.tensor_copy(a2[:, 0:2, :], s2).then_inc(fa_done, 1)
                dve.tensor_scalar(a2[:, 2, :], s2[:, 1, :], -1.0, None, ALU.mult)
                dve.tensor_copy(a2[:, 3, :], s2[:, 0, :]).then_inc(fa_done, 1)
                dve.tensor_copy(fa[BS:BS + 1, W1C:W1C + 2 * BS].rearrange("p (k n) -> p k n", k=2),
                                fs[BS:BS + 1, 1, :, :].rearrange("p n k -> p k n")).then_inc(fa_done, 1)
                dve.wait_ge(fh_done, blk + 1)
                dve.tensor_tensor(fw[:, WCOLS // 2:], fa[:, :], f(fw[:, 0:WCOLS // 2]), ALU.subtract).then_inc(fl_done, 1)
            bnv = bn[:, :].rearrange("p (t h s) -> p t h s", t=CT, h=2)

            def divide(b, h):
                dve.wait_ge(o_loaded[h], 48 * (b + 1))
                for t in range(CT):
                    dve.tensor_tensor(of[:, h, t, :], of[:, h, t, :], rb[:, h, t, :], ALU.mult).then_inc(on_done, 1)

            def split(b, h):
                for t in range(CT):
                    dve.wait_ge(oh_done, after(b, PIECES, h * CT + t))
                    dve.scalar_tensor_tensor(ol[:, h, t, :], of[:, h, t, :], bv[:, t:t + 1], f(oh[:, h, t, :]),
                                             ALU.add, ALU.subtract).then_inc(ol_done, 1)
            divide(0, 0)
            split(0, 0)

            def batch(b, last):
                for s in range(ITEMS):
                    h, m, r = s // CT, s % CT, s % RING
                    if s == 1:
                        divide(b, 1)
                    if s == 2:
                        split(b, 1)
                    if s == CT and not last:
                        divide(b + 1, 0)
                    if s == CT + 1 and not last:
                        split(b + 1, 0)
                    if last and 2 <= s < 2 + NBLK:
                        arrange(s - 2)
                    dve.wait_ge(mm_done, after(b, ITEMS, s))
                    dve.wait_ge(x_loaded[r], 16 * (b * (ITEMS // RING) + s // RING + 1))
                    dve.scalar_tensor_tensor(xt[:, r, :], ps[:, r, :], bp[:, m:m + 1], xt[:, r, :], ALU.add, ALU.add).then_inc(add_done, 1)
                    dve.wait_ge(add_done, after(b, ITEMS, s))
                    dve.bn_stats(bnv[:, m, h, :], xt[:, r, :]).then_inc(bn_done, 1)
                dve.wait_ge(bn_done, after(b, ITEMS, ITEMS - 1))
                dve.tensor_scalar(bn_all[:, bass.ds(b * 12 * CT, 12 * CT)], bn[:, :], 1.0, None, ALU.mult).then_inc(kept, 1)
            if B > 1:
                with dve.Fori(0, B - 1) as b:
                    batch(b, False)
            batch(B - 1, True)
            dve.wait_ge(kept, B)
            for t in range(B * CT):
                dve.bn_aggr(mv[:, t, :], bn_all[:, 12 * t:12 * t + 12]).then_inc(agg_done, 1)
            dve.wait_ge(agg_done, B * CT)
            finish_stats(nc, (dve, None, None), mv, B * CT, avg, mean[:, :], rstd[:, :], small, ps_g, sems)[0]()

        @block.tensor
        def _(pe):
            pe.sem_inc(mm_done, ITEMS)
            pe.wait_ge(wl_done, 1)
            with pe.Fori(0, B) as b:
                for s in range(ITEMS):
                    h, m, r = s // CT, s % CT, s % RING
                    if m == 0:
                        pe.wait_ge(ol_done, after(b, PIECES, h * CT + CT - 1))
                    pe.wait_ge(add_done, after(b, ITEMS, s - RING))
                    k = 0
                    for t in range(CT):
                        for a, o in ((oh, wh), (oh, wl), (ol, wh)):
                            mm = pe.matmul(ps[:, r, :], o[:, t, m * P:(m + 1) * P], a[:, h, t, :], start=(k == 0), stop=(k == 3 * CT - 1))
                            k += 1
                    mm.then_inc(mm_done, 1)
            finish_stats(nc, (None, pe, None), mv, B * CT, avg, mean[:, :], rstd[:, :], small, ps_g, sems)[1]()


HN = HALF // P
KCH = 9
REST = FQ - 2 * P


def filter_stage(nc, B, ident, df_in, di_in, b1, x1_scr, w_scr, mean, rstd, out):
    QT = 3
    QB = NBLK // 2
    QC = QT * P
    TURNS = 2 * B
    T2 = largest_square()
    HP = 4 * FQ + P - REST
    with ExitStack() as ctx:
        sb = lambda n, s, d=F32: ctx.enter_context(nc.sbuf_tensor(n, s, d))
        sem = lambda n: ctx.enter_context(nc.semaphore(n))
        df = sb("f_df", [P, 2, 2, HN, 2 * FQ], F32R)
        di = sb("f_di", [P, 2, KCH, HALF], F32R)
        wt = sb("f_w", [BS + 1, 2, WCOLS], F32R)
        bt = sb("f_b1", [BS, 2, 2])
        xs = sb("f_x", [P, QT, N])
        ev = sb("f_ev", [P, QT, HALF])
        xt = sb("f_xt", [P, 2, NT, QC], F32R)
        xf = sb("f_xf", [BS, 2, 2, 4, FQ], F32R)
        hf = sb("f_hf", [BS, 2, 2, FQ])
        sq = sb("f_sq", [BS, 2, 2, FQ])
        hh = sb("f_hh", [BS + 1, 2, HP], F32R)
        y = sb("f_y", [P, 2, KCH, QC], F32R)
        xr = sb("f_xr", [P, QT, N])
        ps_f = ctx.enter_context(nc.psum_tensor("f_ps_f", [P, 2, 512], F32))
        ps_a = ctx.enter_context(nc.psum_tensor("f_ps_a", [P, 2, 512], F32))
        ps_b = ctx.enter_context(nc.psum_tensor("f_ps_b", [P, 2, 512], F32))
        ps_i = ctx.enter_context(nc.psum_tensor("f_ps_i", [P, 2, 512], F32))
        c_loaded = [sem(f"f_c_loaded{r}") for r in range(5)]
        c_hi, c_lo, pad_set = sem("f_c_hi"), sem("f_c_lo"), sem("f_pad_set")
        w1_loaded = [sem("f_w1_loaded0"), sem("f_w1_loaded1")]
        w2_loaded = [sem("f_w2_loaded0"), sem("f_w2_loaded1")]
        x_loaded = sem("f_x_loaded")
        r_loaded = [sem(f"f_r_loaded{t}") for t in range(QT)]
        stored = [sem(f"f_stored{t}") for t in range(QT)]
        norm_done, fold_done = sem("f_norm_done"), sem("f_fold_done")
        t_mm, t_hi, t_lo = sem("f_t_mm"), sem("f_t_hi"), sem("f_t_lo")
        f_mm, f_hi, f_lo = sem("f_f_mm"), sem("f_f_hi"), sem("f_f_lo")
        a_mm, a_out, sq_done, mag_done, mask_done, h_hi, h_lo = (sem("f_a_mm"), sem("f_a_out"), sem("f_sq_done"), sem("f_mag_done"), sem("f_mask_done"),
                                                                 sem("f_h_hi"), sem("f_h_lo"))
        b_mm, y_hi, y_lo = sem("f_b_mm"), sem("f_y_hi"), sem("f_y_lo")
        i_mm, add1, add2 = sem("f_i_mm"), sem("f_add1"), sem("f_add2")
        block = ctx.enter_context(nc.Block())
        FI = 4 * QB
        TI = NT
        BI = 2 * 3 * QB
        RI = FI + TI
        CS = 5
        CONST = ([(df_in[:, p, t, :], df, (p, t)) for p in range(2) for t in range(HN)] + [(di_in[:, c, :], di, (c,)) for c in range(KCH)])

        def cslot(n):
            src, dst, at = CONST[n]
            width = src.shape[-1]
            stage = xr[:, :, :].rearrange("p t n -> p (t n)")[:, (n % CS) * 600:(n % CS) * 600 + width]
            return stage, src, dst[(slice(None), 0) + at], dst[(slice(None), 1) + at]

        ORDER = [(w[0], int(w[1]), int(w[3])) for w in """
            F0.0 F0.1 F0.2 F0.3 F1.0 A0.0 F1.1 A0.1 M0.0 F1.2 H0.0 A0.2 F1.3 A0.3 M0.1
            F2.0 H0.1 A1.0 N0.0 F2.1 A1.1 M1.0 B0.0 F2.2 B0.1 A1.2 B0.2 H1.0 F2.3 B0.3 A1.3 M1.1 B0.4 B0.5 N0.1
            F3.0 H1.1 A2.0 N0.2 F3.1 A2.1 M2.0 B1.0 F3.2 B1.1 A2.2 B1.2 H2.0 F3.3 B1.3 A2.3 M2.1 B1.4 B1.5
            A3.0 T0.0 H2.1 A3.1 M3.0 I0.0 B2.0 T0.1 B2.1 E0.0 A3.2 B2.2 H3.0 T0.2 B2.3 A3.3 M3.1 B2.4 B2.5
            I0.1 H3.1 B3.0 T0.3 B3.1 E0.1 B3.2 I1.0 B3.3 T0.4 B3.4 E1.0 B3.5 T0.5 I1.1 E1.1 T0.6 I2.0 E2.0 T0.7 I2.1 E2.1
            """.split()]

        @block.sync
        def _(sp):
            sp.dma_start(xs[:, :, :], x1_scr[0:QC, :].rearrange("(t p) n -> p t n", p=P)).then_inc(x_loaded, 16)
            for n in range(len(CONST)):
                if n >= CS:
                    sp.wait_ge(c_lo, n - CS + 1)
                st, src, _, _ = cslot(n)
                sp.dma_start(st, src).then_inc(c_loaded[n % CS], 16)
            for t in range(QT):
                sp.sem_inc(stored[t], 16)
            def load_x(k):
                sp.dma_start(xs[:, :, :], x1_scr[bass.ds(k * QC, QC), :].rearrange("(t p) n -> p t n", p=P)).then_inc(x_loaded, 16)

            sp.wait_ge(c_lo, len(CONST))

            def load_w1(k, par, j):
                sp.wait_ge(a_out, after(k, FI, 4 * (j - 2) + 3))
                blk = par * QB + j
                dst = f(wt[0:BS, j % 2, :]).rearrange("p (a n) -> p a n", a=2)[:, :, 0:W1C]
                src = w_scr[bass.ds(blk, 1), 0:BS, :].rearrange("b p (a n) -> p (b a) n", a=2)[:, :, 0:W1C]
                sp.dma_start(dst, src).then_inc(w1_loaded[j % 2], 16)
                sp.dma_start(bt[:, j % 2, :], b1[bass.ds(blk, 1), :, :].rearrange("a p n -> p (a n)")).then_inc(w1_loaded[j % 2], 16)

            def load_w2(k, par, j):
                sp.wait_ge(b_mm, after(k, BI, 6 * (j - 2) + 5))
                dst = f(wt[:, j % 2, :]).rearrange("p (a n) -> p a n", a=2)[:, :, W1C:W1C + W2C]
                src = w_scr[bass.ds(par * QB + j, 1), :, :].rearrange("b p (a n) -> p (b a) n", a=2)[:, :, W1C:W1C + W2C]
                sp.dma_start(dst, src).then_inc(w2_loaded[j % 2], 16)

            def turn(k, par, last):
                for j in range(2):
                    load_w1(k, par, j)
                for j in range(2):
                    load_w2(k, par, j)
                if not last:
                    sp.wait_ge(fold_done, after(k, 2 * QT, 2 * QT - 1))
                    sp.wait_ge(t_mm, after(k, TI, TI - 1))
                    load_x(k + 1)
                load_w1(k, par, 2)
                for t in range(QT):
                    sp.wait_ge(stored[t], 16 * (k + 1))
                    sp.dma_start(xr[:, t, :], x1_scr[bass.ds(k * QC + t * P, P), :]).then_inc(r_loaded[t], 16)
                load_w1(k, par, 3)
                load_w2(k, par, 2)
                load_w2(k, par, 3)
                for t in range(QT):
                    sp.wait_ge(add2, after(k, 2 * QT, 2 * t + 1))
                    sp.dma_start(out[bass.ds(k * QC + t * P, P), :], xr[:, t, :]).then_inc(stored[t], 16)
            with sp.Fori(0, TURNS - 1) as k:
                turn(k, k % 2, False)
            turn(TURNS - 1, 1, True)
            for t in range(QT):
                sp.wait_ge(stored[t], 16 * (TURNS + 1))

        @block.tensor
        def _(pe):
            for q, n in ((t_mm, TI), (f_mm, FI), (a_mm, 4 * QB), (b_mm, BI), (i_mm, 2 * QT)):
                pe.sem_inc(q, n)
            pe.wait_ge(c_lo, len(CONST))
            pe.wait_ge(pad_set, 4)

            def turned(k, ts):
                for n in ts:
                    par, t = divmod(n, HN)
                    src = ev if par == 0 else xs
                    if n == 0:
                        pe.wait_ge(fold_done, after(k, 2 * QT, 2 * QT - 1))
                    if n >= 2:
                        pe.wait_ge(t_lo, after(k, TI, n - 2))
                    else:
                        pe.wait_ge(f_lo, after(k, FI, n - 2))
                    for q in range(QT):
                        lo = (0 if par == 0 else HALF) + t * P
                        mm = pe.transpose(ps_f[:, n % 2, q * P:(q + 1) * P], src[:, q, lo:lo + P], ident[:, :])
                    mm.then_inc(t_mm, 1)

            def forward(k, j, ns):
                for n in ns:
                    par, ri = divmod(n, 2)
                    i = 4 * j + n
                    if i == 0:
                        pe.wait_ge(t_lo, after(k, TI, TI - 1))
                    if i >= 2:
                        pe.wait_ge(f_lo, after(k, FI, i - 2))
                    q = 0
                    for t in range(HN):
                        for a, c in ((0, 0), (0, 1), (1, 0)):
                            mm = pe.matmul(ps_f[0:BS, i % 2, 0:FQ], xt[:, a, par * HN + t, j * BS:(j + 1) * BS],
                                           df[:, c, par, t, ri * FQ:(ri + 1) * FQ], start=(q == 0), stop=(q == 3 * HN - 1))
                            q += 1
                    mm.then_inc(f_mm, 1)

            def first(k, j, ns):
                w = wt[0:BS, j % 2, :].rearrange("p (a n) -> p a n", a=2)
                for n in ns:
                    if n == 0:
                        pe.wait_ge(w1_loaded[j % 2], 64 * k + 32 * (j // 2 + 1))
                    par, ri = divmod(n, 2)
                    i = 4 * j + n
                    pe.wait_ge(f_lo, after(k, FI, 4 * j + 2 * par + 1))
                    pe.wait_ge(a_out, after(k, FI, i - 2))
                    q = 0
                    for s, col in ((0, 0 if ri == 0 else 1), (1, 2 if ri == 0 else 0)):
                        for a, c in ((0, 0), (0, 1), (1, 0)):
                            mm = pe.matmul(ps_a[0:BS, i % 2, 0:FQ], w[:, c, col * BS:(col + 1) * BS],
                                           xf[:, j % 2, a, 2 * par + s, :], start=(q == 0), stop=(q == 5))
                            q += 1
                    mm.then_inc(a_mm, 1)

            def second(k, j, ns):
                w = wt[:, j % 2, :].rearrange("p (a n) -> p a n", a=2)
                for n in ns:
                    if n == 0:
                        pe.wait_ge(w2_loaded[j % 2], 32 * k + 16 * (j // 2 + 1))
                        pe.wait_ge(h_lo, after(k, 2 * QB, 2 * j + 1))
                    par, ch = divmod(n, 3)
                    i = 6 * j + n
                    pe.wait_ge(y_lo, after(k, BI, i - 2))
                    q = 0
                    for s in range(2):
                        rows = BS + 1 if s == 0 else BS
                        col = (2 * par + s) * FQ + ch * P
                        for a, c in ((0, 0), (0, 1), (1, 0)):
                            mm = pe.matmul(ps_b[:, i % 2, 0:2 * BS], hh[0:rows, a, col:col + P],
                                           w[0:rows, c, W1C + s * 2 * BS:W1C + (s + 1) * 2 * BS], start=(q == 0), stop=(q == 5))
                            q += 1
                    mm.then_inc(b_mm, 1)

            def inverse(k, t, par):
                if par == 0:
                    pe.wait_ge(y_lo, after(k, BI, 6 * min(QB - 1, ((t + 1) * P - 1) // BS) + 5))
                pe.wait_ge((add1, add2)[par], after(k, 2 * QT, 2 * t - 1))
                tiles = [(4 * par + c, slice(0, P)) for c in range(4)] + [(KCH - 1, slice(64 * par, 64 * par + 64))]
                q = 0
                for c, rows in tiles:
                    for a, e in ((0, 0), (0, 1), (1, 0)):
                        mm = pe.matmul(ps_i[:, par, :], y[rows, a, c, t * P:(t + 1) * P], di[rows, e, c, :],
                                       start=(q == 0), stop=(q == 3 * len(tiles) - 1))
                        q += 1
                mm.then_inc(i_mm, 1)

            turned(0, range(TI))

            def turn(k, last):
                for what, j, n in ORDER:
                    if what == "F":
                        forward(k, j, (n,))
                    if what == "A":
                        first(k, j, (n,))
                    if what == "B":
                        second(k, j, (n,))
                    if what == "I":
                        inverse(k, j, n)
                    if what == "T" and not last:
                        turned(k + 1, (n,))
            with pe.Fori(0, TURNS - 1) as k:
                turn(k, False)
            turn(TURNS - 1, True)

        @block.scalar
        def _(act):
            for q, n in ((t_hi, TI), (f_hi, FI), (a_out, FI), (sq_done, 2 * QB), (h_hi, 2 * QB), (y_hi, BI)):
                act.sem_inc(q, n)
            for n in range(len(CONST)):
                st, _, hi, _ = cslot(n)
                act.wait_ge(c_loaded[n % CS], 16 * (n // CS + 1))
                act.activation(hi, st, ACT.Copy).then_inc(c_hi, 1)
            act.wait_ge(pad_set, 4)

            def turned(k, ts):
                for n in ts:
                    act.wait_ge(t_mm, after(k, TI, n))
                    if n == 0:
                        act.wait_ge(f_mm, after(k, FI, -1))
                    act.activation(xt[:, 0, n, :], ps_f[:, n % 2, 0:QC], ACT.Copy).then_inc(t_hi, 1)

            def forward(k, j, ns=range(4)):
                for n in ns:
                    i = 4 * j + n
                    act.wait_ge(f_mm, after(k, FI, i))
                    if n == 0:
                        act.wait_ge(a_mm, after(k, FI, 4 * (j - 2) + 3))
                    act.activation(xf[:, j % 2, 0, n, :], ps_f[0:BS, i % 2, 0:FQ], ACT.Copy).then_inc(f_hi, 1)

            def biased(k, j, n):
                par, ri = divmod(n, 2)
                u = 2 * j + par
                if n == 0:
                    act.wait_ge(w1_loaded[j % 2], 64 * k + 32 * (j // 2 + 1))
                if ri == 0:
                    act.wait_ge(h_lo, after(k, 2 * QB, u - 2))
                act.wait_ge(a_mm, after(k, FI, 2 * u + ri))
                act.activation(hf[:, par, ri, :], ps_a[0:BS, ri, 0:FQ], ACT.Identity, bias=bt[:, j % 2, ri:ri + 1]).then_inc(a_out, 1)
                if ri == 1:
                    act.wait_ge(a_out, after(k, FI, 2 * u + 1))
                    act.wait_ge(mag_done, after(k, 2 * QB, u - 2))
                    act.activation(sq[:, par, :, :], hf[:, par, :, :], ACT.Square).then_inc(sq_done, 1)

            def hidden(k, j, par):
                u = 2 * j + par
                act.wait_ge(mag_done, after(k, 2 * QB, u))
                act.wait_ge(b_mm, after(k, BI, 6 * (j - 1) + 3 * par + 2))
                act.activation(hh[0:BS, 0, 2 * par * FQ:2 * (par + 1) * FQ], hf[:, par, :, :].rearrange("p r n -> p (r n)"), ACT.Copy).then_inc(h_hi, 1)

            def second(k, j, n):
                par, ch = divmod(n, 3)
                i = 6 * j + n
                act.wait_ge(b_mm, after(k, BI, i))
                if i == 0:
                    act.wait_ge(i_mm, after(k, 2 * QT, -1))
                src = ps_b[:, i % 2, 0:2 * BS].rearrange("p (r n) -> p r n", r=2)
                cs = slice(j * BS, (j + 1) * BS)
                if ch < 2:
                    act.activation(y[:, 0, 4 * par + ch:4 * par + ch + 3:2, cs], src, ACT.Copy).then_inc(y_hi, 1)
                else:
                    for r in range(2):
                        lo = 64 * par + 32 * r
                        op = act.activation(y[lo:lo + REST, 0, KCH - 1, cs], src[0:REST, r, :], ACT.Copy)
                    op.then_inc(y_hi, 1)

            turned(0, range(TI))

            def turn(k, last):
                for what, j, n in ORDER:
                    if what == "F":
                        forward(k, j, (n,))
                    if what == "A":
                        biased(k, j, n)
                    if what == "H":
                        hidden(k, j, n)
                    if what == "B":
                        second(k, j, n)
                    if what == "T" and not last:
                        turned(k + 1, (n,))
            with act.Fori(0, TURNS - 1) as k:
                turn(k, False)
            turn(TURNS - 1, True)

        @block.vector
        def _(dve):
            for q, n in ((norm_done, QT), (t_lo, TI), (f_lo, FI), (mag_done, 2 * QB), (mask_done, 4 * QB),
                         (h_lo, 2 * QB), (y_lo, BI), (add1, 2 * QT), (add2, 2 * QT)):
                dve.sem_inc(q, n)
            for n in range(len(CONST)):
                st, _, hi, lo = cslot(n)
                dve.wait_ge(c_hi, n + 1)
                dve.tensor_tensor(lo, st, f(hi), ALU.subtract).then_inc(c_lo, 1)
            dve.memset(f(hh[:, :, 4 * FQ:HP]), 0.0).then_inc(pad_set, 1)
            dve.wait_ge(pad_set, 1)
            dve.memset(f(hh[BS:BS + 1, 0, :]), 1.0).then_inc(pad_set, 1)
            dve.memset(f(hh[BS:BS + 1, 1, :]), 0.0).then_inc(pad_set, 1)
            dve.memset(f(y[:, :, KCH - 1, :]), 0.0).then_inc(pad_set, 1)

            def norm(k, ts):
                for t in ts:
                    if t == 0:
                        dve.wait_ge(x_loaded, 16 * (k + 1))
                    col = k * QT + t
                    dve.tensor_scalar(xs[:, t, :], xs[:, t, :], mean[:, bass.ds(col, 1)], rstd[:, bass.ds(col, 1)],
                                      ALU.subtract, ALU.mult).then_inc(norm_done, 1)

            def turned(k, ts):
                for n in ts:
                    dve.wait_ge(t_hi, after(k, TI, n))
                    dve.tensor_tensor(xt[:, 1, n, :], ps_f[:, n % 2, 0:QC], f(xt[:, 0, n, :]), ALU.subtract).then_inc(t_lo, 1)

            def forward(k, j, ns=range(4)):
                for n in ns:
                    i = 4 * j + n
                    dve.wait_ge(f_hi, after(k, FI, i))
                    dve.tensor_tensor(xf[:, j % 2, 1, n, :], ps_f[0:BS, i % 2, 0:FQ], f(xf[:, j % 2, 0, n, :]), ALU.subtract).then_inc(f_lo, 1)

            def masked(k, j, par):
                u = 2 * j + par
                h, m = hf[:, par, :, :], sq[:, par, :, :]
                dve.wait_ge(sq_done, after(k, 2 * QB, u))
                dve.tensor_tensor(m[:, 0, :], m[:, 0, :], m[:, 1, :], ALU.add).then_inc(mask_done, 1)
                dve.wait_ge(mask_done, after(k, 4 * QB, 2 * u))
                dve.tensor_scalar(m[:, 0, :], m[:, 0, :], FEPS, T2, ALU.add, ALU.is_gt).then_inc(mask_done, 1)
                dve.wait_ge(mask_done, after(k, 4 * QB, 2 * u + 1))
                dve.tensor_tensor(h, h, m[:, 0:1, :].broadcast_to([BS, 2, FQ]), ALU.mult).then_inc(mag_done, 1)

            def hidden(k, j, par):
                u = 2 * j + par
                cols = slice(2 * par * FQ, 2 * (par + 1) * FQ)
                dve.wait_ge(h_hi, after(k, 2 * QB, u))
                dve.tensor_tensor(hh[0:BS, 1, cols], hf[:, par, :, :].rearrange("p r n -> p (r n)"), f(hh[0:BS, 0, cols]),
                                  ALU.subtract).then_inc(h_lo, 1)

            def second(k, j, n):
                par, ch = divmod(n, 3)
                i = 6 * j + n
                src = ps_b[:, i % 2, 0:2 * BS].rearrange("p (r n) -> p r n", r=2)
                cs = slice(j * BS, (j + 1) * BS)
                dve.wait_ge(y_hi, after(k, BI, i))
                if ch < 2:
                    cc = slice(4 * par + ch, 4 * par + ch + 3, 2)
                    dve.tensor_tensor(y[:, 1, cc, cs], src, f(y[:, 0, cc, cs]), ALU.subtract).then_inc(y_lo, 1)
                else:
                    for r in range(2):
                        rows = slice(64 * par + 32 * r, 64 * par + 32 * r + REST)
                        op = dve.tensor_tensor(y[rows, 1, KCH - 1, cs], src[0:REST, r, :], f(y[rows, 0, KCH - 1, cs]), ALU.subtract)
                    op.then_inc(y_lo, 1)

            def added(k, t, par):
                if par == 0:
                    dve.wait_ge(r_loaded[t], 16 * (k + 1))
                dve.wait_ge(i_mm, after(k, 2 * QT, 2 * t + par))
                for q, h in enumerate((slice(0, HALF), slice(HALF, N))):
                    if par == 0:
                        dve.tensor_tensor(xr[:, t, h], ps_i[:, 0, :], xr[:, t, h], ALU.add).then_inc(add1, 1)
                    else:
                        dve.wait_ge(add1, after(k, 2 * QT, 2 * t + q))
                        dve.tensor_tensor(xr[:, t, h], xr[:, t, h], ps_i[:, 1, :], ALU.add if q == 0 else ALU.subtract).then_inc(add2, 1)

            norm(0, range(QT))
            turned(0, range(TI))

            def turn(k, last):
                for what, j, n in ORDER:
                    if what == "F":
                        forward(k, j, (n,))
                    if what == "M":
                        masked(k, j, n)
                    if what == "H":
                        hidden(k, j, n)
                    if what == "B":
                        second(k, j, n)
                    if what == "E":
                        added(k, j, n)
                    if what == "N" and not last:
                        norm(k + 1, (n,))
                    if what == "T" and not last:
                        turned(k + 1, (n,))
            with dve.Fori(0, TURNS - 1) as k:
                turn(k, False)
            turn(TURNS - 1, True)

        @block.gpsimd
        def _(pool):
            pool.sem_inc(fold_done, 2 * QT)
            with pool.Fori(0, TURNS) as k:
                pool.wait_ge(t_mm, after(k, TI, -1))
                for t in range(QT):
                    pool.wait_ge(norm_done, after(k, QT, t))
                    pool.tensor_tensor(ev[:, t, :], xs[:, t, 0:HALF], xs[:, t, HALF:N], ALU.add).then_inc(fold_done, 1)
                    pool.tensor_tensor(xs[:, t, HALF:N], xs[:, t, 0:HALF], xs[:, t, HALF:N], ALU.subtract).then_inc(fold_done, 1)


def build(nc, B, x, w_qkv, b_qkv, w_proj, b_proj, w1, b1, w2, b2, avg_in, ident_in, df_in, di_in, out):
    xv = x.rearrange("b c h w -> b c (h w)")
    qk_scr = nc.dram_tensor("qk_scr", [4, B * C, N], F32, kind="Internal").ap()
    v_scr = nc.dram_tensor("v_scr", [B * HEADS, P, NT, 2 * D], F32, kind="Internal").ap()
    o_scr = nc.dram_tensor("o_scr", [B * C, N], F32, kind="Internal").ap()
    den_scr = nc.dram_tensor("den_scr", [B * HEADS, N], F32, kind="Internal").ap()
    rec_scr = nc.dram_tensor("rec_scr", [B * HEADS, N], F32, kind="Internal").ap()
    x1_scr = nc.dram_tensor("x1_scr", [B * C, N], F32, kind="Internal").ap()
    w_scr = nc.dram_tensor("w_scr", [NBLK, BS + 1, WCOLS], F32, kind="Internal").ap()
    with ExitStack() as ctx:
        sb = lambda n, s, d=F32: ctx.enter_context(nc.sbuf_tensor(n, s, d))
        mean, rstd, ident = sb("mean", [P, B * CT]), sb("rstd", [P, B * CT]), sb("ident", [P, P])
        with nc.sbuf_tensor("avg", [P, len(AVG_PAIRS), P], F32) as avg:
            stats_stage(nc, B, xv, avg_in, ident_in, avg, ident, mean, rstd)
            qkv_stage(nc, B, xv, w_qkv, b_qkv, mean, rstd, qk_scr, v_scr)
            attend_stage(nc, B, ident, qk_scr, v_scr, o_scr, den_scr)
            project_stage(nc, B, xv, w_proj, b_proj, b_qkv[2 * C:3 * C], w1, w2, b2, o_scr, den_scr, rec_scr, x1_scr, w_scr, avg, mean, rstd)
        filter_stage(nc, B, ident, df_in, di_in, b1, x1_scr, w_scr, mean, rstd, out.rearrange("b c h w -> (b c) (h w)"))


def constants():
    avg = np.zeros([P, len(AVG_PAIRS), P], np.float32)
    for i, (a, b) in enumerate(AVG_PAIRS):
        ga, gb = (a * P + np.arange(P)) // GROUP, (b * P + np.arange(P)) // GROUP
        avg[:, i, :] = (ga[:, None] == gb[None, :]) / GROUP
    h, w = np.divmod(np.arange(HALF), W)
    df = np.zeros([P, 2, HN, 2 * FQ], np.float32)
    di = np.zeros([P, KCH, HALF], np.float32)
    for par in range(2):
        kh, kw = np.divmod(np.arange(FQ), KW)
        kh = 2 * kh + par
        turn = (kh[:, None] * h[None, :] * (W // 1) + kw[:, None] * w[None, :] * H) % (H * W)
        ang = 2 * np.pi * turn / (H * W)
        s = 1 / math.sqrt(H * W)
        re, im = np.cos(ang) * s, -np.sin(ang) * s
        full = np.concatenate([re, im], 0).T
        df[:, par] = full.reshape(HN, P, 2 * FQ).transpose(1, 0, 2)
        c = np.where((kw == 0) | (kw == W // 2), 1.0, 2.0)[:, None]
        ire, iim = c * re, c * im
        for ch in range(2):
            di[:, 4 * par + ch] = ire[ch * P:(ch + 1) * P]
            di[:, 4 * par + 2 + ch] = iim[ch * P:(ch + 1) * P]
        di[64 * par:64 * par + REST, 8] = ire[2 * P:]
        di[64 * par + 32:64 * par + 32 + REST, 8] = iim[2 * P:]
    return {"avg": avg, "ident": np.eye(P, dtype=np.float32), "df": df, "di": di}


_INS = ["x", "L0_conv_w_qkv", "L0_conv_b_qkv", "L0_conv_w_proj", "L0_conv_b_proj", "L1_conv_w1", "L1_conv_b1", "L1_conv_w2", "L1_conv_b2"]


def kernel(**inputs):
    import concourse.bacc as bacc
    from concourse.bass_utils import run_bass_kernel_spmd

    nc = bacc.Bacc("TRN2", target_bir_lowering=False, num_devices=1)
    arrays, args = {}, []
    for name, a in [(n, np.ascontiguousarray(inputs[n])) for n in _INS] + list(constants().items()):
        arrays[f"in_{name}"] = a
        args.append(nc.dram_tensor(f"in_{name}", a.shape, mybir.dt.from_np(a.dtype), kind="ExternalInput").ap())
    x = arrays["in_x"]
    out = nc.dram_tensor("out_0", x.shape, F32, kind="ExternalOutput").ap()
    build(nc, x.shape[0], *args, out)
    r = run_bass_kernel_spmd(nc, [arrays], core_ids=[0])
    return r.results[0]["out_0"]
```

```python
import math
from contextlib import ExitStack

import numpy as np
import concourse.bass as bass
from concourse import mybir

F32 = mybir.dt.float32
F32R = mybir.dt.float32r
ACT = mybir.ActivationFunctionType
ALU = mybir.AluOpType
AX = mybir.AxisListType

P = 128
C = 768
CT = C // P
H = W = 32
N = H * W
NT = N // P
HALF = N // 2
HEADS = 12
D = C // HEADS
GROUP = C // 32
NBLK = 8
BS = C // NBLK
KW = W // 2 + 1
FQ = (H // 2) * KW
FEPS = 1e-8
THRESH = np.float32(0.01)


def largest_square():
    t = np.float32(THRESH * THRESH)
    while np.sqrt(np.nextafter(t, np.float32(1)) + np.float32(FEPS)) <= THRESH:
        t = np.nextafter(t, np.float32(1))
    while np.sqrt(t + np.float32(FEPS)) > THRESH:
        t = np.nextafter(t, np.float32(0))
    return float(t)


HN = HALF // P
REST = FQ - 2 * P
KCH = 9


def after(turn, per_turn, k):
    return turn * per_turn + (per_turn + k + 1)


def f(ap):
    return ap.bitcast(F32)


AVG_PAIRS = [(a, b) for b in range(3) for a in range(3)
             if (a * P) // GROUP <= ((b + 1) * P - 1) // GROUP and (b * P) // GROUP <= ((a + 1) * P - 1) // GROUP]


def group_average(pe, out, avg, col):
    last = None
    for b in range(3):
        ins = [i for i, p in enumerate(AVG_PAIRS) if p[1] == b]
        for n, i in enumerate(ins):
            last = pe.matmul(out(b), avg[:, i, :], col(AVG_PAIRS[i][0]), start=(n == 0), stop=(n == len(ins) - 1))
    return last


class GroupStats:
    PER_DVE, PER_PE, PER_ACT = 7, 2, 1

    def __init__(self, mv, n, avg, mean, rstd, small, ps, sems, eps=1e-5):
        self.mv, self.n, self.avg, self.mean, self.rstd, self.ps, self.eps = mv, n, avg, mean, rstd, ps, eps
        self.cm, self.e = small[:, 0, 0:n], small[:, 1, 0:n]
        self.dve_ready, self.pe_done, self.act_done = sems

    def average(self, pe, src, at):
        v3 = lambda ap: ap.rearrange("p (n t) -> p t n", t=3)
        dst = v3(self.ps[:, at:at + self.n])
        return group_average(pe, lambda b: dst[:, b, :], self.avg, lambda a: v3(src)[:, a, :])

    def vector_1(self, dve):
        dve.tensor_scalar(self.cm, self.mv[:, :, 0], 1.0, None, ALU.mult).then_inc(self.dve_ready, 1)

    def tensor_2(self, pe, count):
        pe.wait_ge(self.dve_ready, count(self.PER_DVE, 1))
        self.average(pe, self.cm, 0).then_inc(self.pe_done, 1)

    def vector_3(self, dve, count):
        dve.wait_ge(self.pe_done, count(self.PER_PE, 1))
        dve.tensor_copy(self.mean, self.ps[:, 0:self.n]).then_inc(self.dve_ready, 1)
        dve.wait_ge(self.dve_ready, count(self.PER_DVE, 2))
        dve.tensor_tensor(self.e, self.cm, self.mean, ALU.subtract).then_inc(self.dve_ready, 1)
        dve.wait_ge(self.dve_ready, count(self.PER_DVE, 3))
        dve.tensor_tensor(self.e, self.e, self.e, ALU.mult).then_inc(self.dve_ready, 1)
        dve.wait_ge(self.dve_ready, count(self.PER_DVE, 4))
        dve.tensor_tensor(self.e, self.e, self.mv[:, :, 1], ALU.add).then_inc(self.dve_ready, 1)

    def tensor_4(self, pe, count):
        pe.wait_ge(self.dve_ready, count(self.PER_DVE, 5))
        self.average(pe, self.e, 64).then_inc(self.pe_done, 1)

    def vector_5(self, dve, count):
        dve.wait_ge(self.pe_done, count(self.PER_PE, 2))
        dve.tensor_scalar(self.e, self.ps[:, 64:64 + self.n], self.eps, None, ALU.add).then_inc(self.dve_ready, 1)

    def scalar_6(self, act, count):
        act.wait_ge(self.dve_ready, count(self.PER_DVE, 6))
        act.activation(self.cm, self.e, ACT.Sqrt).then_inc(self.act_done, 1)

    def vector_7(self, dve, count):
        dve.wait_ge(self.act_done, count(self.PER_ACT, 1))
        dve.reciprocal(self.rstd, self.cm).then_inc(self.dve_ready, 1)


def qkv_stage(nc, B, x, w_qkv, b_qkv, avg_in, ident_in, avg, ident, qk_scr, v_scr):
    RING = 4
    QK_TILES = 2 * CT
    VW = 384
    VH = VW // D
    PER_HALF = QK_TILES + (NT // 2) * (C // VW)
    ITEMS = 2 * PER_HALF
    PIECES = 2 * CT
    with ExitStack() as ctx:
        sb = lambda n, s, d=F32: ctx.enter_context(nc.sbuf_tensor(n, s, d))
        sem = lambda n: ctx.enter_context(nc.semaphore(n))
        wh = sb("q_wh", [P, CT, 3 * C], F32R)
        wl = sb("q_wl", [P, CT, 3 * C], F32R)
        xs = sb("q_x", [P, CT, N])
        xh = sb("q_xh", [P, 2, CT, HALF], F32R)
        xl = sb("q_xl", [P, 2, CT, HALF], F32R)
        ob = sb("q_out", [P, RING, 2 * HALF], F32R)
        bias = sb("q_bias", [P, QK_TILES])
        ps = ctx.enter_context(nc.psum_tensor("q_ps", [P, RING, 512], F32))
        bn, mv, small = sb("q_bn", [P, CT, 2, 6]), sb("q_mv", [P, CT, 2]), sb("q_small", [P, 2, CT])
        dev, var = sb("q_dev", [P, CT, 4]), sb("q_var", [P, CT])
        mean, rstd = sb("q_mean", [P, CT]), sb("q_rstd", [P, CT])
        ps_g = ctx.enter_context(nc.psum_tensor("q_ps_g", [P, 512], F32))
        WP, WS = 3 * C // 2, 3
        W_PIECES = [(t, slice(k * WP, (k + 1) * WP)) for t in range(CT) for k in range(2)]
        wst = [f(ob[:, :, :]).rearrange("p r n -> p (r n)")[:, k * WP:(k + 1) * WP] for k in range(WS)]
        w_loaded = [sem(f"q_w_loaded{k}") for k in range(3)]
        bias_loaded, x_loaded = sem("q_bias_loaded"), sem("q_x_loaded")
        wh_done, wl_done = sem("q_wh_done"), sem("q_wl_done")
        norm_done, xh_done, xl_done = sem("q_norm_done"), sem("q_xh_done"), sem("q_xl_done")
        mm_done, hi_done, lo_done = sem("q_mm_done"), sem("q_hi_done"), sem("q_lo_done")
        stored = [sem(f"q_stored{r}") for r in range(RING)]
        const_loaded, bn_done, agg_done = sem("q_const_loaded"), sem("q_bn_done"), sem("q_agg_done")
        dve_ready, pe_done, act_done = sem("q_dve_ready"), sem("q_pe_done"), sem("q_act_done")
        group = GroupStats(mv, CT, avg, mean[:, :], rstd[:, :], small, ps_g, (dve_ready, pe_done, act_done))
        of_turn = lambda b: (lambda per_turn, n: after(b, per_turn, n - 1))
        block = ctx.enter_context(nc.Block())

        def item(s):
            h, r = divmod(s, PER_HALF)
            return (h, r, None) if r < QK_TILES else (h, (r - QK_TILES) // 2, (r - QK_TILES) % 2)

        PIECE_AT = {1 + k: (1, k) for k in range(CT)}
        NEXT_AT = {PER_HALF + 8 + k: (0, k) for k in range(CT)}
        BN_AT = {PER_HALF - 8 + t: t for t in range(CT)}
        AGG = 7
        AGG_AT = PER_HALF - 2
        GROUP_2, GROUP_3, GROUP_4, GROUP_5, GROUP_6, GROUP_7 = (PER_HALF + k for k in (0, 1, 3, 4, 5, 6))

        @block.sync
        def _(sp):
            sp.dma_start(bias[:, :], b_qkv[0:2 * C].rearrange("(m p) -> p m", p=P),
                         allow_slow_non_contiguous=True).then_inc(bias_loaded, 16)
            sp.dma_start(avg[:, :, :], avg_in).then_inc(const_loaded, 16)
            sp.dma_start(ident[:, :], ident_in).then_inc(const_loaded, 16)
            for k, (t, cols) in enumerate(W_PIECES):
                if k >= WS:
                    sp.wait_ge(wl_done, k - WS + 1)
                sp.dma_start(wst[k % WS], w_qkv[t * P:(t + 1) * P, cols]).then_inc(w_loaded[k % WS], 16)
            for r in range(RING):
                sp.sem_inc(stored[r], 16 * ITEMS // RING)

            def batch(b):
                for s in range(ITEMS):
                    h, m, vc = item(s)
                    r = s % RING
                    sp.wait_ge(lo_done, after(b, ITEMS, s))
                    if vc is None:
                        kind = 0 if m < CT else 2
                        row = b * C + (m % CT) * P
                        sp.dma_start(qk_scr[kind:kind + 2, bass.ds(row, P), h * HALF:(h + 1) * HALF].rearrange("k p n -> p k n"),
                                     f(ob[:, r, :]).rearrange("p (k n) -> p k n", k=2)).then_inc(stored[r], 16)
                    else:
                        sp.dma_start(v_scr[bass.ds(b * HEADS + vc * VH, VH), :, h * (NT // 2) + m, :].rearrange("g p e -> p g e"),
                                     f(ob[:, r, 0:2 * VW]).rearrange("p (g e) -> p g e", g=VH)).then_inc(stored[r], 16)
            with sp.Fori(0, B) as b:
                batch(b)
            for r in range(RING):
                sp.wait_ge(stored[r], 16 * ITEMS // RING * (B + 1))

        @block.gpsimd
        def _(pool):
            with pool.Fori(0, B) as b:
                pool.wait_ge(xl_done, after(b, PIECES, -1))
                pool.dma_start(xs[:, :, :], x[b].rearrange("(t p) n -> p t n", p=P)).then_inc(x_loaded, 16)

        @block.scalar
        def _(act):
            act.sem_inc(hi_done, ITEMS)
            act.sem_inc(xh_done, PIECES)
            act.sem_inc(act_done, GroupStats.PER_ACT)
            for k, (t, cols) in enumerate(W_PIECES):
                act.wait_ge(w_loaded[k % WS], 16 * (k // WS + 1))
                act.activation(wh[:, t, cols], wst[k % WS], ACT.Copy).then_inc(wh_done, 1)
                if k == 3:
                    group.scalar_6(act, of_turn(0))
            act.wait_ge(bias_loaded, 16)

            def piece(b, h, t):
                act.wait_ge(norm_done, after(b, PIECES, h * CT + t))
                if t == 0:
                    act.wait_ge(mm_done, after(b, ITEMS, h * PER_HALF + PER_HALF - 1 - ITEMS))
                act.activation(xh[:, h, t, :], xs[:, t, h * HALF:(h + 1) * HALF], ACT.Copy).then_inc(xh_done, 1)

            for t in range(CT):
                piece(0, 0, t)
            act.wait_ge(wl_done, len(W_PIECES))

            def batch(b, last):
                for s in range(ITEMS):
                    if s == GROUP_6 and not last:
                        group.scalar_6(act, of_turn(b + 1))
                    if s in PIECE_AT:
                        piece(b, *PIECE_AT[s])
                    if s in NEXT_AT and not last:
                        piece(b + 1, *NEXT_AT[s])
                    h, m, vc = item(s)
                    r = s % RING
                    act.wait_ge(mm_done, after(b, ITEMS, s))
                    act.wait_ge(stored[r], 16 * after(b, ITEMS // RING, s // RING - 1))
                    if vc is None:
                        act.activation(ob[:, r, 0:HALF], ps[:, r, :], ACT.Identity, bias=bias[:, m:m + 1]).then_inc(hi_done, 1)
                    else:
                        dst = ob[:, r, 0:2 * VW].rearrange("p (g k e) -> p g k e", g=VH, k=2)[:, :, 0, :]
                        act.activation(dst, ps[:, r, 0:VW].rearrange("p (g e) -> p g e", g=VH), ACT.Copy).then_inc(hi_done, 1)
            if B > 1:
                with act.Fori(0, B - 1) as b:
                    batch(b, False)
            batch(B - 1, True)

        @block.vector
        def _(dve):
            for q, n in ((lo_done, ITEMS), (xl_done, PIECES), (norm_done, PIECES), (bn_done, 2 * CT), (agg_done, AGG),
                         (dve_ready, GroupStats.PER_DVE)):
                dve.sem_inc(q, n)

            def bn_piece(b, t):
                if t == 0:
                    dve.wait_ge(x_loaded, 16 * (b + 1))
                    dve.wait_ge(agg_done, after(b, AGG, -1))
                for h in range(2):
                    dve.bn_stats(bn[:, t, h, :], xs[:, t, h * HALF:(h + 1) * HALF]).then_inc(bn_done, 1)

            def aggregate(b):
                parts = bn[:, :, :, :].rearrange("p t h (e k) -> p t (h e) k", k=3)
                means, squares = parts[:, :, :, 1], parts[:, :, :, 2]
                count = N // 4
                dve.wait_ge(bn_done, after(b, 2 * CT, 2 * CT - 1))
                dve.wait_ge(dve_ready, after(b, GroupStats.PER_DVE, -1))
                dve.reduce_sum(mv[:, :, 1], means, axis=AX.X).then_inc(agg_done, 1)
                dve.wait_ge(agg_done, after(b, AGG, 0))
                dve.tensor_scalar(mv[:, :, 0], mv[:, :, 1], 0.25, None, ALU.mult).then_inc(agg_done, 1)
                dve.wait_ge(agg_done, after(b, AGG, 1))
                dve.tensor_tensor(dev[:, :, :], means, mv[:, :, 0:1].broadcast_to([P, CT, 4]), ALU.subtract).then_inc(agg_done, 1)
                dve.wait_ge(agg_done, after(b, AGG, 2))
                dve.tensor_tensor(dev[:, :, :], dev[:, :, :], dev[:, :, :], ALU.mult).then_inc(agg_done, 1)
                dve.wait_ge(agg_done, after(b, AGG, 3))
                dve.scalar_tensor_tensor(dev[:, :, :], squares, 1.0 / count, dev[:, :, :], ALU.mult, ALU.add).then_inc(agg_done, 1)
                dve.wait_ge(agg_done, after(b, AGG, 4))
                dve.reduce_sum(var[:, :], dev[:, :, :], axis=AX.X).then_inc(agg_done, 1)
                dve.wait_ge(agg_done, after(b, AGG, 5))
                dve.tensor_scalar(mv[:, :, 1], var[:, :], 0.25, None, ALU.mult).then_inc(agg_done, 1)
                dve.wait_ge(agg_done, after(b, AGG, 6))
                group.vector_1(dve)

            def split_weights(ks):
                for k in ks:
                    t, cols = W_PIECES[k]
                    dve.wait_ge(wh_done, k + 1)
                    dve.tensor_tensor(wl[:, t, cols], wst[k % WS], f(wh[:, t, cols]), ALU.subtract).then_inc(wl_done, 1)

            def norm(b, h, t):
                if h == 0 and t == 0:
                    dve.wait_ge(dve_ready, after(b, GroupStats.PER_DVE, GroupStats.PER_DVE - 1))
                sl = xs[:, t, h * HALF:(h + 1) * HALF]
                dve.tensor_scalar(sl, sl, mean[:, t:t + 1], rstd[:, t:t + 1], ALU.subtract, ALU.mult).then_inc(norm_done, 1)

            def rest(b, h, t):
                dve.wait_ge(xh_done, after(b, PIECES, h * CT + t))
                dve.tensor_tensor(xl[:, h, t, :], xs[:, t, h * HALF:(h + 1) * HALF], f(xh[:, h, t, :]), ALU.subtract).then_inc(xl_done, 1)

            for t in range(CT):
                bn_piece(0, t)
            aggregate(0)
            split_weights((0, 1))
            group.vector_3(dve, of_turn(0))
            split_weights((2, 3))
            group.vector_5(dve, of_turn(0))
            split_weights((4,))
            group.vector_7(dve, of_turn(0))
            for t in range(CT):
                norm(0, 0, t)
            split_weights(range(5, len(W_PIECES)))
            for t in range(CT):
                rest(0, 0, t)
            dve.wait_ge(bias_loaded, 16)

            def batch(b, last):
                for s in range(ITEMS):
                    if not last:
                        if s in BN_AT:
                            bn_piece(b + 1, BN_AT[s])
                        if s == AGG_AT:
                            aggregate(b + 1)
                        if s == GROUP_3:
                            dve.wait_ge(norm_done, after(b, PIECES, PIECES - 1))
                            group.vector_3(dve, of_turn(b + 1))
                        if s == GROUP_5:
                            group.vector_5(dve, of_turn(b + 1))
                        if s == GROUP_7:
                            group.vector_7(dve, of_turn(b + 1))
                    for table, bb in ((PIECE_AT, b), (NEXT_AT, b + 1)):
                        if table is NEXT_AT and last:
                            continue
                        if s + 1 in table:
                            norm(bb, *table[s + 1])
                        if s in table:
                            rest(bb, *table[s])
                    h, m, vc = item(s)
                    r = s % RING
                    dve.wait_ge(hi_done, after(b, ITEMS, s))
                    if vc is None:
                        dve.scalar_tensor_tensor(ob[:, r, HALF:2 * HALF], ps[:, r, :], bias[:, m:m + 1], f(ob[:, r, 0:HALF]),
                                                 ALU.add, ALU.subtract).then_inc(lo_done, 1)
                    else:
                        o4 = ob[:, r, 0:2 * VW].rearrange("p (g k e) -> p g k e", g=VH, k=2)
                        dve.tensor_tensor(o4[:, :, 1, :], ps[:, r, 0:VW].rearrange("p (g e) -> p g e", g=VH), f(o4[:, :, 0, :]),
                                          ALU.subtract).then_inc(lo_done, 1)
            if B > 1:
                with dve.Fori(0, B - 1) as b:
                    batch(b, False)
            batch(B - 1, True)

        @block.tensor
        def _(pe):
            pe.sem_inc(mm_done, ITEMS)
            pe.sem_inc(pe_done, GroupStats.PER_PE)
            pe.wait_ge(const_loaded, 32)
            group.tensor_2(pe, of_turn(0))
            group.tensor_4(pe, of_turn(0))
            pe.wait_ge(wl_done, len(W_PIECES))

            def batch(b, last):
                for s in range(ITEMS):
                    if s == GROUP_2 and not last:
                        group.tensor_2(pe, of_turn(b + 1))
                    if s == GROUP_4 and not last:
                        group.tensor_4(pe, of_turn(b + 1))
                    h, m, vc = item(s)
                    r = s % RING
                    if s % PER_HALF == 0:
                        pe.wait_ge(xl_done, after(b, PIECES, h * CT + CT - 1))
                    pe.wait_ge(lo_done, after(b, ITEMS, s - RING))
                    k = 0
                    for t in range(CT):
                        for a, o in ((xh, wh), (xh, wl), (xl, wh)):
                            if vc is None:
                                mm = pe.matmul(ps[:, r, :], o[:, t, m * P:(m + 1) * P], a[:, h, t, :],
                                               start=(k == 0), stop=(k == 3 * CT - 1))
                            else:
                                mm = pe.matmul(ps[:, r, 0:VW], a[:, h, t, m * P:(m + 1) * P],
                                               o[:, t, 2 * C + vc * VW:2 * C + (vc + 1) * VW], start=(k == 0), stop=(k == 3 * CT - 1))
                            k += 1
                    mm.then_inc(mm_done, 1)
            if B > 1:
                with pe.Fori(0, B - 1) as b:
                    batch(b, False)
            batch(B - 1, True)


def attend_stage(nc, B, ident, w_proj, pwh, pwl, df, qk_scr, v_scr, o_scr, den_scr):
    HB = 3
    ST = HB * NT
    TURNS = B * HEADS // HB
    RS, RP = 2, 4
    TURN = 3
    LEAD_S, LEAD_M = 3, NT + 5
    with ExitStack() as ctx:
        sb = lambda n, s, d=F32: ctx.enter_context(nc.sbuf_tensor(n, s, d))
        sem = lambda n: ctx.enter_context(nc.semaphore(n))
        k1 = sb("a_k1", [P, HB, N], F32R)
        k2 = sb("a_k2", [D + 1, HB, N], F32R)
        q1 = sb("a_q1", [P, HB, N], F32R)
        q2 = sb("a_q2", [D + 1, HB, N], F32R)
        v = df[:, :, :, :, :].rearrange("p a b c n -> p (a b c n)")[:, 0:HB * NT * 4 * D]
        v = v.rearrange("p (r c k e) -> p r c k e", r=HB, c=NT, k=4)
        prob = sb("a_prob", [P, RP, N])
        ph = sb("a_ph", [P, RP, N], F32R)
        pl = sb("a_pl", [P, RP, N], F32R)
        mx = sb("a_mx", [P, HB, NT])
        ws = sb("a_ws", [P, CT, C])
        ob = sb("a_o", [P, HB, N])
        ps_s = ctx.enter_context(nc.psum_tensor("a_ps_s", [P, RS, N], F32))
        ps_m = ctx.enter_context(nc.psum_tensor("a_ps_m", [P, N], F32))
        ps_o = ctx.enter_context(nc.psum_tensor("a_ps_o", [P, N], F32))
        qk_loaded = [sem(f"a_qk_loaded{r}") for r in range(HB)]
        v_loaded = [sem(f"a_v_loaded{r}") for r in range(HB)]
        o_stored = [sem(f"a_o_stored{r}") for r in range(HB)]
        consts_set, w_loaded, wh_done, wl_done = sem("a_consts_set"), sem("a_w_loaded"), sem("a_wh_done"), sem("a_wl_done")
        max_mm, max_read, turned, shift_set = sem("a_max_mm"), sem("a_max_read"), sem("a_turned"), sem("a_shift_set")
        scores_done, exp_done, hi_done, lo_done = sem("a_scores_done"), sem("a_exp_done"), sem("a_hi_done"), sem("a_lo_done")
        pv_done, sums_out = sem("a_pv_done"), sem("a_sums_out")
        block = ctx.enter_context(nc.Block())
        halves = [slice(h * HALF, (h + 1) * HALF) for h in range(2)]
        first_banks = (ps_m[:, :], ps_s[:, 0, :], ps_s[:, 1, :])

        @block.sync
        def _(sp):
            for r in range(HB):
                sp.sem_inc(o_stored[r], 32)

            def load_qk(g, r):
                rows = bass.ds(g * D, D)
                for dst, kind in ((q1[0:D, r, :], 0), (k2[0:D, r, :], 2), (k1[0:D, r, :], 2), (k1[D:P, r, :], 3),
                                  (q1[D:P, r, :], 0), (q2[0:D, r, :], 1)):
                    sp.dma_start(f(dst), qk_scr[kind, rows, :]).then_inc(qk_loaded[r], 16)

            def load_v(g, r):
                sp.dma_start(f(v[:, r, :, 0::2, :]).rearrange("p c k e -> p (c k) e"), v_scr[g].rearrange("p c (k e) -> p (c k) e", k=2)).then_inc(v_loaded[r], 16)

            for r in range(HB):
                load_qk(r, r)
                load_v(r, r)
            sp.dma_start(ws[:, :, :], w_proj.rearrange("(t p) n -> p t n", p=P)).then_inc(w_loaded, 16)

            def turn(i, last):
                for r in range(HB):
                    if not last:
                        sp.wait_ge(scores_done, after(i, ST, r * NT + NT - 1))
                        load_qk(i * HB + (HB + r), r)
                        sp.wait_ge(pv_done, after(i, 2 * ST, 2 * (r * NT + NT) - 1))
                        load_v(i * HB + (HB + r), r)
                    sp.wait_ge(sums_out, after(i, 2 * HB, 2 * r + 1))
                    sp.dma_start(o_scr[bass.ds((i * HB + r) * D, D), :], ob[0:D, r, :]).then_inc(o_stored[r], 16)
                    sp.dma_start(den_scr[bass.ds(i * HB + r, 1), :], ob[D:D + 1, r, :]).then_inc(o_stored[r], 16)
            with sp.Fori(0, TURNS - 1) as i:
                turn(i, False)
            turn(TURNS - 1, True)
            for r in range(HB):
                sp.wait_ge(o_stored[r], 32 * (TURNS + 1))

        @block.tensor
        def _(pe):
            for q, n in ((max_mm, ST), (turned, HB), (scores_done, ST), (pv_done, 2 * ST)):
                pe.sem_inc(q, n)

            def row_max(i, s, bank=ps_m[:, :], uses=1):
                j, s = divmod(s, ST)
                i, r, c = i + j, s // NT, s % NT
                if c == 0:
                    pe.wait_ge(qk_loaded[r], 96 * (i + 1))
                    pe.wait_ge(shift_set, after(i, HB, r - 1))
                pe.wait_ge(max_read, after(i, ST, s - uses))
                for h in halves:
                    mm = pe.matmul(bank[:, h], q1[0:D, r, c * P:(c + 1) * P], k2[0:D, r, h], start=True, stop=True)
                mm.then_inc(max_mm, 1)

            def turn_max(i, r):
                j, r = divmod(r, HB)
                i = i + j
                pe.wait_ge(max_read, after(i, ST, r * NT + NT - 1))
                for c in range(NT):
                    mm = pe.transpose(ps_m[0:1, c * P:(c + 1) * P], mx[:, r, c:c + 1], ident[:, :])
                mm.then_inc(turned, 1)

            def scores(i, s):
                j, s = divmod(s, ST)
                i, r, c = i + j, s // NT, s % NT
                if c == 0:
                    pe.wait_ge(shift_set, after(i, HB, r))
                pe.wait_ge(exp_done, after(i, ST, s - RS))
                for h in halves:
                    pe.matmul(ps_s[:, s % RS, h], k1[:, r, c * P:(c + 1) * P], q1[:, r, h], start=True, stop=False)
                    mm = pe.matmul(ps_s[:, s % RS, h], k2[:, r, c * P:(c + 1) * P], q2[:, r, h], start=False, stop=True)
                mm.then_inc(scores_done, 1)

            def weighted(i, s, ns=(0, 1)):
                r, c, w = s // NT, s % NT, s % RP
                if 0 in ns:
                    pe.wait_ge(hi_done, after(i, ST, s))
                    pe.wait_ge(lo_done, after(i, ST, s))
                    if c == 0:
                        pe.wait_ge(v_loaded[r], 16 * (i + 1))
                vo = v[:, r, c, 0:2, :].rearrange("p k e -> p (k e)")
                vz = v[:, r, c, 2:4, :].rearrange("p k e -> p (k e)")
                for n in ns:
                    h = halves[n]
                    if c == 0:
                        pe.wait_ge(sums_out, after(i, 2 * HB, 2 * (r - 1) + n))
                    pe.matmul(ps_o[:, h], vo, ph[:, w, h], start=(c == 0), stop=False)
                    pe.matmul(ps_o[:, h], vo, pl[:, w, h], start=False, stop=False)
                    pe.matmul(ps_o[:, h], vz, ph[:, w, h], start=False, stop=(c == NT - 1)).then_inc(pv_done, 1)

            for s in range(NT):
                row_max(0, s, first_banks[s % 3], 3)
            turn_max(0, 0)
            pe.wait_ge(consts_set, 3)
            for s in range(LEAD_M - 1 - NT):
                if s < LEAD_S:
                    scores(0, s)
                row_max(0, NT + s)

            def turn(i, last):
                for s in range(ST):
                    c = s % NT
                    ahead = LEAD_M if c < TURN else LEAD_M - 1
                    if not (last and s + LEAD_S >= ST):
                        scores(i, s + LEAD_S)
                    if c in (NT - 1, 0) and not (last and s + LEAD_M - 1 >= ST):
                        row_max(i, s + LEAD_M - 1)
                    weighted(i, s, (0,))
                    if c == NT - 2 and not (last and s + ahead >= ST):
                        row_max(i, s + ahead)
                    weighted(i, s, (1,))
                    if c == TURN:
                        if not (last and s // NT == HB - 1):
                            turn_max(i, s // NT + 1)
                    elif c < NT - 2 and not (last and s + ahead >= ST):
                        row_max(i, s + ahead)
            with pe.Fori(0, TURNS - 1) as i:
                turn(i, False)
            turn(TURNS - 1, True)

        @block.scalar
        def _(act):
            for q, n in ((exp_done, ST), (hi_done, ST), (shift_set, HB), (sums_out, 2 * HB)):
                act.sem_inc(q, n)

            def shift(i, r):
                j, r = divmod(r, HB)
                i = i + j
                act.wait_ge(turned, after(i, HB, r))
                act.wait_ge(qk_loaded[r], 96 * (i + 1))
                act.activation(q2[D:D + 1, r, :], ps_m[0:1, :], ACT.Copy, scale=-1.0).then_inc(shift_set, 1)

            def exps(i, s):
                j, s = divmod(s, ST)
                i = i + j
                act.wait_ge(scores_done, after(i, ST, s))
                act.wait_ge(lo_done, after(i, ST, s - RP))
                act.activation(prob[:, s % RP, :], ps_s[:, s % RS, :], ACT.Exp, scale=1 / math.sqrt(D)).then_inc(exp_done, 1)

            def high(i, s):
                j, s = divmod(s, ST)
                i = i + j
                act.wait_ge(exp_done, after(i, ST, s))
                act.wait_ge(pv_done, after(i, 2 * ST, 2 * (s - RP) + 1))
                act.activation(ph[:, s % RP, :], prob[:, s % RP, :], ACT.Copy).then_inc(hi_done, 1)

            def take_sums(i, r):
                for n, h in enumerate(halves):
                    act.wait_ge(pv_done, after(i, 2 * ST, 2 * (r * NT + NT - 1) + n))
                    if n == 0:
                        act.wait_ge(o_stored[r], 32 * (i + 1))
                    act.activation(ob[:, r, h], ps_o[:, h], ACT.Copy).then_inc(sums_out, 1)

            shift(0, 0)
            for s in range(2):
                exps(0, s)
                high(0, s)
            exps(0, 2)

            def turn(i, last):
                for s in range(ST):
                    if s % NT != 0 and not (last and s + 2 >= ST):
                        exps(i, s + 2)
                    if not (last and s + 2 >= ST):
                        high(i, s + 2)
                    if last and s % 3 == 2 and s // 3 < CT:
                        act.wait_ge(w_loaded, 16)
                        act.activation(pwh[:, s // 3, :], ws[:, s // 3, :], ACT.Copy).then_inc(wh_done, 1)
                    if s % NT == NT - 1:
                        if not (last and s + 3 >= ST):
                            exps(i, s + 3)
                        take_sums(i, s // NT)
                    if s % NT == TURN + 1 and not (last and s // NT == HB - 1):
                        shift(i, s // NT + 1)
            with act.Fori(0, TURNS - 1) as i:
                turn(i, False)
            turn(TURNS - 1, True)

        @block.vector
        def _(dve):
            for q, n in ((max_read, ST), (lo_done, ST)):
                dve.sem_inc(q, n)
            dve.memset(f(k2[D:D + 1, :, :]), 1.0).then_inc(consts_set, 1)
            dve.memset(f(v[:, :, :, 1, :]), 1.0).then_inc(consts_set, 1)
            dve.memset(f(v[:, :, :, 3, :]), 0.0).then_inc(consts_set, 1)

            def take_max(i, s, bank=ps_m[:, :]):
                j, s = divmod(s, ST)
                i, r, c = i + j, s // NT, s % NT
                dve.wait_ge(max_mm, after(i, ST, s))
                if c == 0:
                    dve.wait_ge(turned, after(i, HB, r - HB))
                dve.reduce_max(mx[:, r, c:c + 1], bank, axis=AX.X).then_inc(max_read, 1)

            def low(i, s):
                j, s = divmod(s, ST)
                i, w = i + j, s % RP
                dve.wait_ge(hi_done, after(i, ST, s))
                dve.wait_ge(pv_done, after(i, 2 * ST, 2 * (s - RP) + 1))
                dve.tensor_tensor(pl[:, w, :], prob[:, w, :], f(ph[:, w, :]), ALU.subtract).then_inc(lo_done, 1)

            for s in range(LEAD_M - 1):
                take_max(0, s, first_banks[s % 3] if s < NT else ps_m[:, :])
            low(0, 0)
            low(0, 1)

            def turn(i, last):
                for s in range(ST):
                    c = s % NT
                    late = TURN < c < NT
                    if not late and not (last and s + LEAD_M - 1 >= ST):
                        take_max(i, s + LEAD_M - 1)
                    if not (last and s + 2 >= ST):
                        low(i, s + 2)
                    if late and not (last and s + LEAD_M - 1 >= ST):
                        take_max(i, s + LEAD_M - 1)
            with dve.Fori(0, TURNS - 1) as i:
                turn(i, False)
            turn(TURNS - 1, True)

        @block.gpsimd
        def _(pool):
            for t in range(CT):
                pool.wait_ge(wh_done, t + 1)
                pool.tensor_tensor(pwl[:, t, :], ws[:, t, :], f(pwh[:, t, :]), ALU.subtract).then_inc(wl_done, 1)


W1C, W2C = 3 * BS, 2 * 2 * BS
WCOLS = 2 * (W1C + W2C)


def project_stage(nc, B, x, wh, wl, avg_in, df_in, df, b_proj, b_v, w1, w2, b2, o_scr, den_scr, rec_scr, x1_scr, w_scr, mean, rstd):
    RING = 4
    ITEMS = 2 * CT
    PIECES = 2 * CT
    with ExitStack() as ctx:
        sb = lambda n, s, d=F32: ctx.enter_context(nc.sbuf_tensor(n, s, d))
        sem = lambda n: ctx.enter_context(nc.semaphore(n))
        bp, bv = sb("p_bp", [P, CT]), sb("p_bv", [P, CT])
        of = sb("p_o", [P, 2, CT, HALF])
        rb = sb("p_rb", [P, 2, CT, HALF])
        rec = sb("p_rec", [P, B * HEADS * NT])
        oh, ol = sb("p_oh", [P, 2, CT, HALF], F32R), sb("p_ol", [P, 2, CT, HALF], F32R)
        xt = sb("p_x", [P, RING, HALF])
        fw = sb("p_fw", [BS + 1, WCOLS], F32R)
        fs = sb("p_fs", [BS + 1, 2, 2, BS, 2])
        fa = sb("p_fa", [BS + 1, W1C + W2C])
        bn = sb("p_bn", [P, 12 * CT])
        bn_all = sb("p_bn_all", [P, B * 12 * CT])
        mv = sb("p_mv", [P, B * CT, 2])
        small = sb("p_small", [P, 2, B * CT])
        ps = ctx.enter_context(nc.psum_tensor("p_ps", [P, RING, 512], F32))
        ps_g = ctx.enter_context(nc.psum_tensor("p_ps_g", [P, 512], F32))
        b_loaded, d_hi, d_lo = sem("p_b_loaded"), sem("p_d_hi"), sem("p_d_lo")
        avg, avg_loaded = sb("p_avg", [P, len(AVG_PAIRS), P]), sem("p_avg_loaded")
        ds = [a[:, 1, :, :].rearrange("p t n -> p (t n)")[:, n * 2 * FQ:(n + 1) * 2 * FQ] for a in (of, rb) for n in range(HN)]
        d_loaded = [sem(f"p_d_loaded{n}") for n in range(2 * HN)]
        D_TILES = [(p, t) for p in range(2) for t in range(HN)]
        fs_loaded, row_set = [sem("p_fs_loaded0"), sem("p_fs_loaded1")], sem("p_row_set")
        fa_done, fh_done, fl_done, fw_stored = sem("p_fa_done"), sem("p_fh_done"), sem("p_fl_done"), sem("p_fw_stored")
        o_loaded = [sem("p_o_loaded0"), sem("p_o_loaded1")]
        x_loaded = [sem(f"p_x_loaded{r}") for r in range(RING)]
        stored = [sem(f"p_stored{r}") for r in range(RING)]
        oh_done, ol_done, mm_done, add_done = sem("p_oh_done"), sem("p_ol_done"), sem("p_mm_done"), sem("p_add_done")
        den_loaded, rec_done, rec_stored, on_done = sem("p_den_loaded"), sem("p_rec_done"), sem("p_rec_stored"), sem("p_on_done")
        bn_done, kept, agg_done = sem("p_bn_done"), sem("p_kept"), sem("p_agg_done")
        group = GroupStats(mv, B * CT, avg, mean[:, :], rstd[:, :], small, ps_g, (sem("p_dve_ready"), sem("p_pe_done"), sem("p_act_done")))
        once = lambda per_turn, n: n
        block = ctx.enter_context(nc.Block())
        half = lambda h: slice(h * HALF, (h + 1) * HALF)
        xrows = x.rearrange("b c n -> (b c) n")

        @block.sync
        def _(sp):
            sp.dma_start(rec[:, :], den_scr.rearrange("g n -> (g n)").rearrange("(p c) -> p c", p=P)).then_inc(den_loaded, 16)
            sp.dma_start(avg[:, :, :], avg_in).then_inc(avg_loaded, 16)
            sp.dma_start(bp[:, :], b_proj.rearrange("(m p) -> p m", p=P), allow_slow_non_contiguous=True).then_inc(b_loaded, 16)
            sp.dma_start(bv[:, :], b_v.rearrange("(m p) -> p m", p=P), allow_slow_non_contiguous=True).then_inc(b_loaded, 16)
            for r in range(RING):
                sp.sem_inc(stored[r], 16 * ITEMS // RING)

            def load_o(b, h):
                sp.wait_ge(ol_done, after(b, PIECES, h * CT + CT - 1 - PIECES))
                sp.dma_start(of[:, h, :, :], o_scr[bass.ds(b * C, C), half(h)].rearrange("(t p) n -> p t n", p=P)).then_inc(o_loaded[h], 16)

            def load_rec(b, h):
                for j in range(2):
                    src = rec_scr.rearrange("(g j) n -> j g n", j=2)[j:j + 1, bass.ds(b * CT, CT), half(h)]
                    sp.dma_start(rb[j * D:(j + 1) * D, h, :, :], src.broadcast_to([D, CT, HALF])).then_inc(o_loaded[h], 16)

            def load_x(b, s):
                h, m, r = s // CT, s % CT, s % RING
                sp.wait_ge(bn_done, after(b, ITEMS, s - RING))
                sp.wait_ge(stored[r], 16 * after(b, ITEMS // RING, s // RING - 1))
                sp.dma_start(xt[:, r, :], xrows[bass.ds(b * C + m * P, P), half(h)]).then_inc(x_loaded[r], 16)

            def batch(b, last):
                for s in range(ITEMS):
                    h, m, r = s // CT, s % CT, s % RING
                    if s in (0, 3) and not last:
                        load_o(b + 1, s // 3)
                        load_rec(b + 1, s // 3)
                    sp.wait_ge(add_done, after(b, ITEMS, s))
                    sp.dma_start(x1_scr[bass.ds(b * C + m * P, P), half(h)], xt[:, r, :]).then_inc(stored[r], 16)
                    j, s3 = divmod(s + RING - 1, ITEMS)
                    if not (last and j):
                        load_x(b + j, s3)

            load_o(0, 0)
            sp.wait_ge(rec_done, 1)
            sp.dma_start(rec_scr.rearrange("g n -> (g n)").rearrange("(p c) -> p c", p=P), rec[:, :]).then_inc(rec_stored, 16)
            sp.wait_ge(rec_stored, 16)
            load_rec(0, 0)
            for n, (p, t) in enumerate(D_TILES):
                sp.dma_start(ds[n], df_in[:, p, t, :]).then_inc(d_loaded[n], 16)
            for s in range(RING - 1):
                load_x(0, s)
            sp.wait_ge(d_lo, len(D_TILES))
            load_o(0, 1)
            load_rec(0, 1)
            if B > 1:
                with sp.Fori(0, B - 1) as b:
                    batch(b, False)
            batch(B - 1, True)
            for r in range(RING):
                sp.wait_ge(stored[r], 16 * ITEMS // RING * (B + 1))

        @block.gpsimd
        def _(pool):
            def weights(blk):
                pool.wait_ge(fs_loaded[blk % 2], 48 * (blk // 2 + 1))
                if blk:
                    pool.wait_ge(fl_done, blk)
                a1 = fa[0:BS, 0:W1C].rearrange("p (k n) -> p k n", k=3)
                a2 = fa[0:BS, W1C:].rearrange("p (k n) -> p k n", k=4)
                s1, s2 = (fs[0:BS, blk % 2, k, :, :].rearrange("p n k -> p k n") for k in range(2))
                pool.tensor_copy(a1[:, 0:2, :], s1).then_inc(fa_done, 1)
                pool.tensor_scalar(a1[:, 2, :], s1[:, 1, :], -1.0, None, ALU.mult).then_inc(fa_done, 1)
                pool.tensor_copy(a2[:, 0:2, :], s2).then_inc(fa_done, 1)
                pool.tensor_scalar(a2[:, 2, :], s2[:, 1, :], -1.0, None, ALU.mult)
                pool.tensor_copy(a2[:, 3, :], s2[:, 0, :]).then_inc(fa_done, 1)
                pool.tensor_copy(fa[BS:BS + 1, W1C:W1C + 2 * BS].rearrange("p (k n) -> p k n", k=2),
                                 fs[BS:BS + 1, blk % 2, 1, :, :].rearrange("p n k -> p k n")).then_inc(fa_done, 1)
                pool.wait_ge(fh_done, blk + 1)
                pool.tensor_tensor(fw[:, WCOLS // 2:], fa[:, :], f(fw[:, 0:WCOLS // 2]), ALU.subtract).then_inc(fl_done, 1)

            pool.memset(fa[BS:BS + 1, :], 0.0).then_inc(row_set, 1)
            pool.wait_ge(row_set, 1)
            for blk in range(NBLK):
                weights(blk)

        @block.scalar
        def _(act):
            act.sem_inc(oh_done, PIECES)

            def load_weights(blk):
                if blk >= 2:
                    act.wait_ge(fa_done, 5 * (blk - 1))
                act.dma_start(fs[0:BS, blk % 2, 0, :, :], w1[blk]).then_inc(fs_loaded[blk % 2], 16)
                act.dma_start(fs[0:BS, blk % 2, 1, :, :], w2[blk]).then_inc(fs_loaded[blk % 2], 16)
                act.dma_start(fs[BS:BS + 1, blk % 2, 1, :, :], b2[blk:blk + 1]).then_inc(fs_loaded[blk % 2], 16)
            load_weights(0)
            load_weights(1)
            act.wait_ge(b_loaded, 32)

            def high(b, h):
                act.wait_ge(mm_done, after(b, ITEMS, h * CT + CT - 1 - ITEMS))
                for t in range(CT):
                    act.wait_ge(on_done, after(b, PIECES, h * CT + t))
                    act.activation(oh[:, h, t, :], of[:, h, t, :], ACT.Identity, bias=bv[:, t:t + 1]).then_inc(oh_done, 1)

            high(0, 0)
            for n, (p, t) in enumerate(D_TILES):
                act.wait_ge(d_loaded[n], 16)
                act.activation(df[:, 0, p, t, :], ds[n], ACT.Copy).then_inc(d_hi, 1)
            if B > 1:
                with act.Fori(0, B - 1) as b:
                    high(b, 1)
                    high(b + 1, 0)
            high(B - 1, 1)
            for blk in range(NBLK):
                act.wait_ge(fa_done, 5 * (blk + 1))
                if blk:
                    act.wait_ge(fw_stored, 16 * blk)
                act.activation(fw[:, 0:WCOLS // 2], fa[:, :], ACT.Copy).then_inc(fh_done, 1)
                if blk + 2 < NBLK:
                    load_weights(blk + 2)
                act.wait_ge(fl_done, blk + 1)
                act.dma_start(w_scr[blk], f(fw[:, :])).then_inc(fw_stored, 16)
            act.wait_ge(fw_stored, 16 * NBLK)
            group.scalar_6(act, once)

        @block.vector
        def _(dve):
            for q, n in ((ol_done, PIECES), (on_done, PIECES), (add_done, ITEMS), (bn_done, ITEMS)):
                dve.sem_inc(q, n)
            dve.wait_ge(den_loaded, 16)
            dve.reciprocal(rec[:, :], rec[:, :]).then_inc(rec_done, 1)
            dve.wait_ge(b_loaded, 32)
            bnv = bn[:, :].rearrange("p (t h s) -> p t h s", t=CT, h=2)

            def divide(b, h):
                dve.wait_ge(o_loaded[h], 48 * (b + 1))
                for t in range(CT):
                    dve.tensor_tensor(of[:, h, t, :], of[:, h, t, :], rb[:, h, t, :], ALU.mult).then_inc(on_done, 1)

            def split(b, h):
                for t in range(CT):
                    dve.wait_ge(oh_done, after(b, PIECES, h * CT + t))
                    dve.scalar_tensor_tensor(ol[:, h, t, :], of[:, h, t, :], bv[:, t:t + 1], f(oh[:, h, t, :]),
                                             ALU.add, ALU.subtract).then_inc(ol_done, 1)
            divide(0, 0)
            split(0, 0)
            for n, (p, t) in enumerate(D_TILES):
                dve.wait_ge(d_hi, n + 1)
                dve.tensor_tensor(df[:, 1, p, t, :], ds[n], f(df[:, 0, p, t, :]), ALU.subtract).then_inc(d_lo, 1)

            def batch(b, last):
                for s in range(ITEMS):
                    h, m, r = s // CT, s % CT, s % RING
                    if s == 1:
                        divide(b, 1)
                    if s == 2:
                        split(b, 1)
                    if s == CT and not last:
                        divide(b + 1, 0)
                    if s == CT + 1 and not last:
                        split(b + 1, 0)
                    dve.wait_ge(mm_done, after(b, ITEMS, s))
                    dve.wait_ge(x_loaded[r], 16 * (b * (ITEMS // RING) + s // RING + 1))
                    dve.scalar_tensor_tensor(xt[:, r, :], ps[:, r, :], bp[:, m:m + 1], xt[:, r, :], ALU.add, ALU.add).then_inc(add_done, 1)
                    dve.wait_ge(add_done, after(b, ITEMS, s))
                    dve.bn_stats(bnv[:, m, h, :], xt[:, r, :]).then_inc(bn_done, 1)
                dve.wait_ge(bn_done, after(b, ITEMS, ITEMS - 1))
                dve.tensor_scalar(bn_all[:, bass.ds(b * 12 * CT, 12 * CT)], bn[:, :], 1.0, None, ALU.mult).then_inc(kept, 1)
            if B > 1:
                with dve.Fori(0, B - 1) as b:
                    batch(b, False)
            batch(B - 1, True)
            dve.wait_ge(kept, B)
            for t in range(B * CT):
                dve.bn_aggr(mv[:, t, :], bn_all[:, 12 * t:12 * t + 12]).then_inc(agg_done, 1)
            dve.wait_ge(agg_done, B * CT)
            group.vector_1(dve)
            group.vector_3(dve, once)
            group.vector_5(dve, once)
            group.vector_7(dve, once)

        @block.tensor
        def _(pe):
            pe.sem_inc(mm_done, ITEMS)
            with pe.Fori(0, B) as b:
                for s in range(ITEMS):
                    h, m, r = s // CT, s % CT, s % RING
                    if m == 0:
                        pe.wait_ge(ol_done, after(b, PIECES, h * CT + CT - 1))
                    pe.wait_ge(add_done, after(b, ITEMS, s - RING))
                    k = 0
                    for t in range(CT):
                        for a, o in ((oh, wh), (oh, wl), (ol, wh)):
                            mm = pe.matmul(ps[:, r, :], o[:, t, m * P:(m + 1) * P], a[:, h, t, :], start=(k == 0), stop=(k == 3 * CT - 1))
                            k += 1
                    mm.then_inc(mm_done, 1)
            pe.wait_ge(avg_loaded, 16)
            group.tensor_2(pe, once)
            group.tensor_4(pe, once)


def filter_stage(nc, B, ident, df, di_in, b1, x1_scr, w_scr, mean, rstd, out):
    QT = 3
    QB = NBLK // 2
    QC = QT * P
    TURNS = 2 * B
    T2 = largest_square()
    BN = 5
    B_COL = (0, P, 2 * P, FQ + REST, FQ + REST + P)
    B_TILE = (0, 1, None, 4, 5)
    with ExitStack() as ctx:
        sb = lambda n, s, d=F32: ctx.enter_context(nc.sbuf_tensor(n, s, d))
        sem = lambda n: ctx.enter_context(nc.semaphore(n))
        di = sb("f_di", [P, 2, KCH, HALF], F32R)
        wt = sb("f_w", [BS + 1, 2, WCOLS], F32R)
        bt = sb("f_b1", [BS, 2, 2])
        xs = sb("f_x", [P, QT, N])
        ev = sb("f_ev", [P, QT, HALF])
        xt = sb("f_xt", [P, 2, NT, QC], F32R)
        xf = sb("f_xf", [BS, 2, 2, 4, FQ], F32R)
        hf = sb("f_hf", [BS, 2, 2, FQ])
        sq = sb("f_sq", [BS, 2, 2, FQ])
        hh = sb("f_hh", [BS + 1, 2, 2, 2 * FQ], F32R)
        y = sb("f_y", [P, 2, KCH, QC], F32R)
        xr = sb("f_xr", [P, QT, N])
        ps_f = ctx.enter_context(nc.psum_tensor("f_ps_f", [P, 2, 512], F32))
        ps_a = ctx.enter_context(nc.psum_tensor("f_ps_a", [P, 2, 512], F32))
        ps_b = ctx.enter_context(nc.psum_tensor("f_ps_b", [P, 2, 512], F32))
        ps_i = ctx.enter_context(nc.psum_tensor("f_ps_i", [P, 2, 512], F32))
        c_loaded = [sem(f"f_c_loaded{r}") for r in range(5)]
        c_hi, c_lo, ones_set = sem("f_c_hi"), sem("f_c_lo"), sem("f_ones_set")
        w1_loaded = [sem("f_w1_loaded0"), sem("f_w1_loaded1")]
        w2_loaded = [sem("f_w2_loaded0"), sem("f_w2_loaded1")]
        x_loaded = sem("f_x_loaded")
        r_loaded = [sem(f"f_r_loaded{t}") for t in range(QT)]
        stored = [sem(f"f_stored{t}") for t in range(QT)]
        norm_done, fold_done = sem("f_norm_done"), sem("f_fold_done")
        t_mm, t_hi, t_lo = sem("f_t_mm"), sem("f_t_hi"), sem("f_t_lo")
        f_mm, f_hi, f_lo = sem("f_f_mm"), sem("f_f_hi"), sem("f_f_lo")
        a_mm, a_out, sq_done, mag_done, sum_done, h_hi, h_lo = (sem("f_a_mm"), sem("f_a_out"), sem("f_sq_done"), sem("f_mag_done"), sem("f_sum_done"),
                                                                 sem("f_h_hi"), sem("f_h_lo"))
        b_mm, y_hi, y_lo = sem("f_b_mm"), sem("f_y_hi"), sem("f_y_lo")
        i_mm, add1, add2 = sem("f_i_mm"), sem("f_add1"), sem("f_add2")
        block = ctx.enter_context(nc.Block())
        FI = 4 * QB
        TI = NT
        BI = BN * QB
        RI = FI + TI
        CS = 5
        cslot = lambda c: xr[:, :, :].rearrange("p t n -> p (t n)")[:, (c % CS) * HALF:(c % CS + 1) * HALF]

        ORDER = [(w[0], int(w[1]), int(w[3])) for w in """
            F0.0 F0.1 F0.2 F0.3 F1.0 A0.0 F1.1 A0.1 M0.0 F1.2 H0.0 A0.2 F1.3 A0.3 M0.1
            F2.0 H0.1 A1.0 N0.0 F2.1 A1.1 M1.0 F2.2 B0.0 A1.2 B0.1 A1.3 M1.1 B0.2 H1.0 F2.3 A2.0 B0.3
            F3.0 B0.4 H1.1 N0.1 A2.1 M2.0 F3.1 N0.2 A2.2 B1.0 F3.2 B1.1 A2.3 M2.1 B1.2 H2.0 F3.3 B1.3 A3.0 B1.4 T0.0
            H2.1 T0.1 A3.1 M3.0 T0.2 I0.0 B2.0 B2.1 E0.0 A3.2 B2.2 H3.0 A3.3 M3.1 B2.3 T0.3 T0.4 B2.4 H3.1
            I0.1 B3.0 E0.1 B3.1 I1.0 B3.2 T0.5 B3.3 E1.0 T0.6 B3.4 I1.1 E1.1 T0.7 I2.0 E2.0 I2.1 E2.1
            """.split()]

        @block.sync
        def _(sp):
            sp.dma_start(xs[:, :, :], x1_scr[0:QC, :].rearrange("(t p) n -> p t n", p=P)).then_inc(x_loaded, 16)
            for c in range(KCH):
                if c >= CS:
                    sp.wait_ge(c_lo, c - CS + 1)
                sp.dma_start(cslot(c), di_in[:, c, :]).then_inc(c_loaded[c % CS], 16)
            for t in range(QT):
                sp.sem_inc(stored[t], 16)
            def load_x(k):
                sp.dma_start(xs[:, :, :], x1_scr[bass.ds(k * QC, QC), :].rearrange("(t p) n -> p t n", p=P)).then_inc(x_loaded, 16)

            sp.wait_ge(c_lo, KCH)

            def load_w1(k, par, j):
                sp.wait_ge(a_out, after(k, FI, 4 * (j - 2) + 3))
                blk = par * QB + j
                dst = f(wt[0:BS, j % 2, :]).rearrange("p (a n) -> p a n", a=2)[:, :, 0:W1C]
                src = w_scr[bass.ds(blk, 1), 0:BS, :].rearrange("b p (a n) -> p (b a) n", a=2)[:, :, 0:W1C]
                sp.dma_start(dst, src).then_inc(w1_loaded[j % 2], 16)
                sp.dma_start(bt[:, j % 2, :], b1[bass.ds(blk, 1), :, :].rearrange("a p n -> p (a n)")).then_inc(w1_loaded[j % 2], 16)

            def load_w2(k, par, j):
                sp.wait_ge(b_mm, after(k, BI, BN * (j - 2) + BN - 1))
                dst = f(wt[:, j % 2, :]).rearrange("p (a n) -> p a n", a=2)[:, :, W1C:W1C + W2C]
                src = w_scr[bass.ds(par * QB + j, 1), :, :].rearrange("b p (a n) -> p (b a) n", a=2)[:, :, W1C:W1C + W2C]
                sp.dma_start(dst, src).then_inc(w2_loaded[j % 2], 16)

            def turn(k, par, last):
                for j in range(2):
                    load_w1(k, par, j)
                for j in range(2):
                    load_w2(k, par, j)
                if not last:
                    sp.wait_ge(fold_done, after(k, 2 * QT, 2 * QT - 1))
                    sp.wait_ge(t_mm, after(k, TI, TI - 1))
                    load_x(k + 1)
                load_w1(k, par, 2)
                for t in range(QT):
                    sp.wait_ge(stored[t], 16 * (k + 1))
                    sp.dma_start(xr[:, t, :], x1_scr[bass.ds(k * QC + t * P, P), :]).then_inc(r_loaded[t], 16)
                load_w1(k, par, 3)
                load_w2(k, par, 2)
                load_w2(k, par, 3)
                for t in range(QT):
                    sp.wait_ge(add2, after(k, 2 * QT, 2 * t + 1))
                    sp.dma_start(out[bass.ds(k * QC + t * P, P), :], xr[:, t, :]).then_inc(stored[t], 16)
            with sp.Fori(0, TURNS - 1) as k:
                turn(k, k % 2, False)
            turn(TURNS - 1, 1, True)
            for t in range(QT):
                sp.wait_ge(stored[t], 16 * (TURNS + 1))

        @block.tensor
        def _(pe):
            for q, n in ((t_mm, TI), (f_mm, FI), (a_mm, 4 * QB), (b_mm, BI), (i_mm, 2 * QT)):
                pe.sem_inc(q, n)
            pe.wait_ge(c_lo, KCH)
            pe.wait_ge(ones_set, 2)

            def turned(k, ts):
                for n in ts:
                    par, t = divmod(n, HN)
                    src = ev if par == 0 else xs
                    if n == 0:
                        pe.wait_ge(fold_done, after(k, 2 * QT, 2 * QT - 1))
                    if n >= 2:
                        pe.wait_ge(t_lo, after(k, TI, n - 2))
                    else:
                        pe.wait_ge(f_lo, after(k, FI, n - 2))
                    for q in range(QT):
                        lo = (0 if par == 0 else HALF) + t * P
                        mm = pe.transpose(ps_f[:, n % 2, q * P:(q + 1) * P], src[:, q, lo:lo + P], ident[:, :])
                    mm.then_inc(t_mm, 1)

            def forward(k, j, ns):
                for n in ns:
                    par, ri = divmod(n, 2)
                    i = 4 * j + n
                    if i == 0:
                        pe.wait_ge(t_lo, after(k, TI, TI - 1))
                    if i >= 2:
                        pe.wait_ge(f_lo, after(k, FI, i - 2))
                    q = 0
                    for t in range(HN):
                        for a, c in ((0, 0), (0, 1), (1, 0)):
                            mm = pe.matmul(ps_f[0:BS, i % 2, 0:FQ], xt[:, a, par * HN + t, j * BS:(j + 1) * BS],
                                           df[:, c, par, t, ri * FQ:(ri + 1) * FQ], start=(q == 0), stop=(q == 3 * HN - 1))
                            q += 1
                    mm.then_inc(f_mm, 1)

            def first(k, j, ns):
                w = wt[0:BS, j % 2, :].rearrange("p (a n) -> p a n", a=2)
                for n in ns:
                    if n == 0:
                        pe.wait_ge(w1_loaded[j % 2], 64 * k + 32 * (j // 2 + 1))
                    par, ri = divmod(n, 2)
                    i = 4 * j + n
                    pe.wait_ge(f_lo, after(k, FI, 4 * j + 2 * par + 1))
                    pe.wait_ge(a_out, after(k, FI, i - 2))
                    q = 0
                    for s, col in ((0, 0 if ri == 0 else 1), (1, 2 if ri == 0 else 0)):
                        for a, c in ((0, 0), (0, 1), (1, 0)):
                            mm = pe.matmul(ps_a[0:BS, i % 2, 0:FQ], w[:, c, col * BS:(col + 1) * BS],
                                           xf[:, j % 2, a, 2 * par + s, :], start=(q == 0), stop=(q == 5))
                            q += 1
                    mm.then_inc(a_mm, 1)

            def second(k, j, ns):
                w = wt[:, j % 2, :].rearrange("p (a n) -> p a n", a=2)
                for n in ns:
                    if n == 0:
                        pe.wait_ge(w2_loaded[j % 2], 32 * k + 16 * (j // 2 + 1))
                        pe.wait_ge(h_lo, after(k, 2 * QB, 2 * j + 1))
                    i = BN * j + n
                    pe.wait_ge(y_lo, after(k, BI, i - 2))
                    q = 0
                    for s in range(2):
                        rows = BS + 1 if s == 0 else BS
                        for a, c in ((0, 0), (0, 1), (1, 0)):
                            mm = pe.matmul(ps_b[:, i % 2, 0:2 * BS], hh[0:rows, a, s, B_COL[n]:B_COL[n] + P],
                                           w[0:rows, c, W1C + s * 2 * BS:W1C + (s + 1) * 2 * BS], start=(q == 0), stop=(q == 5))
                            q += 1
                    mm.then_inc(b_mm, 1)

            def inverse(k, t, par):
                if par == 0:
                    pe.wait_ge(y_lo, after(k, BI, BN * min(QB - 1, ((t + 1) * P - 1) // BS) + BN - 1))
                pe.wait_ge((add1, add2)[par], after(k, 2 * QT, 2 * t - 1))
                tiles = [(4 * par + c, slice(0, P)) for c in range(4)] + [(KCH - 1, slice(64 * par, 64 * par + 64))]
                q = 0
                for c, rows in tiles:
                    for a, e in ((0, 0), (0, 1), (1, 0)):
                        mm = pe.matmul(ps_i[:, par, :], y[rows, a, c, t * P:(t + 1) * P], di[rows, e, c, :],
                                       start=(q == 0), stop=(q == 3 * len(tiles) - 1))
                        q += 1
                mm.then_inc(i_mm, 1)

            turned(0, range(TI))

            def turn(k, last):
                for what, j, n in ORDER:
                    if what == "F":
                        forward(k, j, (n,))
                    if what == "A":
                        first(k, j, (n,))
                    if what == "B":
                        second(k, j, (n,))
                    if what == "I":
                        inverse(k, j, n)
                    if what == "T" and not last:
                        turned(k + 1, (n,))
            with pe.Fori(0, TURNS - 1) as k:
                turn(k, False)
            turn(TURNS - 1, True)

        @block.scalar
        def _(act):
            for q, n in ((t_hi, TI), (f_hi, FI), (a_out, FI), (sq_done, 2 * QB), (h_hi, 2 * QB), (y_hi, BI)):
                act.sem_inc(q, n)
            for c in range(KCH):
                act.wait_ge(c_loaded[c % CS], 16 * (c // CS + 1))
                act.activation(di[:, 0, c, :], cslot(c), ACT.Copy).then_inc(c_hi, 1)

            def turned(k, ts):
                for n in ts:
                    act.wait_ge(t_mm, after(k, TI, n))
                    if n == 0:
                        act.wait_ge(f_mm, after(k, FI, -1))
                    act.activation(xt[:, 0, n, :], ps_f[:, n % 2, 0:QC], ACT.Copy).then_inc(t_hi, 1)

            def forward(k, j, ns=range(4)):
                for n in ns:
                    i = 4 * j + n
                    act.wait_ge(f_mm, after(k, FI, i))
                    if n == 0:
                        act.wait_ge(a_mm, after(k, FI, 4 * (j - 2) + 3))
                    act.activation(xf[:, j % 2, 0, n, :], ps_f[0:BS, i % 2, 0:FQ], ACT.Copy).then_inc(f_hi, 1)

            def biased(k, j, n):
                par, ri = divmod(n, 2)
                u = 2 * j + par
                if n == 0:
                    act.wait_ge(w1_loaded[j % 2], 64 * k + 32 * (j // 2 + 1))
                if ri == 0:
                    act.wait_ge(h_lo, after(k, 2 * QB, u - 2))
                act.wait_ge(a_mm, after(k, FI, 2 * u + ri))
                act.activation(hf[:, par, ri, :], ps_a[0:BS, ri, 0:FQ], ACT.Identity, bias=bt[:, j % 2, ri:ri + 1]).then_inc(a_out, 1)
                if ri == 1:
                    act.wait_ge(a_out, after(k, FI, 2 * u + 1))
                    act.wait_ge(mag_done, after(k, 2 * QB, u - 2))
                    act.activation(sq[:, par, :, :], hf[:, par, :, :], ACT.Square).then_inc(sq_done, 1)

            def hidden(k, j, par):
                u = 2 * j + par
                act.wait_ge(mag_done, after(k, 2 * QB, u))
                act.wait_ge(b_mm, after(k, BI, BN * (j - 1) + (2, 4)[par]))
                act.activation(hh[0:BS, 0, :, par * FQ:(par + 1) * FQ], hf[:, par, :, :], ACT.Copy).then_inc(h_hi, 1)

            def second(k, j, n):
                i = BN * j + n
                act.wait_ge(b_mm, after(k, BI, i))
                if i == 0:
                    act.wait_ge(i_mm, after(k, 2 * QT, -1))
                src = ps_b[:, i % 2, 0:2 * BS].rearrange("p (r n) -> p r n", r=2)
                cs = slice(j * BS, (j + 1) * BS)
                if B_TILE[n] is not None:
                    act.activation(y[:, 0, B_TILE[n]:B_TILE[n] + 3:2, cs], src, ACT.Copy).then_inc(y_hi, 1)
                else:
                    for q in range(4):
                        op = act.activation(y[32 * q:32 * (q + 1), 0, KCH - 1, cs], src[0:2 * REST, q % 2, :], ACT.Copy)
                    op.then_inc(y_hi, 1)

            turned(0, range(TI))

            def turn(k, last):
                for what, j, n in ORDER:
                    if what == "F":
                        forward(k, j, (n,))
                    if what == "A":
                        biased(k, j, n)
                    if what == "H":
                        hidden(k, j, n)
                    if what == "B":
                        second(k, j, n)
                    if what == "T" and not last:
                        turned(k + 1, (n,))
            with act.Fori(0, TURNS - 1) as k:
                turn(k, False)
            turn(TURNS - 1, True)

        @block.vector
        def _(dve):
            for q, n in ((norm_done, QT), (t_lo, TI), (f_lo, FI), (mag_done, 2 * QB), (sum_done, 2 * QB),
                         (h_lo, 2 * QB), (y_lo, BI), (add1, 2 * QT), (add2, 2 * QT)):
                dve.sem_inc(q, n)
            dve.memset(f(hh[BS:BS + 1, 0, :, :]), 1.0).then_inc(ones_set, 1)
            dve.memset(f(hh[BS:BS + 1, 1, :, :]), 0.0).then_inc(ones_set, 1)

            def norm(k, ts):
                for t in ts:
                    if t == 0:
                        dve.wait_ge(x_loaded, 16 * (k + 1))
                    col = k * QT + t
                    dve.tensor_scalar(xs[:, t, :], xs[:, t, :], mean[:, bass.ds(col, 1)], rstd[:, bass.ds(col, 1)],
                                      ALU.subtract, ALU.mult).then_inc(norm_done, 1)

            def turned(k, ts):
                for n in ts:
                    dve.wait_ge(t_hi, after(k, TI, n))
                    dve.tensor_tensor(xt[:, 1, n, :], ps_f[:, n % 2, 0:QC], f(xt[:, 0, n, :]), ALU.subtract).then_inc(t_lo, 1)

            def forward(k, j, ns=range(4)):
                for n in ns:
                    i = 4 * j + n
                    dve.wait_ge(f_hi, after(k, FI, i))
                    dve.tensor_tensor(xf[:, j % 2, 1, n, :], ps_f[0:BS, i % 2, 0:FQ], f(xf[:, j % 2, 0, n, :]), ALU.subtract).then_inc(f_lo, 1)

            def masked(k, j, par):
                u = 2 * j + par
                h, m = hf[:, par, :, :], sq[:, par, :, :]
                dve.wait_ge(sq_done, after(k, 2 * QB, u))
                dve.tensor_tensor(m[:, 0, :], m[:, 0, :], m[:, 1, :], ALU.add).then_inc(sum_done, 1)
                dve.wait_ge(sum_done, after(k, 2 * QB, u))
                dve.scalar_tensor_tensor(h, m[:, 0:1, :].broadcast_to([BS, 2, FQ]), T2, h, ALU.is_gt, ALU.mult).then_inc(mag_done, 1)

            def hidden(k, j, par):
                u = 2 * j + par
                cols = slice(par * FQ, (par + 1) * FQ)
                dve.wait_ge(h_hi, after(k, 2 * QB, u))
                dve.tensor_tensor(hh[0:BS, 1, :, cols], hf[:, par, :, :], f(hh[0:BS, 0, :, cols]),
                                  ALU.subtract).then_inc(h_lo, 1)

            def second(k, j, n):
                i = BN * j + n
                src = ps_b[:, i % 2, 0:2 * BS].rearrange("p (r n) -> p r n", r=2)
                cs = slice(j * BS, (j + 1) * BS)
                dve.wait_ge(y_hi, after(k, BI, i))
                if B_TILE[n] is not None:
                    cc = slice(B_TILE[n], B_TILE[n] + 3, 2)
                    dve.tensor_tensor(y[:, 1, cc, cs], src, f(y[:, 0, cc, cs]), ALU.subtract).then_inc(y_lo, 1)
                else:
                    for q in range(4):
                        rows = slice(32 * q, 32 * (q + 1))
                        op = dve.tensor_tensor(y[rows, 1, KCH - 1, cs], src[0:2 * REST, q % 2, :], f(y[rows, 0, KCH - 1, cs]), ALU.subtract)
                    op.then_inc(y_lo, 1)

            def added(k, t, par):
                if par == 0:
                    dve.wait_ge(r_loaded[t], 16 * (k + 1))
                dve.wait_ge(i_mm, after(k, 2 * QT, 2 * t + par))
                for q, h in enumerate((slice(0, HALF), slice(HALF, N))):
                    if par == 0:
                        dve.tensor_tensor(xr[:, t, h], ps_i[:, 0, :], xr[:, t, h], ALU.add).then_inc(add1, 1)
                    else:
                        dve.wait_ge(add1, after(k, 2 * QT, 2 * t + q))
                        dve.tensor_tensor(xr[:, t, h], xr[:, t, h], ps_i[:, 1, :], ALU.add if q == 0 else ALU.subtract).then_inc(add2, 1)

            norm(0, range(QT))
            for c in range(KCH):
                dve.wait_ge(c_hi, c + 1)
                dve.tensor_tensor(di[:, 1, c, :], cslot(c), f(di[:, 0, c, :]), ALU.subtract).then_inc(c_lo, 1)
            turned(0, range(TI))

            def turn(k, last):
                for what, j, n in ORDER:
                    if what == "F":
                        forward(k, j, (n,))
                    if what == "M":
                        masked(k, j, n)
                    if what == "H":
                        hidden(k, j, n)
                    if what == "B":
                        second(k, j, n)
                    if what == "E":
                        added(k, j, n)
                    if what == "N" and not last:
                        norm(k + 1, (n,))
                    if what == "T" and not last:
                        turned(k + 1, (n,))
            with dve.Fori(0, TURNS - 1) as k:
                turn(k, False)
            turn(TURNS - 1, True)

        @block.gpsimd
        def _(pool):
            pool.sem_inc(fold_done, 2 * QT)
            with pool.Fori(0, TURNS) as k:
                pool.wait_ge(t_mm, after(k, TI, -1))
                for t in range(QT):
                    pool.wait_ge(norm_done, after(k, QT, t))
                    pool.tensor_tensor(ev[:, t, :], xs[:, t, 0:HALF], xs[:, t, HALF:N], ALU.add).then_inc(fold_done, 1)
                    pool.tensor_tensor(xs[:, t, HALF:N], xs[:, t, 0:HALF], xs[:, t, HALF:N], ALU.subtract).then_inc(fold_done, 1)


def build(nc, B, x, w_qkv, b_qkv, w_proj, b_proj, w1, b1, w2, b2, avg_in, ident_in, df_in, di_in, out):
    xv = x.rearrange("b c h w -> b c (h w)")
    qk_scr = nc.dram_tensor("qk_scr", [4, B * C, N], F32, kind="Internal").ap()
    v_scr = nc.dram_tensor("v_scr", [B * HEADS, P, NT, 2 * D], F32, kind="Internal").ap()
    o_scr = nc.dram_tensor("o_scr", [B * C, N], F32, kind="Internal").ap()
    den_scr = nc.dram_tensor("den_scr", [B * HEADS, N], F32, kind="Internal").ap()
    rec_scr = nc.dram_tensor("rec_scr", [B * HEADS, N], F32, kind="Internal").ap()
    x1_scr = nc.dram_tensor("x1_scr", [B * C, N], F32, kind="Internal").ap()
    w_scr = nc.dram_tensor("w_scr", [NBLK, BS + 1, WCOLS], F32, kind="Internal").ap()
    with ExitStack() as ctx:
        sb = lambda n, s, d=F32: ctx.enter_context(nc.sbuf_tensor(n, s, d))
        mean, rstd, ident = sb("mean", [P, B * CT]), sb("rstd", [P, B * CT]), sb("ident", [P, P])
        with nc.sbuf_tensor("avg", [P, len(AVG_PAIRS), P], F32) as avg:
            qkv_stage(nc, B, xv, w_qkv, b_qkv, avg_in, ident_in, avg, ident, qk_scr, v_scr)
        df = sb("df", [P, 2, 2, HN, 2 * FQ], F32R)
        with nc.sbuf_tensor("proj_wh", [P, CT, C], F32R) as pwh, nc.sbuf_tensor("proj_wl", [P, CT, C], F32R) as pwl:
            attend_stage(nc, B, ident, w_proj, pwh, pwl, df, qk_scr, v_scr, o_scr, den_scr)
            project_stage(nc, B, xv, pwh, pwl, avg_in, df_in, df, b_proj, b_qkv[2 * C:3 * C], w1, w2, b2, o_scr, den_scr, rec_scr,
                          x1_scr, w_scr, mean, rstd)
        filter_stage(nc, B, ident, df, di_in, b1, x1_scr, w_scr, mean, rstd, out.rearrange("b c h w -> (b c) (h w)"))


def constants():
    avg = np.zeros([P, len(AVG_PAIRS), P], np.float32)
    for i, (a, b) in enumerate(AVG_PAIRS):
        ga, gb = (a * P + np.arange(P)) // GROUP, (b * P + np.arange(P)) // GROUP
        avg[:, i, :] = (ga[:, None] == gb[None, :]) / GROUP
    h, w = np.divmod(np.arange(HALF), W)
    df = np.zeros([P, 2, HN, 2 * FQ], np.float32)
    di = np.zeros([P, KCH, HALF], np.float32)
    for par in range(2):
        kh, kw = np.divmod(np.roll(np.arange(FQ), par * REST), KW)
        kh = 2 * kh + par
        turn = (kh[:, None] * h[None, :] * (W // 1) + kw[:, None] * w[None, :] * H) % (H * W)
        ang = 2 * np.pi * turn / (H * W)
        s = 1 / math.sqrt(H * W)
        re, im = np.cos(ang) * s, -np.sin(ang) * s
        full = np.concatenate([re, im], 0).T
        df[:, par] = full.reshape(HN, P, 2 * FQ).transpose(1, 0, 2)
        c = np.where((kw == 0) | (kw == W // 2), 1.0, 2.0)[:, None]
        ire, iim = c * re, c * im
        for ch in range(2):
            rows = slice(par * REST + ch * P, par * REST + (ch + 1) * P)
            di[:, 4 * par + ch] = ire[rows]
            di[:, 4 * par + 2 + ch] = iim[rows]
        rest = slice(0, REST) if par else slice(2 * P, FQ)
        di[(64 + REST) * par:(64 + REST) * par + REST, KCH - 1] = ire[rest]
        di[(64 + REST) * par + 32:(64 + REST) * par + 32 + REST, KCH - 1] = iim[rest]
    return {"avg": avg, "ident": np.eye(P, dtype=np.float32), "df": df, "di": di}


_INS = ["x", "L0_conv_w_qkv", "L0_conv_b_qkv", "L0_conv_w_proj", "L0_conv_b_proj", "L1_conv_w1", "L1_conv_b1", "L1_conv_w2", "L1_conv_b2"]


def kernel(**inputs):
    import concourse.bacc as bacc
    from concourse.bass_utils import run_bass_kernel_spmd

    nc = bacc.Bacc("TRN2", target_bir_lowering=False, num_devices=1)
    arrays, args = {}, []
    for name, a in [(n, np.ascontiguousarray(inputs[n])) for n in _INS] + list(constants().items()):
        arrays[f"in_{name}"] = a
        args.append(nc.dram_tensor(f"in_{name}", a.shape, mybir.dt.from_np(a.dtype), kind="ExternalInput").ap())
    x = arrays["in_x"]
    out = nc.dram_tensor("out_0", x.shape, F32, kind="ExternalOutput").ap()
    build(nc, x.shape[0], *args, out)
    r = run_bass_kernel_spmd(nc, [arrays], core_ids=[0])
    return r.results[0]["out_0"]
```
